# Optimizing a Trainium2 kernel written in Bass

```python
import numpy as np
import jax
import jax.numpy as jnp

def _softmax(x, axis=-1):
    return jax.nn.softmax(x, axis=axis)

def _gelu(x):
    return jax.nn.gelu(x, approximate=True)

def _silu(x):
    return jax.nn.silu(x)

def _sigmoid(x):
    return jax.nn.sigmoid(x)

def _layernorm(x, axis=-1, eps=1e-05):
    m = jnp.mean(x, axis=axis, keepdims=True)
    v = jnp.var(x, axis=axis, keepdims=True)
    return (x - m) / jnp.sqrt(v + eps)

def _scatter_add(tgt, idx, src, axis=0):
    return tgt.at[idx].add(src)

def _segment_sum(src, seg, n):
    return jax.ops.segment_sum(src, seg, n)
kernel_name = 'mk_xattn_seq_d4_seqx_r4_3f9fc1'

def setup_inputs(seed: int=0):
    np.random.seed(seed)
    _w = jnp.asarray

    def _rec_inputs():
        import jax
        import jax.numpy as jnp
        _rk = jax.random.key(seed)
        x = 7.22e-05 + 1 * jax.random.normal(jax.random.fold_in(_rk, 1), (4, 512, 512), jnp.float32)
        _lenS = 512 - jax.random.randint(jax.random.fold_in(_rk, 7), (4,), 0, max(1, 512 // 4) + 1, jnp.int32)
        _lenS2 = 1024 - jax.random.randint(jax.random.fold_in(_rk, 8), (4,), 0, max(1, 1024 // 4) + 1, jnp.int32)
        _ctx_2048P = jax.random.normal(jax.random.fold_in(_rk, 11), (4, 16, 512), jnp.float32)
        _ctx_2048c = jax.random.dirichlet(jax.random.fold_in(_rk, 511), 0.3 * jnp.ones((16,), jnp.float32), (4, 1024))
        _ctx_2048t = jnp.einsum('bsk,bkd->bsd', _ctx_2048c, _ctx_2048P)
        _ctx_2048t = _ctx_2048t * jax.lax.rsqrt(jnp.mean(jnp.square(_ctx_2048t)) + 1e-12) * 0.953939
        ctx_2048 = 2.81802e-05 + 1.00001 * (_ctx_2048t + 0.3 * jax.random.normal(jax.random.fold_in(_rk, 611), (4, 1024, 512), jnp.float32))
        _validS = jnp.arange(512)[None, :] < _lenS[:, None]
        _validS2 = jnp.arange(1024)[None, :] < _lenS2[:, None]
        _causal = jnp.tril(jnp.ones((512, 512), dtype=bool))
        mask_BxS2_bf1 = jnp.ones((4, 1024), dtype=bool)
        mask_Bx1xSxS2_ff0 = jnp.where(jnp.ones((4, 1, 512, 1024), dtype=bool), 0.0, -1000000000.0).astype(jnp.float32)
        return (x, ctx_2048, mask_BxS2_bf1, mask_Bx1xSxS2_ff0)
    x, ctx_2048, mask_BxS2_bf1, mask_Bx1xSxS2_ff0 = _rec_inputs()

    def _L0_xattn_setup():
        import jax, jax.numpy as jnp
        import numpy as np
        D = 512
        H = 16
        HD = D // H
        INNER = 4 * D
        EPS = 1e-05

        def layer_norm(x, w, b):
            mu = jnp.mean(x, axis=-1, keepdims=True)
            var = jnp.mean(jnp.square(x - mu), axis=-1, keepdims=True)
            return (x - mu) * jax.lax.rsqrt(var + EPS) * w + b
        key = jax.random.key(seed)
        ks = jax.random.split(key, 12)
        B, LQ, LK = (4, 256, 512)
        std = 0.02
        inp = {'hidden_states': jax.random.normal(ks[0], (B, LQ, D), jnp.float32), 'encoder_hidden_states': jax.random.normal(ks[1], (B, LK, D), jnp.float32), 'encoder_attention_mask': jnp.ones((B, LK), dtype=bool), 'ln1_w': jnp.ones((D,), jnp.float32), 'ln1_b': jnp.zeros((D,), jnp.float32), 'q_w': jax.random.normal(ks[2], (D, D), jnp.float32) * std, 'q_b': jnp.zeros((D,), jnp.float32), 'k_w': jax.random.normal(ks[3], (D, D), jnp.float32) * std, 'k_b': jnp.zeros((D,), jnp.float32), 'v_w': jax.random.normal(ks[4], (D, D), jnp.float32) * std, 'v_b': jnp.zeros((D,), jnp.float32), 'cproj_w': jax.random.normal(ks[5], (D, D), jnp.float32) * std, 'cproj_b': jnp.zeros((D,), jnp.float32), 'ln2_w': jnp.ones((D,), jnp.float32), 'ln2_b': jnp.zeros((D,), jnp.float32), 'fc_w': jax.random.normal(ks[6], (D, INNER), jnp.float32) * std, 'fc_b': jnp.zeros((INNER,), jnp.float32), 'proj_w': jax.random.normal(ks[7], (INNER, D), jnp.float32) * std, 'proj_b': jnp.zeros((D,), jnp.float32)}
        return inp
    _L0_xattn_all = _L0_xattn_setup()
    _L0_xattn_in = {k: v for k, v in _L0_xattn_all.items() if k in ('ln1_w', 'ln1_b', 'q_w', 'q_b', 'k_w', 'k_b', 'v_w', 'v_b', 'cproj_w', 'cproj_b', 'ln2_w', 'ln2_b', 'fc_w', 'fc_b', 'proj_w', 'proj_b')}
    del _L0_xattn_all

    def _L1_xattn_setup():
        import jax, jax.numpy as jnp
        import numpy as np
        D = 512
        H = 16
        HD = D // H
        INNER = 4 * D
        EPS = 1e-05

        def layer_norm(x, w, b):
            mu = jnp.mean(x, axis=-1, keepdims=True)
            var = jnp.mean(jnp.square(x - mu), axis=-1, keepdims=True)
            return (x - mu) * jax.lax.rsqrt(var + EPS) * w + b
        key = jax.random.key(seed)
        ks = jax.random.split(key, 12)
        B, LQ, LK = (4, 256, 512)
        std = 0.02
        inp = {'hidden_states': jax.random.normal(ks[0], (B, LQ, D), jnp.float32), 'encoder_hidden_states': jax.random.normal(ks[1], (B, LK, D), jnp.float32), 'encoder_attention_mask': jnp.ones((B, LK), dtype=bool), 'ln1_w': jnp.ones((D,), jnp.float32), 'ln1_b': jnp.zeros((D,), jnp.float32), 'q_w': jax.random.normal(ks[2], (D, D), jnp.float32) * std, 'q_b': jnp.zeros((D,), jnp.float32), 'k_w': jax.random.normal(ks[3], (D, D), jnp.float32) * std, 'k_b': jnp.zeros((D,), jnp.float32), 'v_w': jax.random.normal(ks[4], (D, D), jnp.float32) * std, 'v_b': jnp.zeros((D,), jnp.float32), 'cproj_w': jax.random.normal(ks[5], (D, D), jnp.float32) * std, 'cproj_b': jnp.zeros((D,), jnp.float32), 'ln2_w': jnp.ones((D,), jnp.float32), 'ln2_b': jnp.zeros((D,), jnp.float32), 'fc_w': jax.random.normal(ks[6], (D, INNER), jnp.float32) * std, 'fc_b': jnp.zeros((INNER,), jnp.float32), 'proj_w': jax.random.normal(ks[7], (INNER, D), jnp.float32) * std, 'proj_b': jnp.zeros((D,), jnp.float32)}
        return inp
    _L1_xattn_all = _L1_xattn_setup()
    _L1_xattn_in = {k: v for k, v in _L1_xattn_all.items() if k in ('ln1_w', 'ln1_b', 'q_w', 'q_b', 'k_w', 'k_b', 'v_w', 'v_b', 'cproj_w', 'cproj_b', 'ln2_w', 'ln2_b', 'fc_w', 'fc_b', 'proj_w', 'proj_b')}
    del _L1_xattn_all

    def _L2_xattn_setup():
        import jax, jax.numpy as jnp
        import numpy as np
        H = 512
        NH = 32
        KVH = 8
        HD = H // NH
        GROUPS = NH // KVH
        EPS = 1e-06
        B, L, S = (4, 256, 256)

        def _gqa_forward(hidden_state, encoder_hidden_state, encoder_attention_mask, Wq, bq, Wk, bk, Wv, bv, Wo, bo, gamma, beta):
            b, l, _ = hidden_state.shape
            s = encoder_hidden_state.shape[1]
            q = hidden_state @ Wq + bq
            k = encoder_hidden_state @ Wk + bk
            v = encoder_hidden_state @ Wv + bv
            q = q.reshape(b, l, KVH, GROUPS, HD).transpose(0, 2, 3, 1, 4)
            k = k.reshape(b, s, KVH, HD).transpose(0, 2, 1, 3)
            v = v.reshape(b, s, KVH, HD).transpose(0, 2, 1, 3)
            scale = 1.0 / jnp.sqrt(jnp.asarray(HD, q.dtype))
            scores = jnp.einsum('bkgld,bksd->bkgls', q, k) * scale
            scores = scores + encoder_attention_mask[:, :, None, :, :]
            attn = jax.nn.softmax(scores, axis=-1)
            out = jnp.einsum('bkgls,bksd->bkgld', attn, v)
            out = out.transpose(0, 3, 1, 2, 4).reshape(b, l, H)
            out = out @ Wo + bo
            x = out + hidden_state
            mu = jnp.mean(x, axis=-1, keepdims=True)
            var = jnp.var(x, axis=-1, keepdims=True)
            return (x - mu) * jax.lax.rsqrt(var + EPS) * gamma + beta
        key = jax.random.key(seed)
        ks = jax.random.split(key, 12)
        sd = 0.02
        return {'hidden_state': jax.random.normal(ks[0], (B, L, H), jnp.float32), 'encoder_hidden_state': jax.random.normal(ks[1], (B, S, H), jnp.float32), 'encoder_attention_mask': jnp.zeros((B, 1, L, S), jnp.float32), 'Wq': jax.random.normal(ks[2], (H, H), jnp.float32) * sd, 'bq': jnp.zeros((H,), jnp.float32), 'Wk': jax.random.normal(ks[3], (H, KVH * HD), jnp.float32) * sd, 'bk': jnp.zeros((KVH * HD,), jnp.float32), 'Wv': jax.random.normal(ks[4], (H, KVH * HD), jnp.float32) * sd, 'bv': jnp.zeros((KVH * HD,), jnp.float32), 'Wo': jax.random.normal(ks[5], (H, H), jnp.float32) * sd, 'bo': jnp.zeros((H,), jnp.float32), 'gamma': jnp.ones((H,), jnp.float32), 'beta': jnp.zeros((H,), jnp.float32)}
    _L2_xattn_all = _L2_xattn_setup()
    _L2_xattn_in = {k: v for k, v in _L2_xattn_all.items() if k in ('Wq', 'bq', 'Wk', 'bk', 'Wv', 'bv', 'Wo', 'bo', 'gamma', 'beta')}
    del _L2_xattn_all

    def _L3_xattn_setup():
        import jax, jax.numpy as jnp
        import numpy as np
        E, H, L, B = (512, 32, 256, 4)
        S = E // H
        DM, DD = (32, 64)

        def _ln(x, w, b, eps=1e-05):
            m = x.mean(-1, keepdims=True)
            v = ((x - m) ** 2).mean(-1, keepdims=True)
            return (x - m) / jnp.sqrt(v + eps) * w + b

        def _block(x, state, ln1_w, ln1_b, ln2_w, ln2_b, maa_x, maa_w1, maa_w2, maa_stack, time_decay, td_w1, td_w2, u, Wr, Wk, Wv, Wg, Wo, gn_w, gn_b, ffn_maa_k, ffn_maa_r, Wfk, Wfr, Wfv):
            b, l, e = x.shape
            h = u.shape[0]
            s_ = e // h
            xa = _ln(x, ln1_w, ln1_b)
            sx = jnp.concatenate([state[:, 1:2] - xa[:, :1], xa[:, :-1] - xa[:, 1:]], axis=1)
            xxx = jnp.tanh((xa + sx * maa_x) @ maa_w1).reshape(b, l, 5, DM)
            xxx = jnp.einsum('blfd,fde->blfe', xxx, maa_w2)
            xm = xa[:, :, None] + sx[:, :, None] * (maa_stack + xxx)
            xk, xw, xv, xr, xg = (xm[:, :, j] for j in range(5))
            w = jnp.exp(-jnp.exp(time_decay + jnp.tanh(xw @ td_w1) @ td_w2)).reshape(b, l, h, s_)
            r = (xr @ Wr.T).reshape(b, l, h, s_)
            k = (xk @ Wk.T).reshape(b, l, h, s_)
            v = (xv @ Wv.T).reshape(b, l, h, s_)
            g = jax.nn.silu(xg @ Wg.T)
            s0 = state[:, 2:2 + s_].reshape(b, h, s_, s_)

            def step(s, rkvw):
                r_t, k_t, v_t, w_t = rkvw
                a = k_t[..., :, None] * v_t[..., None, :]
                out = jnp.einsum('bhi,bhij->bhj', r_t, u * a + s)
                s = a + w_t[..., :, None] * s
                return (s, out)
            rkvw = tuple((jnp.moveaxis(t, 1, 0) for t in (r, k, v, w)))
            _, out = jax.lax.scan(step, s0, rkvw)
            out = jnp.moveaxis(out, 0, 1).reshape(b, l, e)
            og = out.reshape(b, l, h, s_)
            m = og.mean(-1, keepdims=True)
            va = ((og - m) ** 2).mean(-1, keepdims=True)
            og = ((og - m) / jnp.sqrt(va + 1e-05)).reshape(b, l, e) * gn_w + gn_b
            x1 = x + og * g @ Wo.T
            xc = _ln(x1, ln2_w, ln2_b)
            sx2 = jnp.concatenate([state[:, 0:1] - xc[:, :1], xc[:, :-1] - xc[:, 1:]], axis=1)
            xk2 = xc + sx2 * ffn_maa_k
            xr2 = xc + sx2 * ffn_maa_r
            rr = jax.nn.sigmoid(xr2 @ Wfr.T)
            kk = jnp.square(jax.nn.relu(xk2 @ Wfk.T))
            return x1 + rr * (kk @ Wfv.T)
        key = jax.random.key(seed)
        ks = jax.random.split(key, 24)
        sc = 0.02
        d = {'x': jax.random.normal(ks[0], (B, L, E), jnp.float32), 'state': jax.random.normal(ks[1], (B, 2 + S, E), jnp.float32) * 0.1, 'ln1_w': jnp.ones((E,), jnp.float32), 'ln1_b': jnp.zeros((E,), jnp.float32), 'ln2_w': jnp.ones((E,), jnp.float32), 'ln2_b': jnp.zeros((E,), jnp.float32), 'maa_x': jax.random.normal(ks[2], (E,), jnp.float32) * 0.1, 'maa_w1': jax.random.normal(ks[3], (E, 5 * DM), jnp.float32) * sc, 'maa_w2': jax.random.normal(ks[4], (5, DM, E), jnp.float32) * sc, 'maa_stack': jax.random.normal(ks[5], (1, 5, E), jnp.float32) * 0.1, 'time_decay': jax.random.normal(ks[6], (E,), jnp.float32) * 0.5, 'td_w1': jax.random.normal(ks[7], (E, DD), jnp.float32) * sc, 'td_w2': jax.random.normal(ks[8], (DD, E), jnp.float32) * sc, 'u': jax.random.normal(ks[9], (H, S, 1), jnp.float32) * 0.1, 'Wr': jax.random.normal(ks[10], (E, E), jnp.float32) * sc, 'Wk': jax.random.normal(ks[11], (E, E), jnp.float32) * sc, 'Wv': jax.random.normal(ks[12], (E, E), jnp.float32) * sc, 'Wg': jax.random.normal(ks[13], (E, E), jnp.float32) * sc, 'Wo': jax.random.normal(ks[14], (E, E), jnp.float32) * sc, 'gn_w': jnp.ones((E,), jnp.float32), 'gn_b': jnp.zeros((E,), jnp.float32), 'ffn_maa_k': jax.random.normal(ks[15], (E,), jnp.float32) * 0.1, 'ffn_maa_r': jax.random.normal(ks[16], (E,), jnp.float32) * 0.1, 'Wfk': jax.random.normal(ks[17], (E, E), jnp.float32) * sc, 'Wfr': jax.random.normal(ks[18], (E, E), jnp.float32) * sc, 'Wfv': jax.random.normal(ks[19], (E, E), jnp.float32) * sc}
        return d
    _L3_xattn_all = _L3_xattn_setup()
    _L3_xattn_in = {k: v for k, v in _L3_xattn_all.items() if k in ('ln1_w', 'ln1_b', 'ln2_w', 'ln2_b', 'maa_x', 'maa_w1', 'maa_w2', 'maa_stack', 'time_decay', 'td_w1', 'td_w2', 'u', 'Wr', 'Wk', 'Wv', 'Wg', 'Wo', 'gn_w', 'gn_b', 'ffn_maa_k', 'ffn_maa_r', 'Wfk', 'Wfr', 'Wfv')}
    del _L3_xattn_all
    return {'x': x, 'ctx_2048': ctx_2048, 'mask_BxS2_bf1': mask_BxS2_bf1, 'mask_Bx1xSxS2_ff0': mask_Bx1xSxS2_ff0, 'L0_xattn_ln1_w': _L0_xattn_in['ln1_w'], 'L0_xattn_ln1_b': _L0_xattn_in['ln1_b'], 'L0_xattn_q_w': _L0_xattn_in['q_w'], 'L0_xattn_q_b': _L0_xattn_in['q_b'], 'L0_xattn_k_w': _L0_xattn_in['k_w'], 'L0_xattn_k_b': _L0_xattn_in['k_b'], 'L0_xattn_v_w': _L0_xattn_in['v_w'], 'L0_xattn_v_b': _L0_xattn_in['v_b'], 'L0_xattn_cproj_w': _L0_xattn_in['cproj_w'], 'L0_xattn_cproj_b': _L0_xattn_in['cproj_b'], 'L0_xattn_ln2_w': _L0_xattn_in['ln2_w'], 'L0_xattn_ln2_b': _L0_xattn_in['ln2_b'], 'L0_xattn_fc_w': _L0_xattn_in['fc_w'], 'L0_xattn_fc_b': _L0_xattn_in['fc_b'], 'L0_xattn_proj_w': _L0_xattn_in['proj_w'], 'L0_xattn_proj_b': _L0_xattn_in['proj_b'], 'L1_xattn_ln1_w': _L1_xattn_in['ln1_w'], 'L1_xattn_ln1_b': _L1_xattn_in['ln1_b'], 'L1_xattn_q_w': _L1_xattn_in['q_w'], 'L1_xattn_q_b': _L1_xattn_in['q_b'], 'L1_xattn_k_w': _L1_xattn_in['k_w'], 'L1_xattn_k_b': _L1_xattn_in['k_b'], 'L1_xattn_v_w': _L1_xattn_in['v_w'], 'L1_xattn_v_b': _L1_xattn_in['v_b'], 'L1_xattn_cproj_w': _L1_xattn_in['cproj_w'], 'L1_xattn_cproj_b': _L1_xattn_in['cproj_b'], 'L1_xattn_ln2_w': _L1_xattn_in['ln2_w'], 'L1_xattn_ln2_b': _L1_xattn_in['ln2_b'], 'L1_xattn_fc_w': _L1_xattn_in['fc_w'], 'L1_xattn_fc_b': _L1_xattn_in['fc_b'], 'L1_xattn_proj_w': _L1_xattn_in['proj_w'], 'L1_xattn_proj_b': _L1_xattn_in['proj_b'], 'L2_xattn_Wq': _L2_xattn_in['Wq'], 'L2_xattn_bq': _L2_xattn_in['bq'], 'L2_xattn_Wk': _L2_xattn_in['Wk'], 'L2_xattn_bk': _L2_xattn_in['bk'], 'L2_xattn_Wv': _L2_xattn_in['Wv'], 'L2_xattn_bv': _L2_xattn_in['bv'], 'L2_xattn_Wo': _L2_xattn_in['Wo'], 'L2_xattn_bo': _L2_xattn_in['bo'], 'L2_xattn_gamma': _L2_xattn_in['gamma'], 'L2_xattn_beta': _L2_xattn_in['beta'], 'L3_xattn_ln1_w': _L3_xattn_in['ln1_w'], 'L3_xattn_ln1_b': _L3_xattn_in['ln1_b'], 'L3_xattn_ln2_w': _L3_xattn_in['ln2_w'], 'L3_xattn_ln2_b': _L3_xattn_in['ln2_b'], 'L3_xattn_maa_x': _L3_xattn_in['maa_x'], 'L3_xattn_maa_w1': _L3_xattn_in['maa_w1'], 'L3_xattn_maa_w2': _L3_xattn_in['maa_w2'], 'L3_xattn_maa_stack': _L3_xattn_in['maa_stack'], 'L3_xattn_time_decay': _L3_xattn_in['time_decay'], 'L3_xattn_td_w1': _L3_xattn_in['td_w1'], 'L3_xattn_td_w2': _L3_xattn_in['td_w2'], 'L3_xattn_u': _L3_xattn_in['u'], 'L3_xattn_Wr': _L3_xattn_in['Wr'], 'L3_xattn_Wk': _L3_xattn_in['Wk'], 'L3_xattn_Wv': _L3_xattn_in['Wv'], 'L3_xattn_Wg': _L3_xattn_in['Wg'], 'L3_xattn_Wo': _L3_xattn_in['Wo'], 'L3_xattn_gn_w': _L3_xattn_in['gn_w'], 'L3_xattn_gn_b': _L3_xattn_in['gn_b'], 'L3_xattn_ffn_maa_k': _L3_xattn_in['ffn_maa_k'], 'L3_xattn_ffn_maa_r': _L3_xattn_in['ffn_maa_r'], 'L3_xattn_Wfk': _L3_xattn_in['Wfk'], 'L3_xattn_Wfr': _L3_xattn_in['Wfr'], 'L3_xattn_Wfv': _L3_xattn_in['Wfv']}

def reference(x, ctx_2048, mask_BxS2_bf1, mask_Bx1xSxS2_ff0, L0_xattn_ln1_w, L0_xattn_ln1_b, L0_xattn_q_w, L0_xattn_q_b, L0_xattn_k_w, L0_xattn_k_b, L0_xattn_v_w, L0_xattn_v_b, L0_xattn_cproj_w, L0_xattn_cproj_b, L0_xattn_ln2_w, L0_xattn_ln2_b, L0_xattn_fc_w, L0_xattn_fc_b, L0_xattn_proj_w, L0_xattn_proj_b, L1_xattn_ln1_w, L1_xattn_ln1_b, L1_xattn_q_w, L1_xattn_q_b, L1_xattn_k_w, L1_xattn_k_b, L1_xattn_v_w, L1_xattn_v_b, L1_xattn_cproj_w, L1_xattn_cproj_b, L1_xattn_ln2_w, L1_xattn_ln2_b, L1_xattn_fc_w, L1_xattn_fc_b, L1_xattn_proj_w, L1_xattn_proj_b, L2_xattn_Wq, L2_xattn_bq, L2_xattn_Wk, L2_xattn_bk, L2_xattn_Wv, L2_xattn_bv, L2_xattn_Wo, L2_xattn_bo, L2_xattn_gamma, L2_xattn_beta, L3_xattn_ln1_w, L3_xattn_ln1_b, L3_xattn_ln2_w, L3_xattn_ln2_b, L3_xattn_maa_x, L3_xattn_maa_w1, L3_xattn_maa_w2, L3_xattn_maa_stack, L3_xattn_time_decay, L3_xattn_td_w1, L3_xattn_td_w2, L3_xattn_u, L3_xattn_Wr, L3_xattn_Wk, L3_xattn_Wv, L3_xattn_Wg, L3_xattn_Wo, L3_xattn_gn_w, L3_xattn_gn_b, L3_xattn_ffn_maa_k, L3_xattn_ffn_maa_r, L3_xattn_Wfk, L3_xattn_Wfr, L3_xattn_Wfv):
    import jax
    import jax.numpy as jnp

    def _L0_xattn_ref(hidden_states, encoder_hidden_states, encoder_attention_mask, ln1_w, ln1_b, q_w, q_b, k_w, k_b, v_w, v_b, cproj_w, cproj_b, ln2_w, ln2_b, fc_w, fc_b, proj_w, proj_b):
        import jax, jax.numpy as jnp
        import numpy as np
        D = 512
        H = 16
        HD = D // H
        INNER = 4 * D
        EPS = 1e-05

        def layer_norm(x, w, b):
            mu = jnp.mean(x, axis=-1, keepdims=True)
            var = jnp.mean(jnp.square(x - mu), axis=-1, keepdims=True)
            return (x - mu) * jax.lax.rsqrt(var + EPS) * w + b
        B, LQ, _ = hidden_states.shape
        LK = encoder_hidden_states.shape[1]
        residual = hidden_states
        x = layer_norm(hidden_states, ln1_w, ln1_b)
        q = (x @ q_w + q_b).reshape(B, LQ, H, HD).transpose(0, 2, 1, 3)
        k = (encoder_hidden_states @ k_w + k_b).reshape(B, LK, H, HD).transpose(0, 2, 1, 3)
        v = (encoder_hidden_states @ v_w + v_b).reshape(B, LK, H, HD).transpose(0, 2, 1, 3)
        scale = 1.0 / np.sqrt(HD).astype(np.float32)
        scores = jnp.einsum('bhqd,bhkd->bhqk', q, k) * scale
        mask = encoder_attention_mask[:, None, None, :]
        mask_value = jnp.finfo(scores.dtype).min
        scores = jnp.where(mask, scores, mask_value)
        attn = jax.nn.softmax(scores, axis=-1)
        out = jnp.einsum('bhqk,bhkd->bhqd', attn, v)
        out = out.transpose(0, 2, 1, 3).reshape(B, LQ, D)
        out = out @ cproj_w + cproj_b
        hidden = out + residual
        residual = hidden
        y = layer_norm(hidden, ln2_w, ln2_b)
        y = jax.nn.gelu(y @ fc_w + fc_b, approximate=True)
        y = y @ proj_w + proj_b
        return residual + y

    def _L1_xattn_ref(hidden_states, encoder_hidden_states, encoder_attention_mask, ln1_w, ln1_b, q_w, q_b, k_w, k_b, v_w, v_b, cproj_w, cproj_b, ln2_w, ln2_b, fc_w, fc_b, proj_w, proj_b):
        import jax, jax.numpy as jnp
        import numpy as np
        D = 512
        H = 16
        HD = D // H
        INNER = 4 * D
        EPS = 1e-05

        def layer_norm(x, w, b):
            mu = jnp.mean(x, axis=-1, keepdims=True)
            var = jnp.mean(jnp.square(x - mu), axis=-1, keepdims=True)
            return (x - mu) * jax.lax.rsqrt(var + EPS) * w + b
        B, LQ, _ = hidden_states.shape
        LK = encoder_hidden_states.shape[1]
        residual = hidden_states
        x = layer_norm(hidden_states, ln1_w, ln1_b)
        q = (x @ q_w + q_b).reshape(B, LQ, H, HD).transpose(0, 2, 1, 3)
        k = (encoder_hidden_states @ k_w + k_b).reshape(B, LK, H, HD).transpose(0, 2, 1, 3)
        v = (encoder_hidden_states @ v_w + v_b).reshape(B, LK, H, HD).transpose(0, 2, 1, 3)
        scale = 1.0 / np.sqrt(HD).astype(np.float32)
        scores = jnp.einsum('bhqd,bhkd->bhqk', q, k) * scale
        mask = encoder_attention_mask[:, None, None, :]
        mask_value = jnp.finfo(scores.dtype).min
        scores = jnp.where(mask, scores, mask_value)
        attn = jax.nn.softmax(scores, axis=-1)
        out = jnp.einsum('bhqk,bhkd->bhqd', attn, v)
        out = out.transpose(0, 2, 1, 3).reshape(B, LQ, D)
        out = out @ cproj_w + cproj_b
        hidden = out + residual
        residual = hidden
        y = layer_norm(hidden, ln2_w, ln2_b)
        y = jax.nn.gelu(y @ fc_w + fc_b, approximate=True)
        y = y @ proj_w + proj_b
        return residual + y

    def _L2_xattn_ref(hidden_state, encoder_hidden_state, encoder_attention_mask, Wq, bq, Wk, bk, Wv, bv, Wo, bo, gamma, beta):
        import jax, jax.numpy as jnp
        import numpy as np
        H = 512
        NH = 32
        KVH = 8
        HD = H // NH
        GROUPS = NH // KVH
        EPS = 1e-06
        B, L, S = (4, 256, 256)

        def _gqa_forward(hidden_state, encoder_hidden_state, encoder_attention_mask, Wq, bq, Wk, bk, Wv, bv, Wo, bo, gamma, beta):
            b, l, _ = hidden_state.shape
            s = encoder_hidden_state.shape[1]
            q = hidden_state @ Wq + bq
            k = encoder_hidden_state @ Wk + bk
            v = encoder_hidden_state @ Wv + bv
            q = q.reshape(b, l, KVH, GROUPS, HD).transpose(0, 2, 3, 1, 4)
            k = k.reshape(b, s, KVH, HD).transpose(0, 2, 1, 3)
            v = v.reshape(b, s, KVH, HD).transpose(0, 2, 1, 3)
            scale = 1.0 / jnp.sqrt(jnp.asarray(HD, q.dtype))
            scores = jnp.einsum('bkgld,bksd->bkgls', q, k) * scale
            scores = scores + encoder_attention_mask[:, :, None, :, :]
            attn = jax.nn.softmax(scores, axis=-1)
            out = jnp.einsum('bkgls,bksd->bkgld', attn, v)
            out = out.transpose(0, 3, 1, 2, 4).reshape(b, l, H)
            out = out @ Wo + bo
            x = out + hidden_state
            mu = jnp.mean(x, axis=-1, keepdims=True)
            var = jnp.var(x, axis=-1, keepdims=True)
            return (x - mu) * jax.lax.rsqrt(var + EPS) * gamma + beta
        return _gqa_forward(hidden_state, encoder_hidden_state, encoder_attention_mask, Wq, bq, Wk, bk, Wv, bv, Wo, bo, gamma, beta)

    def _L3_xattn_ref(x, state, ln1_w, ln1_b, ln2_w, ln2_b, maa_x, maa_w1, maa_w2, maa_stack, time_decay, td_w1, td_w2, u, Wr, Wk, Wv, Wg, Wo, gn_w, gn_b, ffn_maa_k, ffn_maa_r, Wfk, Wfr, Wfv):
        import jax, jax.numpy as jnp
        import numpy as np
        E, H, L, B = (512, 32, 256, 4)
        S = E // H
        DM, DD = (32, 64)

        def _ln(x, w, b, eps=1e-05):
            m = x.mean(-1, keepdims=True)
            v = ((x - m) ** 2).mean(-1, keepdims=True)
            return (x - m) / jnp.sqrt(v + eps) * w + b

        def _block(x, state, ln1_w, ln1_b, ln2_w, ln2_b, maa_x, maa_w1, maa_w2, maa_stack, time_decay, td_w1, td_w2, u, Wr, Wk, Wv, Wg, Wo, gn_w, gn_b, ffn_maa_k, ffn_maa_r, Wfk, Wfr, Wfv):
            b, l, e = x.shape
            h = u.shape[0]
            s_ = e // h
            xa = _ln(x, ln1_w, ln1_b)
            sx = jnp.concatenate([state[:, 1:2] - xa[:, :1], xa[:, :-1] - xa[:, 1:]], axis=1)
            xxx = jnp.tanh((xa + sx * maa_x) @ maa_w1).reshape(b, l, 5, DM)
            xxx = jnp.einsum('blfd,fde->blfe', xxx, maa_w2)
            xm = xa[:, :, None] + sx[:, :, None] * (maa_stack + xxx)
            xk, xw, xv, xr, xg = (xm[:, :, j] for j in range(5))
            w = jnp.exp(-jnp.exp(time_decay + jnp.tanh(xw @ td_w1) @ td_w2)).reshape(b, l, h, s_)
            r = (xr @ Wr.T).reshape(b, l, h, s_)
            k = (xk @ Wk.T).reshape(b, l, h, s_)
            v = (xv @ Wv.T).reshape(b, l, h, s_)
            g = jax.nn.silu(xg @ Wg.T)
            s0 = state[:, 2:2 + s_].reshape(b, h, s_, s_)

            def step(s, rkvw):
                r_t, k_t, v_t, w_t = rkvw
                a = k_t[..., :, None] * v_t[..., None, :]
                out = jnp.einsum('bhi,bhij->bhj', r_t, u * a + s)
                s = a + w_t[..., :, None] * s
                return (s, out)
            rkvw = tuple((jnp.moveaxis(t, 1, 0) for t in (r, k, v, w)))
            _, out = jax.lax.scan(step, s0, rkvw)
            out = jnp.moveaxis(out, 0, 1).reshape(b, l, e)
            og = out.reshape(b, l, h, s_)
            m = og.mean(-1, keepdims=True)
            va = ((og - m) ** 2).mean(-1, keepdims=True)
            og = ((og - m) / jnp.sqrt(va + 1e-05)).reshape(b, l, e) * gn_w + gn_b
            x1 = x + og * g @ Wo.T
            xc = _ln(x1, ln2_w, ln2_b)
            sx2 = jnp.concatenate([state[:, 0:1] - xc[:, :1], xc[:, :-1] - xc[:, 1:]], axis=1)
            xk2 = xc + sx2 * ffn_maa_k
            xr2 = xc + sx2 * ffn_maa_r
            rr = jax.nn.sigmoid(xr2 @ Wfr.T)
            kk = jnp.square(jax.nn.relu(xk2 @ Wfk.T))
            return x1 + rr * (kk @ Wfv.T)
        return _block(x, state, ln1_w, ln1_b, ln2_w, ln2_b, maa_x, maa_w1, maa_w2, maa_stack, time_decay, td_w1, td_w2, u, Wr, Wk, Wv, Wg, Wo, gn_w, gn_b, ffn_maa_k, ffn_maa_r, Wfk, Wfr, Wfv)
    x = _L0_xattn_ref(x, ctx_2048, mask_BxS2_bf1, L0_xattn_ln1_w, L0_xattn_ln1_b, L0_xattn_q_w, L0_xattn_q_b, L0_xattn_k_w, L0_xattn_k_b, L0_xattn_v_w, L0_xattn_v_b, L0_xattn_cproj_w, L0_xattn_cproj_b, L0_xattn_ln2_w, L0_xattn_ln2_b, L0_xattn_fc_w, L0_xattn_fc_b, L0_xattn_proj_w, L0_xattn_proj_b)
    x = _L1_xattn_ref(x, ctx_2048, mask_BxS2_bf1, L1_xattn_ln1_w, L1_xattn_ln1_b, L1_xattn_q_w, L1_xattn_q_b, L1_xattn_k_w, L1_xattn_k_b, L1_xattn_v_w, L1_xattn_v_b, L1_xattn_cproj_w, L1_xattn_cproj_b, L1_xattn_ln2_w, L1_xattn_ln2_b, L1_xattn_fc_w, L1_xattn_fc_b, L1_xattn_proj_w, L1_xattn_proj_b)
    x = _L2_xattn_ref(x, ctx_2048, mask_Bx1xSxS2_ff0, L2_xattn_Wq, L2_xattn_bq, L2_xattn_Wk, L2_xattn_bk, L2_xattn_Wv, L2_xattn_bv, L2_xattn_Wo, L2_xattn_bo, L2_xattn_gamma, L2_xattn_beta)
    x = _L3_xattn_ref(x, ctx_2048, L3_xattn_ln1_w, L3_xattn_ln1_b, L3_xattn_ln2_w, L3_xattn_ln2_b, L3_xattn_maa_x, L3_xattn_maa_w1, L3_xattn_maa_w2, L3_xattn_maa_stack, L3_xattn_time_decay, L3_xattn_td_w1, L3_xattn_td_w2, L3_xattn_u, L3_xattn_Wr, L3_xattn_Wk, L3_xattn_Wv, L3_xattn_Wg, L3_xattn_Wo, L3_xattn_gn_w, L3_xattn_gn_b, L3_xattn_ffn_maa_k, L3_xattn_ffn_maa_r, L3_xattn_Wfk, L3_xattn_Wfr, L3_xattn_Wfv)
    return x

_drawn_inputs = setup_inputs


def setup_inputs(seed=0):
    import zlib

    import numpy as np

    out = dict(_drawn_inputs(seed))
    spreads = {'L0_xattn_ln1_w': (1.0, 0.6),
     'L0_xattn_ln1_b': (0.0, 0.8),
     'L0_xattn_q_b': (0.0, 0.8),
     'L0_xattn_k_b': (0.0, 0.8),
     'L0_xattn_v_b': (0.0, 0.1),
     'L0_xattn_cproj_b': (0.0, 0.1),
     'L0_xattn_ln2_w': (1.0, 0.2),
     'L0_xattn_ln2_b': (0.0, 0.353),
     'L0_xattn_fc_b': (0.0, 0.1),
     'L0_xattn_proj_b': (0.0, 0.1),
     'L1_xattn_ln1_w': (1.0, 0.6),
     'L1_xattn_ln1_b': (0.0, 0.8),
     'L1_xattn_q_b': (0.0, 0.8),
     'L1_xattn_k_b': (0.0, 0.8),
     'L1_xattn_v_b': (0.0, 0.1),
     'L1_xattn_cproj_b': (0.0, 0.1),
     'L1_xattn_ln2_w': (1.0, 0.2),
     'L1_xattn_ln2_b': (0.0, 0.358),
     'L1_xattn_fc_b': (0.0, 0.1),
     'L1_xattn_proj_b': (0.0, 0.1),
     'L2_xattn_bq': (0.0, 0.8),
     'L2_xattn_bk': (0.0, 0.8),
     'L2_xattn_bv': (0.0, 0.1),
     'L2_xattn_bo': (0.0, 0.1),
     'L2_xattn_gamma': (1.0, 0.2),
     'L2_xattn_beta': (0.0, 0.1),
     'L3_xattn_ln1_w': (1.0, 0.2),
     'L3_xattn_ln1_b': (0.0, 0.28),
     'L3_xattn_ln2_w': (1.0, 0.6),
     'L3_xattn_ln2_b': (0.0, 0.8),
     'L3_xattn_gn_w': (1.0, 0.6),
     'L3_xattn_gn_b': (0.0, 0.741)}
    factors = {'L0_xattn_q_w': 7.372,
     'L0_xattn_k_w': 7.333,
     'L1_xattn_q_w': 8.0,
     'L1_xattn_k_w': 7.919,
     'L2_xattn_Wq': 7.497,
     'L2_xattn_Wk': 7.325,
     'L3_xattn_maa_x': 8.0,
     'L3_xattn_maa_w1': 2.998,
     'L3_xattn_maa_w2': 2.996,
     'L3_xattn_td_w1': 8.0,
     'L3_xattn_td_w2': 8.0,
     'L3_xattn_u': 2.945,
     'L3_xattn_ffn_maa_k': 5.93,
     'L3_xattn_ffn_maa_r': 8.0,
     'L3_xattn_Wfr': 4.055}
    for name, (base, spread) in spreads.items():
        noise = np.random.default_rng([zlib.crc32(name.encode()), seed]).standard_normal(out[name].shape)
        drawn = base * np.exp(spread * noise) if base else spread * noise
        out[name] = jnp.asarray(drawn.astype(out[name].dtype))
    for name, factor in factors.items():
        out[name] = (out[name] * factor).astype(out[name].dtype)
    return out
```

```python
from contextlib import ExitStack

import concourse.bass as bass
from concourse import mybir

F32 = mybir.dt.float32
U8 = mybir.dt.uint8
ALU = mybir.AluOpType
ACT = mybir.ActivationFunctionType

P = 128
B = 4
T = 512
D = 512
S = 1024
FT = D // P
QT = T // P
KT = S // P
HPG = 4
HR = P // HPG
F_TILES = 4 * D // P
FF = 4
UNITS = HPG * QT
BIG = 1.0e30


def attention_block(nc, name, layers, groups, scale, dram, x_res, feed_forward):
    G = groups
    with ExitStack() as ctx:
        def sb(what, shape, dt=F32):
            return ctx.enter_context(nc.sbuf_tensor(f"{name}_{what}", shape, dt))

        def sem(what):
            return ctx.enter_context(nc.semaphore(f"{name}_{what}"))

        bank = [ctx.enter_context(nc.psum_tensor(f"{name}_score{i}", [P, 2 * 512], F32)) for i in range(2)]
        half = [ctx.enter_context(nc.psum_tensor(f"{name}_half{i}", [P, 512], F32)) for i in range(2)]
        head_out = ctx.enter_context(nc.psum_tensor(f"{name}_head_out", [P, 512], F32))
        turn = ctx.enter_context(nc.psum_tensor(f"{name}_turn", [P, 512], F32))
        four = [bank[i // 2][:, 512 * (i % 2):512 * (i % 2) + 512] for i in range(4)]

        ident = sb("ident", [P, P])
        ones = sb("ones", [1, P])
        ctx_t = sb("ctx_t", [P, FT, S])
        xn = sb("xn", [P, QT, D])
        h_t = sb("h_t", [P, FT, T])
        w_qkv = sb("w_qkv", [P, 3, FT, P])
        w_out = sb("w_out", [P, G, D])
        vec = sb("vec", [P, layers, dram["vec"].shape[2]])
        row = sb("row", [1, 2, D])
        q_t = sb("q_t", [P, T])
        k_t = sb("k_t", [P, S])
        v = sb("v", [P, KT, P])
        masked = sb("masked", [P, 2, S])
        probs = sb("probs", [P, 2, S])
        probs_t = sb("probs_t", [P, 2, KT, T])
        low = sb("low", [P, UNITS])
        total = sb("total", [P, UNITS])
        rec = sb("rec", [P, UNITS])
        out_u = sb("out_u", [P, T])
        out_n = sb("out_n", [P, QT, P])
        o_t = sb("o_t", [P, G, T])
        stats = sb("stats", [P, QT, 6])
        mv = sb("mv", [P, QT, 2])
        rstd = sb("rstd", [P, QT, 1])
        power = sb("power", [P, QT, 1])
        if feed_forward:
            mask_u8 = sb("mask_u8", [P, S], U8)
            mask = sb("mask", [P, 1, S])
            w_fc = [sb(f"w_fc{i}", [P, FT, P]) for i in range(FF)]
            w_pr = [sb(f"w_pr{i}", [P, D]) for i in range(FF)]
            hid = [sb(f"hid{i}", [P, T]) for i in range(2)]
            QB, KB, VB, LW, LB, LW2, LB2, FB = 0, G, 2 * G, 3 * G, 3 * G + 4, 3 * G + 8, 3 * G + 12, 3 * G + 16
        else:
            mask = sb("mask", [P, QT, S])
            gamma = sb("gamma", [P, D])
            beta = sb("beta", [P, D])
            QB, KB, VB = 0, G, 2 * G
        LN = 2 if feed_forward else 1
        NORMS = LN

        s_pass_pe, s_pass_act, s_pass_dve, s_pass_sp = (sem("pass_" + e) for e in ("pe", "act", "dve", "sp"))
        CONST = 16 * (3 if feed_forward else 5)
        s_const = sem("const_loaded")
        s_ctx = sem("ctx_loaded")
        s_wqkv = sem("wqkv_loaded")
        s_wout = sem("wout_loaded")
        s_row = sem("row_loaded")
        s_mask = sem("mask_loaded")
        s_mready = sem("mask_ready")
        s_xn = sem("xn_ready")
        s_tp = sem("h_turned")
        s_ht = sem("h_ready")
        s_pj = sem("projected")
        s_pjd = sem("q_v0_copied")
        s_pja = sem("k_v1_copied")
        s_qk = sem("scores_ready")
        s_low = sem("scores_masked")
        s_exp = sem("probs_ready")
        s_tr = sem("probs_turned")
        s_ptd = sem("probs_t_first_half")
        s_pta = sem("probs_t_second_half")
        s_av = sem("head_summed")
        s_ou = sem("out_copied")
        s_n1 = sem("out_token_major")
        s_rec = sem("rec_ready")
        s_on = sem("out_normalised")
        s_n2 = sem("out_feature_major")
        s_ot = sem("o_t_ready")
        s_c = sem("attended")
        s_dve = sem("dve_chain")
        s_xadd = sem("x_updated")
        s_power = sem("power_set")
        s_var = sem("variance_ready")
        s_rstd = sem("rstd_ready")
        if feed_forward:
            s_wf = [sem(f"ff_weights_loaded{i}") for i in range(FF)]
            s_h1 = sem("hidden_ready")
            s_gl = sem("gelu_done")
            s_p2 = [sem(f"hidden_used{i}") for i in range(FF)]

        block = ctx.enter_context(nc.Block())

        @block.sync
        def _(sp):
            sp.dma_start(ident[:, :], dram["ident"]).then_inc(s_const, 16)
            sp.dma_start(ones[:, :], dram["ones"]).then_inc(s_const, 16)
            sp.dma_start(vec[:, :, :], dram["vec"]).then_inc(s_const, 16)
            if not feed_forward:
                sp.dma_start(gamma[:, :], dram["gamma"].to_broadcast((P, D))).then_inc(s_const, 16)
                sp.dma_start(beta[:, :], dram["beta"].to_broadcast((P, D))).then_inc(s_const, 16)
            with sp.Fori(0, layers) as lay:
                with sp.Fori(0, B) as b:
                    n = lay * B + b
                    sp.wait_ge(s_pj, 1 + n * (5 * G))
                    sp.sem_inc(s_pass_sp, 1)
                    sp.dma_start(ctx_t[:, :, :], dram["ctx_t"][bass.ds(b, 1)].rearrange("a p f s -> (a p) f s")).then_inc(s_ctx, 16)
                    sp.wait_ge(s_low, 1 + n * (UNITS * G))
                    sp.sem_inc(s_pass_sp, 1)
                    if feed_forward:
                        sp.dma_start(mask_u8[:, :], dram["mask"][bass.ds(b, 1), :].to_broadcast((P, S))).then_inc(s_mask, 16)
                    else:
                        sp.dma_start(mask[:, :, :], dram["mask"][bass.ds(b, 1)].rearrange("a p q s -> (a p) q s")).then_inc(s_mask, 16)
                    with sp.Fori(0, G) as g:
                        sp.wait_ge(s_pj, 1 + n * (5 * G) + g * 5)
                        sp.sem_inc(s_pass_sp, 1)
                        sp.dma_start(w_qkv[:, :, :, :], dram["w_qkv"][bass.ds(lay * G + g, 1)].rearrange("a p k f m -> (a p) k f m")).then_inc(s_wqkv, 16)
                    sp.wait_ge(s_xadd, 1 + n * (QT * LN))
                    sp.sem_inc(s_pass_sp, 1)
                    sp.dma_start(w_out[:, :, :], dram["w_out"][bass.ds(lay, 1)].rearrange("a p f m -> (a p) f m")).then_inc(s_wout, 16)
                    sp.dma_start(row[:, :, :], dram["row"][bass.ds(lay, 1)]).then_inc(s_row, 16)
                    if feed_forward:
                        with sp.Fori(0, F_TILES // FF) as ff:
                            for i in range(FF):
                                sp.wait_ge(s_p2[i], 1 + n * (F_TILES // FF) + ff)
                                sp.sem_inc(s_pass_sp, 1)
                                sp.dma_start(w_fc[i][:, :, :], dram["w_fc"][bass.ds(lay * F_TILES + ff * FF + i, 1)].rearrange("a p f m -> (a p) f m")).then_inc(s_wf[i], 16)
                                sp.dma_start(w_pr[i][:, :], dram["w_pr"][bass.ds(lay * F_TILES + ff * FF + i, 1)].rearrange("a p m -> (a p) m")).then_inc(s_wf[i], 16)

        @block.tensor
        def _(pe):
            for s in (s_pj, s_tp) + ((*s_p2,) if feed_forward else ()):
                pe.sem_inc(s, 1)
            pe.wait_ge(s_const, CONST)

            def turn_stream(n, which):
                pe.wait_ge(s_xn, n * LN + which + 1)
                for ft in range(FT):
                    for qt in range(QT):
                        last = pe.transpose(four[ft][:, qt * P:(qt + 1) * P], xn[:, qt, ft * P:(ft + 1) * P], ident[:, :])
                    last.then_inc(s_tp, 1)

            with pe.Fori(0, layers) as lay:
                with pe.Fori(0, B) as b:
                    n = lay * B + b
                    pe.wait_ge(s_xadd, 1 + n * (QT * LN))
                    turn_stream(n, 0)
                    pe.wait_ge(s_ht, n * (FT * LN) + FT)
                    pe.wait_ge(s_ctx, n * 16 + 16)
                    pe.sem_inc(s_pass_pe, 1)
                    with pe.Fori(0, G) as g:
                        m = n * G + g
                        pe.wait_ge(s_wqkv, m * 16 + 16)
                        pe.wait_ge(s_low, 1 + m * UNITS)
                        pe.wait_ge(s_ot, 1 + m)
                        for ft in range(FT):
                            last = pe.matmul(four[0], w_qkv[:, 0, ft, :], h_t[:, ft, :], start=(ft == 0), stop=(ft == FT - 1))
                        last.then_inc(s_pj, 1)
                        for s in range(2):
                            for ft in range(FT):
                                last = pe.matmul(four[1 + s], w_qkv[:, 1, ft, :], ctx_t[:, ft, 512 * s:512 * s + 512], start=(ft == 0), stop=(ft == FT - 1))
                            last.then_inc(s_pj, 1)
                        for s in range(2):
                            dst = four[3] if s == 0 else turn[:, :]
                            for c in range(4):
                                kt = 4 * s + c
                                for ft in range(FT):
                                    last = pe.matmul(dst[:, c * P:(c + 1) * P], ctx_t[:, ft, kt * P:(kt + 1) * P], w_qkv[:, 2, ft, :], start=(ft == 0), stop=(ft == FT - 1))
                            last.then_inc(s_pj, 1)
                        pe.wait_ge(s_pjd, m * 2 + 2)
                        pe.wait_ge(s_pja, m * 3 + 3)

                        def scores(u):
                            j, qt = divmod(u, QT)
                            if u >= 2:
                                pe.wait_ge(s_low, 1 + m * UNITS + (u - 1))
                            for s in range(2):
                                last = pe.matmul(bank[u % 2][:, 512 * s:512 * s + 512], q_t[HR * j:HR * j + HR, qt * P:(qt + 1) * P],
                                                 k_t[HR * j:HR * j + HR, 512 * s:512 * s + 512], start=True, stop=True)
                            last.then_inc(s_qk, 1)

                        def turn_probs(u):
                            pe.wait_ge(s_exp, 1 + m * UNITS + (u + 1))
                            for s in range(2):
                                pe.wait_ge((s_ptd, s_pta)[s], 1 + m * UNITS + u)
                                for c in range(4):
                                    last = pe.transpose(half[s][:, c * P:(c + 1) * P], probs[:, u % 2, (4 * s + c) * P:(4 * s + c + 1) * P], ident[:, :])
                                last.then_inc(s_tr, 1)

                        def weigh(j):
                            pe.wait_ge(s_ptd, 1 + m * UNITS + QT * (j + 1))
                            pe.wait_ge(s_pta, 1 + m * UNITS + QT * (j + 1))
                            if j == 0:
                                pe.wait_ge(s_ou, 1 + m)
                            for kt in range(KT):
                                last = pe.matmul(head_out[HR * j:HR * j + HR, :], v[:, kt, HR * j:HR * j + HR], probs_t[:, j % 2, kt, :],
                                                 start=(kt == 0), stop=(kt == KT - 1))
                            last.then_inc(s_av, 1)

                        for i in range(UNITS + 3):
                            if i < UNITS:
                                scores(i)
                            if 2 <= i < UNITS + 2:
                                turn_probs(i - 2)
                            if i >= 3 and (i - 3) % QT == QT - 1:
                                weigh((i - 3) // QT)
                        pe.wait_ge(s_ou, 1 + m + 1)
                        for qt in range(QT):
                            last = pe.transpose(turn[:, qt * P:(qt + 1) * P], out_u[:, qt * P:(qt + 1) * P], ident[:, :])
                        last.then_inc(s_n1, 1)
                        pe.wait_ge(s_on, m + 1)
                        for qt in range(QT):
                            last = pe.transpose(turn[:, qt * P:(qt + 1) * P], out_n[:, qt, :], ident[:, :])
                        last.then_inc(s_n2, 1)
                    pe.wait_ge(s_ot, 1 + n * G + G)
                    pe.wait_ge(s_wout, n * 16 + 16)
                    pe.wait_ge(s_row, n * 16 + 16)
                    pe.wait_ge(s_low, 1 + n * (G * UNITS) + G * UNITS)
                    for qt in range(QT):
                        pe.matmul(four[qt], ones[:, :], row[:, 0, :], start=True, stop=False)
                        for g in range(G):
                            last = pe.matmul(four[qt], o_t[:, g, qt * P:(qt + 1) * P], w_out[:, g, :], start=False, stop=(g == G - 1))
                        last.then_inc(s_c, 1)
                    if feed_forward:
                        turn_stream(n, 1)
                        pe.wait_ge(s_ht, n * (FT * LN) + 2 * FT)
                        for qt in range(QT):
                            pe.matmul(four[qt], ones[:, :], row[:, 1, :], start=True, stop=False, skip_group_check=True)
                        pe.sem_inc(s_pass_pe, 1)
                        with pe.Fori(0, F_TILES // FF) as ff:
                            k = n * (F_TILES // FF) + ff

                            def hidden(i):
                                pe.wait_ge(s_wf[i], k * 32 + 32)
                                pe.wait_ge(s_gl, 1 + k * FF + max(i - 1, 0))
                                for ft in range(FT):
                                    last = pe.matmul(half[i % 2][:, :], w_fc[i][:, ft, :], h_t[:, ft, :], start=(ft == 0), stop=(ft == FT - 1))
                                last.then_inc(s_h1, 1)

                            def back(i):
                                pe.wait_ge(s_gl, 1 + k * FF + (i + 1))
                                for qt in range(QT):
                                    last = pe.matmul(four[qt], hid[i % 2][:, qt * P:(qt + 1) * P], w_pr[i][:, :], start=False, stop=False, skip_group_check=True)
                                last.then_inc(s_p2[i], 1)

                            hidden(0)
                            for i in range(1, FF):
                                hidden(i)
                                back(i - 1)
                            back(FF - 1)

        @block.gpsimd
        def _(pool):
            pool.memset(power[:, :, :], -0.5).then_inc(s_power, 1)
            pool.wait_ge(s_power, 1)
            with pool.Fori(0, layers * B * NORMS) as k:
                pool.wait_ge(s_var, k + 1)
                pool.tensor_tensor(rstd[:, :, :], rstd[:, :, :], power[:, :, :], ALU.pow).then_inc(s_rstd, 1)

        @block.scalar
        def _(act):
            for s in (s_ot, s_pta, s_ou, s_exp) + ((s_gl,) if feed_forward else ()):
                act.sem_inc(s, 1)
            act.wait_ge(s_const, CONST)

            def feature_major(n, lay, which):
                for ft in range(FT):
                    act.wait_ge(s_tp, 1 + n * (FT * LN) + (which * FT + ft + 1))
                    if feed_forward:
                        lw, lb = ((LW, LB), (LW2, LB2))[which]
                        act.activation(h_t[:, ft, :], four[ft], ACT.Identity, bias=vec[:, bass.ds(lay, 1), lb + ft:lb + ft + 1].rearrange("p a b -> p (a b)"),
                                       scale=vec[:, bass.ds(lay, 1), lw + ft:lw + ft + 1].rearrange("p a b -> p (a b)")).then_inc(s_ht, 1)
                    else:
                        act.copy(h_t[:, ft, :], four[ft]).then_inc(s_ht, 1)

            def column(lay, c):
                return vec[:, bass.ds(lay, 1), bass.ds(c, 1)].rearrange("p a b -> p (a b)")

            with act.Fori(0, layers) as lay:
                with act.Fori(0, B) as b:
                    n = lay * B + b
                    feature_major(n, lay, 0)
                    with act.Fori(0, G) as g:
                        m = n * G + g
                        for s in range(2):
                            act.wait_ge(s_pj, 1 + m * 5 + (s + 2))
                            act.sem_inc(s_pass_act, 1)
                            act.activation(k_t[:, 512 * s:512 * s + 512], four[1 + s], ACT.Identity, bias=column(lay, g + KB)).then_inc(s_pja, 1)
                        act.wait_ge(s_pj, 1 + m * 5 + 5)
                        act.copy(v[:, 4:8, :].rearrange("p a b -> p (a b)"), turn[:, :]).then_inc(s_pja, 1)
                        for i in range(UNITS + 2):
                            if i < UNITS:
                                act.wait_ge(s_low, 1 + m * UNITS + (i + 1))
                                if i >= 2:
                                    act.wait_ge(s_tr, m * (2 * UNITS) + 2 * (i - 1))
                                act.activation(probs[:, i % 2, :], masked[:, i % 2, :], ACT.Exp, bias=low[:, i:i + 1], scale=-1.0,
                                               accum_out=total[:, i:i + 1]).then_inc(s_exp, 1)
                            if i >= 2:
                                u = i - 2
                                j, qt = divmod(u, QT)
                                act.wait_ge(s_tr, m * (2 * UNITS) + (2 * u + 2))
                                if qt == 0 and j >= 2:
                                    act.wait_ge(s_av, m * HPG + (j - 1))
                                act.copy(probs_t[:, j % 2, 4:8, qt * P:(qt + 1) * P],
                                         half[1][:, :].rearrange("p (a b) -> p a b", b=P)).then_inc(s_pta, 1)
                        act.wait_ge(s_av, m * HPG + HPG)
                        act.copy(out_u[:, :], head_out[:, :]).then_inc(s_ou, 1)
                        act.wait_ge(s_n2, m + 1)
                        act.sem_inc(s_pass_act, 1)
                        act.activation(o_t[:, bass.ds(g, 1), :].rearrange("p a b -> p (a b)"), turn[:, :], ACT.Identity, bias=column(lay, g + VB)).then_inc(s_ot, 1)
                    if feed_forward:
                        feature_major(n, lay, 1)
                        with act.Fori(0, F_TILES // FF) as ff:
                            k = n * (F_TILES // FF) + ff
                            for i in range(FF):
                                act.wait_ge(s_h1, k * FF + (i + 1))
                                act.wait_ge(s_p2[(i + 2) % FF], 1 + k + (i >= 2))
                                act.sem_inc(s_pass_act, 1)
                                act.activation(hid[i % 2][:, :], half[i % 2][:, :], ACT.Gelu_apprx_tanh, bias=column(lay, ff * FF + (FB + i))).then_inc(s_gl, 1)

        @block.vector
        def _(dve):
            for s in (s_low, s_xadd, s_ptd):
                dve.sem_inc(s, 1)
            dve.wait_ge(s_const, CONST)

            CH = 2 * QT
            with dve.Fori(0, layers) as lay:
                with dve.Fori(0, B) as b:
                    n = lay * B + b
                    chain = n * (CH * LN + (0 if feed_forward else 3 * QT))
                    if feed_forward:
                        for qt in range(QT):
                            dve.sem_inc(s_pass_dve, 1)
                            dve.bn_stats(stats[:, qt, :], x_res[:, bass.ds(b, 1), qt, :].rearrange("p a d -> p (a d)")).then_inc(s_dve, 1)
                        for qt in range(QT):
                            dve.wait_ge(s_dve, chain + (qt + 1))
                            dve.sem_inc(s_pass_dve, 1)
                            dve.bn_aggr(mv[:, qt, :], stats[:, qt, :]).then_inc(s_dve, 1)
                        dve.wait_ge(s_dve, chain + 2 * QT)
                        dve.tensor_scalar(rstd[:, :, 0:1], mv[:, :, 1:2], 1e-5, None, ALU.add).then_inc(s_var, 1)
                        dve.wait_ge(s_rstd, n * NORMS + 1)
                        dve.wait_ge(s_tp, 1 + n * (FT * LN))
                        for qt in range(QT):
                            last = dve.tensor_scalar(xn[:, qt, :], x_res[:, bass.ds(b, 1), qt, :].rearrange("p a d -> p (a d)"), mv[:, qt, 0:1], rstd[:, qt, 0:1],
                                                     ALU.subtract, ALU.mult)
                        last.then_inc(s_xn, 1)
                        dve.wait_ge(s_mask, n * 16 + 16)
                        dve.tensor_scalar(mask[:, 0, :], mask_u8[:, :], -BIG, BIG, ALU.mult, ALU.add).then_inc(s_mready, 1)
                    else:
                        dve.wait_ge(s_tp, 1 + n * (FT * LN))
                        dve.tensor_copy(xn[:, :, :], x_res[:, bass.ds(b, 1), :, :].rearrange("p a q d -> p (a q) d")).then_inc(s_xn, 1)
                        dve.wait_ge(s_mask, n * 16 + 16)
                        dve.tensor_scalar(mask[:, :, :], mask[:, :, :], -1.0, None, ALU.mult).then_inc(s_mready, 1)
                    dve.wait_ge(s_mready, n + 1)
                    dve.sem_inc(s_pass_dve, 1)
                    with dve.Fori(0, G) as g:
                        m = n * G + g
                        dve.wait_ge(s_pj, 1 + m * 5 + 1)
                        dve.tensor_scalar(q_t[:, :], four[0], vec[:, bass.ds(lay, 1), bass.ds(g + QB, 1)].rearrange("p a b -> p (a b)"), -scale,
                                          ALU.add, ALU.mult).then_inc(s_pjd, 1)
                        dve.wait_ge(s_pj, 1 + m * 5 + 4)
                        dve.tensor_copy(v[:, 0:4, :].rearrange("p a b -> p (a b)"), four[3]).then_inc(s_pjd, 1)
                        for i in range(UNITS + 2):
                            if i < UNITS:
                                qt = i % QT
                                dve.wait_ge(s_qk, m * UNITS + (i + 1))
                                if i >= 2:
                                    dve.wait_ge(s_exp, 1 + m * UNITS + (i - 1))
                                else:
                                    dve.wait_ge(s_exp, 1 + m * UNITS)
                                dve.sem_inc(s_pass_dve, 1)
                                dve.tensor_tensor_reduce(out=masked[:, i % 2, :], in0=bank[i % 2][:, :], in1=mask[:, 0 if feed_forward else qt, :], scale=1.0,
                                                         scalar=3.0e38, op0=ALU.add, op1=ALU.min, accum_out=low[:, i:i + 1]).then_inc(s_low, 1)
                            if i >= 2:
                                u = i - 2
                                j, qt = divmod(u, QT)
                                dve.wait_ge(s_tr, m * (2 * UNITS) + (2 * u + 1))
                                if qt == 0 and j >= 2:
                                    dve.wait_ge(s_av, m * HPG + (j - 1))
                                dve.tensor_copy(probs_t[:, j % 2, 0:4, qt * P:(qt + 1) * P],
                                                half[0][:, :].rearrange("p (a b) -> p a b", b=P)).then_inc(s_ptd, 1)
                        dve.wait_ge(s_exp, 1 + m * UNITS + UNITS)
                        dve.reciprocal(rec[:, :], total[:, :]).then_inc(s_rec, 1)
                        dve.wait_ge(s_rec, m + 1)
                        dve.wait_ge(s_n1, m + 1)
                        dve.tensor_tensor(out_n[:, :, :].rearrange("p q (j d) -> p q j d", j=HPG), turn[:, :].rearrange("p (q j d) -> p q j d", q=QT, j=HPG),
                                          rec[:, :].rearrange("p (j q a) -> p q j a", j=HPG, a=1).to_broadcast((P, QT, HPG, HR)), ALU.mult).then_inc(s_on, 1)
                    for qt in range(QT):
                        xs = x_res[:, bass.ds(b, 1), qt, :].rearrange("p a d -> p (a d)")
                        dve.wait_ge(s_c, n * QT + (qt + 1))
                        dve.tensor_tensor(xs, xs, four[qt], ALU.add).then_inc(s_xadd, 1)
                    dve.wait_ge(s_xadd, 1 + n * (QT * LN) + QT)
                    chain2 = chain + (CH if feed_forward else 0)
                    for qt in range(QT):
                        dve.sem_inc(s_pass_dve, 1)
                        dve.bn_stats(stats[:, qt, :], x_res[:, bass.ds(b, 1), qt, :].rearrange("p a d -> p (a d)")).then_inc(s_dve, 1)
                    for qt in range(QT):
                        dve.wait_ge(s_dve, chain2 + (qt + 1))
                        dve.sem_inc(s_pass_dve, 1)
                        dve.bn_aggr(mv[:, qt, :], stats[:, qt, :]).then_inc(s_dve, 1)
                    dve.wait_ge(s_dve, chain2 + 2 * QT)
                    dve.tensor_scalar(rstd[:, :, 0:1], mv[:, :, 1:2], 1e-5 if feed_forward else 1e-6, None, ALU.add).then_inc(s_var, 1)
                    dve.wait_ge(s_rstd, n * NORMS + NORMS)
                    if feed_forward:
                        for qt in range(QT):
                            last = dve.tensor_scalar(xn[:, qt, :], x_res[:, bass.ds(b, 1), qt, :].rearrange("p a d -> p (a d)"), mv[:, qt, 0:1], rstd[:, qt, 0:1],
                                                     ALU.subtract, ALU.mult)
                        last.then_inc(s_xn, 1)
                        dve.wait_ge(s_p2[FF - 1], 1 + n * (F_TILES // FF) + F_TILES // FF)
                        for qt in range(QT):
                            xs = x_res[:, bass.ds(b, 1), qt, :].rearrange("p a d -> p (a d)")
                            dve.tensor_tensor(xs, xs, four[qt], ALU.add).then_inc(s_xadd, 1)
                        dve.wait_ge(s_xadd, 1 + n * (QT * LN) + QT * LN)
                    else:
                        for step in range(3):
                            for qt in range(QT):
                                xs = x_res[:, bass.ds(b, 1), qt, :].rearrange("p a d -> p (a d)")
                                if step:
                                    dve.wait_ge(s_dve, chain2 + (CH + (step - 1) * QT + qt + 1))
                                if step == 0:
                                    dve.tensor_scalar(xs, xs, mv[:, qt, 0:1], rstd[:, qt, 0:1], ALU.subtract, ALU.mult).then_inc(s_dve, 1)
                                elif step == 1:
                                    dve.tensor_tensor(xs, xs, gamma[:, :], ALU.mult).then_inc(s_dve, 1)
                                else:
                                    dve.tensor_tensor(xs, xs, beta[:, :], ALU.add).then_inc(s_dve, 1)
                        dve.wait_ge(s_dve, chain2 + (CH + 3 * QT))

VEC3 = ("ln1_w", "ln1_b", "ln2_w", "ln2_b", "maa_x", "maa_k", "maa_w", "maa_v", "maa_r", "maa_g", "decay", "u", "gn_w", "gn_b", "ffn_k", "ffn_r")


def time_mix_block(nc, dram, x_res):
    NAMES = ("k", "w", "v", "r", "g")
    SLOTS = 23
    N = 16
    with ExitStack() as ctx:
        def sb(what, shape, dt=F32):
            return ctx.enter_context(nc.sbuf_tensor(f"mix_{what}", shape, dt))

        def sem(what):
            return ctx.enter_context(nc.semaphore(f"mix_{what}"))

        bank = [ctx.enter_context(nc.psum_tensor(f"mix_bank{i}", [P, 512], F32)) for i in range(8)]
        ident = sb("ident", [P, P])
        spread = sb("spread", [P, N, P])
        gather = sb("gather", [P, N, P])
        heads = sb("heads", [P, P])
        w_maa1 = sb("w_maa1", [P, FT, 5 * 32])
        w_maa2 = sb("w_maa2", [P, D])
        w_maa2g = sb("w_maa2g", [32, D])
        w_td1 = sb("w_td1", [P, FT, 64])
        w_td2 = sb("w_td2", [64, D])
        w_big = sb("w_big", [P, 8, FT, D])
        W = {name: w_big[:, i, :, :] for i, name in enumerate(("k", "v", "r", "g", "o", "fk", "fr", "fv"))}
        vec = sb("vec", [P, dram["vec"].shape[1]])
        column = {name: (lambda i: (lambda ft: vec[:, 4 * i + ft:4 * i + ft + 1]))(i) for i, name in enumerate(VEC3)}
        xn = sb("xn", [P, QT, D])
        xa = sb("xa", [P, FT, T + 1])
        sx = xn
        mixed = [sb(f"mixed{i}", [P, FT, T]) for i in range(2)]
        lora = sb("lora", [P, T])
        tmp = sb("tmp", [P, T])
        lora_g = sb("lora_g", [32, T])
        lora_w = tmp[0:64, :]
        act_t = {name: sb(f"{name}_t", [P, FT, T]) for name in NAMES}
        s0 = sb("s0", [P, FT, N])
        before = sb("before", [P, B, 2, FT])
        a_j = [mixed[1][:, i, :] for i in range(2)]
        state = [sb(f"state{i}", [P, T + 1]) for i in range(2)]
        y_j = [mixed[1][:, 2 + i, :] for i in range(2)]
        o_s = lora
        stats = sb("stats", [P, QT, 6])
        mv = sb("mv", [P, QT, 2])
        rstd = sb("rstd", [P, QT, 1])
        power = sb("power", [P, QT, 1])
        og = mixed[0]
        kk = act_t["r"]
        gate = act_t["k"]

        LOADS = 12 * 16
        s_const = sem("const_loaded")
        s_first = sem("first_loaded")
        s_xn, s_tp, s_xa, s_sx, s_z = (sem(x) for x in ("xn_ready", "turned", "xa_ready", "sx_ready", "z_ready"))
        s_pp, s_pev = sem("projected"), sem("projection_copied")
        s_xx = sem("mix_ready")
        s_mix = sem("mixed_ready")
        s_vb, s_a = sem("v_spread"), sem("a_ready")
        s_s0, s_st, s_y, s_yu = sem("state_first"), sem("state_ready"), sem("y_ready"), sem("y_used")
        s_ruk, s_gp, s_gd, s_ga = sem("ruk_ready"), sem("norm_pe"), sem("norm_dve"), sem("norm_act")
        s_og, s_dec, s_pair, s_bonus, s_veps, s_half = (sem(x) for x in ("og_ready", "decay_exp", "mix_product", "bonus_ready", "norm_eps", "gate_product"))
        s_c, s_xadd = sem("mixed_out"), sem("x_updated")
        s_kk, s_kku, s_rr, s_gate, s_fv, s_end = (sem(x) for x in ("kk_psum", "kk_ready", "rr_psum", "gate_ready", "fv_psum", "x_final"))
        s_power, s_var, s_rstd, s_bn, s_mv = (sem(x) for x in ("power_set", "variance_ready", "rstd_ready", "bn_stats", "bn_aggr"))
        s_relu = sem("relu_ready")
        pass_by = {e: sem("pass_" + e) for e in ("pe", "act", "dve", "pool", "sp")}
        block = ctx.enter_context(nc.Block())

        @block.sync
        def _(sp):
            for dst, name in ((ident[:, :], "ident"), (spread[:, :, :], "spread"), (gather[:, :, :], "gather"), (heads[:, :], "heads"),
                              (w_maa1[:, :, :], "maa1"), (w_maa2[:, :], "maa2"), (w_maa2g[:, :], "maa2g"), (w_td1[:, :, :], "td1"),
                              (w_td2[:, :], "td2"), (vec[:, :], "vec"), (before[:, :, :, :], "before")):
                sp.dma_start(dst, dram[name]).then_inc(s_const, 16)
            sp.dma_start(w_big[:, :, :, :], dram["big"]).then_inc(s_const, 16)
            with sp.Fori(0, B) as b:
                sp.wait_ge(s_end, 1 + b * QT)
                sp.sem_inc(pass_by["sp"], 1)
                sp.dma_start(s0[:, :, :], dram["s0"][bass.ds(b, 1)].rearrange("a p f j -> (a p) f j")).then_inc(s_first, 16)

        @block.tensor
        def _(pe):
            for s in (s_pp, s_xx, s_vb, s_yu, s_gp, s_c, s_kk, s_rr, s_fv, s_tp):
                pe.sem_inc(s, 1)
            pe.wait_ge(s_const, LOADS)

            def turn_stream(b, which):
                pe.wait_ge(s_xn, b * 2 + (which + 1))
                for ft in range(FT):
                    for qt in range(QT):
                        last = pe.transpose(bank[ft][:, qt * P:(qt + 1) * P], xn[:, qt, ft * P:(ft + 1) * P], ident[:, :])
                    last.then_inc(s_tp, 1)

            def slot(b, s):
                pe.wait_ge(s_pev, 1 + b * SLOTS + (s - 1 if s >= 2 else 0))
                return bank[4 + s % 2]

            with pe.Fori(0, B) as b:
                pe.wait_ge(s_end, 1 + b * QT)
                turn_stream(b, 0)
                pe.wait_ge(s_z, b * FT + FT)
                for s, (lo, hi) in enumerate(((0, 128), (128, 160))):
                    dst = slot(b, s)
                    for ft in range(FT):
                        last = pe.matmul(dst[0:hi - lo, :], w_maa1[:, ft, lo:hi], mixed[0][:, ft, :], start=(ft == 0), stop=(ft == FT - 1))
                    last.then_inc(s_pp, 1)

                def mix_in(f):
                    pe.wait_ge(s_pev, 1 + b * SLOTS + 2)
                    for ft in range(FT):
                        i = f * FT + ft
                        pe.wait_ge(s_pair, 1 + b * (5 * FT) + max(i - 1, 0))
                        if f < 4:
                            pe.matmul(bank[6 + i % 2][:, :], w_maa2[32 * f:32 * f + 32, ft * P:(ft + 1) * P], lora[32 * f:32 * f + 32, :], start=True, stop=True).then_inc(s_xx, 1)
                        else:
                            pe.matmul(bank[6 + i % 2][:, :], w_maa2g[:, ft * P:(ft + 1) * P], lora_g[:, :], start=True, stop=True).then_inc(s_xx, 1)

                def project(w, x, first, outs=FT, width=P, kt=FT):
                    for o in range(outs):
                        dst = slot(b, first + o)
                        for ft in range(kt):
                            last = pe.matmul(dst[0:width, :], w[:, ft, o * width:(o + 1) * width] if kt > 1 else w[:, o * width:(o + 1) * width],
                                             x[:, ft, :] if kt > 1 else x, start=(ft == 0), stop=(ft == kt - 1))
                        last.then_inc(s_pp, 1)

                mix_in(0)
                at = 2
                for f, name in enumerate(NAMES):
                    if f + 1 < 4:
                        mix_in(f + 1)
                    pe.wait_ge(s_mix, 1 + b * (5 * FT) + (f + 1) * FT)
                    x = mixed[1 - f % 2]
                    if name == "w":
                        project(w_td1, x, at, outs=1, width=64)
                        pe.wait_ge(s_pev, 1 + b * SLOTS + (at + 1))
                        project(w_td2, lora_w, at + 1, kt=1)
                        at += 5
                    else:
                        project(W[name], x, at)
                        at += 4
                    if f == 3:
                        mix_in(4)
                pe.wait_ge(s_pev, 1 + b * SLOTS + SLOTS)
                pe.wait_ge(s_pair, 1 + b * (5 * FT) + 5 * FT)
                pe.sem_inc(pass_by["pe"], 1)
                with pe.Fori(0, FT) as ft:
                    m = b * FT + ft

                    def per_ft(t):
                        return t[:, bass.ds(ft, 1), :].rearrange("p a t -> p (a t)")

                    pe.wait_ge(s_og, 1 + m)
                    for j in range(N + 1):
                        if j < N:
                            pe.wait_ge(s_a, 1 + m * N + max(j - 1, 0))
                            pe.matmul(bank[6 + j % 2][:, :], spread[:, j, :], per_ft(act_t["v"]), start=True, stop=True).then_inc(s_vb, 1)
                        if j >= 1:
                            pe.wait_ge(s_y, 1 + m * N + j)
                            pe.matmul(bank[5][:, :], gather[:, j - 1, :], y_j[(j - 1) % 2], start=(j == 1), stop=(j == N)).then_inc(s_yu, 1)
                    pe.wait_ge(s_ruk, m + 1)
                    pe.matmul(bank[4][:, :], heads[:, :], tmp[:, :], start=True, stop=True).then_inc(s_gp, 1)
                    pe.wait_ge(s_gd, m * 4 + 1)
                    pe.matmul(bank[4][:, :], heads[:, :], o_s[:, :], start=True, stop=True).then_inc(s_gp, 1)
                    pe.wait_ge(s_ga, m * 3 + 1)
                    pe.matmul(bank[4][:, :], heads[:, :], tmp[:, :], start=True, stop=True).then_inc(s_gp, 1)
                pe.wait_ge(s_og, 1 + b * FT + FT)
                for qt in range(QT):
                    for ft in range(FT):
                        last = pe.matmul(bank[qt][:, :], og[:, ft, qt * P:(qt + 1) * P], W["o"][:, ft, :], start=(ft == 0), stop=(ft == FT - 1))
                    last.then_inc(s_c, 1)
                turn_stream(b, 1)
                pe.wait_ge(s_sx, b * 4 + 3)
                for o in range(FT):
                    pe.wait_ge(s_kku, 1 + b * FT + max(o - 1, 0))
                    for ft in range(FT):
                        last = pe.matmul(bank[4 + o % 2][:, :], W["fk"][:, ft, o * P:(o + 1) * P], mixed[0][:, ft, :], start=(ft == 0), stop=(ft == FT - 1))
                    last.then_inc(s_kk, 1)
                pe.wait_ge(s_sx, b * 4 + 4)
                for qt in range(QT):
                    for ft in range(FT):
                        last = pe.matmul(bank[qt][:, :], mixed[1][:, ft, qt * P:(qt + 1) * P], W["fr"][:, ft, :], start=(ft == 0), stop=(ft == FT - 1))
                    last.then_inc(s_rr, 1)
                pe.wait_ge(s_kku, 1 + b * FT + FT)
                for qt in range(QT):
                    for ft in range(FT):
                        last = pe.matmul(bank[4 + qt][:, :], kk[:, ft, qt * P:(qt + 1) * P], W["fv"][:, ft, :], start=(ft == 0), stop=(ft == FT - 1))
                    last.then_inc(s_fv, 1)

        @block.scalar
        def _(act):
            for s in (s_pev, s_gate):
                act.sem_inc(s, 1)
            act.wait_ge(s_const, LOADS)
            with act.Fori(0, B) as b:
                def feature_major(which, w, bias):
                    for ft in range(FT):
                        act.wait_ge(s_tp, 1 + b * (2 * FT) + (which * FT + ft + 1))
                        act.activation(xa[:, ft, 1:T + 1], bank[ft][:, :], ACT.Identity, bias=column[bias](ft), scale=column[w](ft)).then_inc(s_xa, 1)
                    act.sem_inc(pass_by["act"], 1)
                    act.activation(xa[:, :, 0:1], before[:, bass.ds(b, 1), which, :].rearrange("p a (f c) -> p (a f) c", c=1), ACT.Copy).then_inc(s_xa, 1)

                feature_major(0, "ln1_w", "ln1_b")

                def evacuate(s, dst, src, func, **kw):
                    act.wait_ge(s_pp, 1 + b * SLOTS + (s + 1))
                    return act.activation(dst, src, func, **kw)

                evacuate(0, lora[:, :], bank[4][:, :], ACT.Tanh).then_inc(s_pev, 1)
                evacuate(1, lora_g[:, :], bank[5][0:32, :], ACT.Tanh).then_inc(s_pev, 1)
                at = 2
                for name in NAMES:
                    if name == "w":
                        evacuate(at, lora_w, bank[4 + at % 2][0:64, :], ACT.Tanh).then_inc(s_pev, 1)
                        at += 1
                    for ft in range(FT):
                        src, dst = bank[4 + at % 2][:, :], act_t[name][:, ft, :]
                        if name == "w":
                            evacuate(at, state[ft % 2][:, 0:T], src, ACT.Exp, bias=column["decay"](ft)).then_inc(s_dec, 1)
                            act.wait_ge(s_dec, b * FT + (ft + 1))
                            act.activation(dst, state[ft % 2][:, 0:T], ACT.Exp, scale=-1.0).then_inc(s_pev, 1)
                        elif name == "g":
                            evacuate(at, dst, src, ACT.Silu).then_inc(s_pev, 1)
                        else:
                            evacuate(at, dst, src, ACT.Copy).then_inc(s_pev, 1)
                        at += 1
                act.wait_ge(s_first, b * 16 + 16)
                act.sem_inc(pass_by["act"], 1)
                with act.Fori(0, FT) as ft:
                    m = b * FT + ft
                    for j in range(N):
                        act.wait_ge(s_y, 1 + m * N + max(j - 1, 0))
                        act.sem_inc(pass_by["act"], 1)
                        act.activation(state[j % 2][:, 0:1], s0[:, bass.ds(ft, 1), j:j + 1].rearrange("p a j -> p (a j)"), ACT.Copy).then_inc(s_s0, 1)
                    act.wait_ge(s_gd, m * 4 + 2)
                    act.activation(tmp[:, :], o_s[:, :], ACT.Square).then_inc(s_ga, 1)
                    act.wait_ge(s_gd, m * 4 + 3)
                    act.activation(tmp[:, :], tmp[:, :], ACT.Sqrt).then_inc(s_ga, 1)
                    act.wait_ge(s_gd, m * 4 + 4)
                    act.sem_inc(pass_by["act"], 1)
                    act.activation(tmp[:, :], o_s[:, :], ACT.Identity, bias=vec[:, bass.ds(ft + 4 * VEC3.index("gn_b"), 1)],
                                   scale=vec[:, bass.ds(ft + 4 * VEC3.index("gn_w"), 1)]).then_inc(s_ga, 1)
                act.wait_ge(s_mix, 1 + b * (5 * FT) + 5 * FT)
                feature_major(1, "ln2_w", "ln2_b")
                for o in range(FT):
                    act.wait_ge(s_kk, 1 + b * FT + (o + 1))
                    act.activation(kk[:, o, :], bank[4 + o % 2][:, :], ACT.Relu).then_inc(s_relu, 1)
                for qt in range(QT):
                    act.wait_ge(s_rr, 1 + b * QT + (qt + 1))
                    act.activation(gate[:, qt, :], bank[qt][:, :], ACT.Sigmoid).then_inc(s_gate, 1)

        @block.gpsimd
        def _(pool):
            for s in (s_mix, s_y):
                pool.sem_inc(s, 1)
            pool.memset(power[:, :, :], -0.5).then_inc(s_power, 1)
            pool.wait_ge(s_power, 1)
            with pool.Fori(0, B) as b:
                pool.wait_ge(s_var, b * 2 + 1)
                pool.tensor_tensor(rstd[:, :, :], rstd[:, :, :], power[:, :, :], ALU.pow).then_inc(s_rstd, 1)
                for f in range(5):
                    for ft in range(FT):
                        dst = mixed[1 - f % 2][:, ft, :]
                        pool.wait_ge(s_pair, 1 + b * (5 * FT) + (f * FT + ft + 1))
                        pool.tensor_tensor(dst, dst, xa[:, ft, 1:T + 1], ALU.add).then_inc(s_mix, 1)
                pool.wait_ge(s_pev, 1 + b * SLOTS + SLOTS)
                pool.sem_inc(pass_by["pool"], 1)
                with pool.Fori(0, FT) as ft:
                    m = b * FT + ft
                    for j in range(N):
                        pool.wait_ge(s_yu, 1 + m * N + max(j - 1, 0))
                        pool.wait_ge(s_s0, m * N + (j + 1))
                        pool.wait_ge(s_st, m * N + (j + 1))
                        pool.sem_inc(pass_by["pool"], 1)
                        pool.tensor_tensor(y_j[j % 2], act_t["r"][:, bass.ds(ft, 1), :].rearrange("p a t -> p (a t)"), state[j % 2][:, 0:T], ALU.mult).then_inc(s_y, 1)
                pool.wait_ge(s_var, b * 2 + 2)
                pool.tensor_tensor(rstd[:, :, :], rstd[:, :, :], power[:, :, :], ALU.pow).then_inc(s_rstd, 1)

        @block.vector
        def _(dve):
            for s in (s_pair, s_a, s_og, s_kku, s_end):
                dve.sem_inc(s, 1)
            dve.wait_ge(s_const, LOADS)
            with dve.Fori(0, B) as b:
                def stream(qt):
                    return x_res[:, bass.ds(b, 1), qt, :].rearrange("p a d -> p (a d)")

                def layer_norm(which):
                    k = b * 2 + which
                    for qt in range(QT):
                        dve.sem_inc(pass_by["dve"], 1)
                        dve.bn_stats(stats[:, qt, :], stream(qt)).then_inc(s_bn, 1)
                    for qt in range(QT):
                        dve.wait_ge(s_bn, k * QT + (qt + 1))
                        dve.sem_inc(pass_by["dve"], 1)
                        dve.bn_aggr(mv[:, qt, :], stats[:, qt, :]).then_inc(s_mv, 1)
                    dve.wait_ge(s_mv, k * QT + QT)
                    dve.tensor_scalar(rstd[:, :, 0:1], mv[:, :, 1:2], 1e-5, None, ALU.add).then_inc(s_var, 1)
                    dve.wait_ge(s_rstd, k + 1)
                    dve.wait_ge(s_tp, 1 + k * FT)
                    for qt in range(QT):
                        last = dve.tensor_scalar(xn[:, qt, :], stream(qt), mv[:, qt, 0:1], rstd[:, qt, 0:1], ALU.subtract, ALU.mult)
                    last.then_inc(s_xn, 1)

                def difference(which):
                    dve.wait_ge(s_xa, b * (2 * FT + 2) + (which + 1) * (FT + 1))
                    dve.tensor_tensor(sx[:, :, :], xa[:, :, 0:T], xa[:, :, 1:T + 1], ALU.subtract).then_inc(s_sx, 1)
                    dve.wait_ge(s_sx, b * 4 + (2 * which + 1 if which == 0 else 2))

                layer_norm(0)
                difference(0)
                for ft in range(FT):
                    dve.scalar_tensor_tensor(mixed[0][:, ft, :], sx[:, ft, :], column["maa_x"](ft), xa[:, ft, 1:T + 1], ALU.mult, ALU.add).then_inc(s_z, 1)
                for f, used in enumerate((0, 2, 6, 7, 15)):
                    dve.wait_ge(s_pp, 1 + b * SLOTS + used)
                    for ft in range(FT):
                        i = f * FT + ft
                        dve.wait_ge(s_xx, 1 + b * (5 * FT) + (i + 1))
                        dve.scalar_tensor_tensor(mixed[1 - f % 2][:, ft, :], bank[6 + i % 2][:, :], column["maa_" + NAMES[f]](ft), sx[:, ft, :], ALU.add, ALU.mult).then_inc(s_pair, 1)
                dve.wait_ge(s_pev, 1 + b * SLOTS + SLOTS)
                dve.wait_ge(s_first, b * 16 + 16)
                dve.sem_inc(pass_by["dve"], 1)
                with dve.Fori(0, FT) as ft:
                    m = b * FT + ft

                    def per_ft(name):
                        return act_t[name][:, bass.ds(ft, 1), :].rearrange("p a t -> p (a t)")

                    for j in range(N + 1):
                        if j < N:
                            dve.wait_ge(s_vb, 1 + m * N + (j + 1))
                            dve.tensor_tensor(a_j[j % 2], bank[6 + j % 2][:, :], per_ft("k"), ALU.mult).then_inc(s_a, 1)
                        if j >= 1:
                            i = j - 1
                            dve.wait_ge(s_a, 1 + m * N + (i + 1))
                            dve.wait_ge(s_y, 1 + m * N + max(i - 1, 0))
                            dve.tensor_tensor_scan(state[i % 2][:, 1:T + 1], per_ft("w"), a_j[i % 2],
                                                   s0[:, bass.ds(ft, 1), i:i + 1].rearrange("p a j -> p (a j)"), ALU.mult, ALU.add).then_inc(s_st, 1)
                    dve.scalar_tensor_tensor(tmp[:, :], per_ft("r"), vec[:, bass.ds(ft + 4 * VEC3.index("u"), 1)], per_ft("k"), ALU.mult, ALU.mult).then_inc(s_ruk, 1)
                    dve.wait_ge(s_gp, 1 + m * 3 + 1)
                    dve.tensor_tensor(o_s[:, :], bank[4][:, :], per_ft("v"), ALU.mult).then_inc(s_bonus, 1)
                    dve.wait_ge(s_yu, 1 + m * N + N)
                    dve.wait_ge(s_bonus, m + 1)
                    dve.tensor_tensor(o_s[:, :], bank[5][:, :], o_s[:, :], ALU.add).then_inc(s_gd, 1)
                    dve.wait_ge(s_gp, 1 + m * 3 + 2)
                    dve.scalar_tensor_tensor(o_s[:, :], bank[4][:, :], -1.0 / N, o_s[:, :], ALU.mult, ALU.add).then_inc(s_gd, 1)
                    dve.wait_ge(s_gp, 1 + m * 3 + 3)
                    dve.tensor_scalar(tmp[:, :], bank[4][:, :], 1.0 / N, 1e-5, ALU.mult, ALU.add).then_inc(s_veps, 1)
                    dve.wait_ge(s_veps, m + 1)
                    dve.reciprocal(tmp[:, :], tmp[:, :]).then_inc(s_gd, 1)
                    dve.wait_ge(s_ga, m * 3 + 2)
                    dve.tensor_tensor(o_s[:, :], o_s[:, :], tmp[:, :], ALU.mult).then_inc(s_gd, 1)
                    dve.wait_ge(s_ga, m * 3 + 3)
                    dve.tensor_tensor(og[:, bass.ds(ft, 1), :].rearrange("p a t -> p (a t)"), tmp[:, :], per_ft("g"), ALU.mult).then_inc(s_og, 1)
                for qt in range(QT):
                    dve.wait_ge(s_c, 1 + b * QT + (qt + 1))
                    dve.tensor_tensor(stream(qt), stream(qt), bank[qt][:, :], ALU.add).then_inc(s_xadd, 1)
                dve.wait_ge(s_xadd, b * QT + QT)
                layer_norm(1)
                difference(1)
                for which, name in enumerate(("ffn_k", "ffn_r")):
                    for ft in range(FT):
                        last = dve.scalar_tensor_tensor(mixed[which][:, ft, :], sx[:, ft, :], column[name](ft), xa[:, ft, 1:T + 1], ALU.mult, ALU.add)
                    last.then_inc(s_sx, 1)
                for o in range(FT):
                    dve.wait_ge(s_relu, b * FT + (o + 1))
                    dve.tensor_tensor(kk[:, o, :], kk[:, o, :], kk[:, o, :], ALU.mult).then_inc(s_kku, 1)
                for qt in range(QT):
                    dve.wait_ge(s_fv, 1 + b * QT + (qt + 1))
                    dve.wait_ge(s_gate, 1 + b * QT + (qt + 1))
                    dve.tensor_tensor(xn[:, qt, :], bank[4 + qt][:, :], gate[:, qt, :], ALU.mult).then_inc(s_half, 1)
                for qt in range(QT):
                    dve.wait_ge(s_half, b * QT + (qt + 1))
                    dve.tensor_tensor(stream(qt), stream(qt), xn[:, qt, :], ALU.add).then_inc(s_end, 1)
                dve.wait_ge(s_end, 1 + b * QT + QT)


def load_stream(nc, x, x_res):
    with nc.semaphore("x_loaded") as s_x, nc.Block() as block:
        @block.sync
        def _(sp):
            sp.dma_start(x_res[:, :, :, :], x.rearrange("b (q p) d -> p b q d", p=P)).then_inc(s_x, 16)
            sp.wait_ge(s_x, 16)


def store_stream(nc, out, x_res):
    with nc.semaphore("x_stored") as s_x, nc.Block() as block:
        @block.sync
        def _(sp):
            sp.dma_start(out.rearrange("b (q p) d -> p b q d", p=P), x_res[:, :, :, :]).then_inc(s_x, 16)
            sp.wait_ge(s_x, 16)


def network(nc, x, out, two, gqa, mix):
    with nc.sbuf_tensor("x_res", [P, B, QT, D], F32) as x_res:
        load_stream(nc, x, x_res)
        attention_block(nc, "mha", 2, 4, 32 ** -0.5, two, x_res, True)
        attention_block(nc, "gqa", 1, 8, 16 ** -0.5, gqa, x_res, False)
        time_mix_block(nc, mix, x_res)
        store_stream(nc, out, x_res)


def kernel(**inputs):
    import numpy as np
    import concourse.bacc as bacc
    from concourse.bass_utils import run_bass_kernel_spmd

    a = {k: np.ascontiguousarray(v) for k, v in inputs.items()}
    f32 = np.float32

    def tiles_in(w):
        return w.reshape(-1, P, w.shape[1]).transpose(1, 0, 2)

    def columns(w):
        return w.reshape(-1, P).T

    def spread_heads(w, repeat):
        heads = w.reshape(*w.shape[:-1], -1, 1, 16)
        out = np.zeros((*w.shape[:-1], heads.shape[-3], repeat, 32), f32)
        out[..., :16] = heads
        return out.reshape(*w.shape[:-1], -1)

    def qkv(wq, wk, wv):
        return np.stack([tiles_in(w).reshape(P, FT, -1, P).transpose(2, 0, 1, 3) for w in (wq, wk, wv)], axis=2)

    data = {"ident": np.eye(P, dtype=f32), "ones": np.ones((1, P), f32)}
    data["ctx_t"] = a["ctx_2048"].transpose(0, 2, 1).reshape(B, FT, P, S).transpose(0, 2, 1, 3)
    data["mask_u8"] = a["mask_BxS2_bf1"].view(np.uint8)
    data["x"] = a["x"]

    L = ["L0_xattn_", "L1_xattn_"]
    data["w_qkv"] = np.concatenate([qkv(a[l + "q_w"], a[l + "k_w"], a[l + "v_w"]) for l in L])
    data["w_out"] = np.stack([tiles_in(a[l + "cproj_w"]) for l in L])
    data["w_fc"] = np.concatenate([tiles_in(a[l + "fc_w"]).reshape(P, FT, F_TILES, P).transpose(2, 0, 1, 3) for l in L])
    data["w_pr"] = np.concatenate([a[l + "proj_w"].reshape(F_TILES, P, D) for l in L])
    data["vec"] = np.stack([np.concatenate([columns(a[l + k]) for k in ("q_b", "k_b", "v_b", "ln1_w", "ln1_b", "ln2_w", "ln2_b", "fc_b")], axis=1)
                            for l in L], axis=1)
    data["row"] = np.stack([np.stack([a[l + "cproj_b"], a[l + "proj_b"]]) for l in L])

    l = "L2_xattn_"
    data["w_qkv2"] = qkv(spread_heads(a[l + "Wq"], 1), spread_heads(a[l + "Wk"], 4), spread_heads(a[l + "Wv"], 4))
    data["w_out2"] = tiles_in(spread_heads(a[l + "Wo"].T, 1).T)[None]
    data["vec2"] = np.concatenate([columns(spread_heads(a[l + "bq"], 1)), columns(spread_heads(a[l + "bk"], 4)), columns(spread_heads(a[l + "bv"], 4))], axis=1)[:, None]
    data["row2"] = np.stack([a[l + "bo"], a[l + "bo"]])[None]
    data["gamma"] = a[l + "gamma"][None]
    data["beta"] = a[l + "beta"][None]
    data["mask2"] = a["mask_Bx1xSxS2_ff0"].reshape(B, QT, P, S).transpose(0, 2, 1, 3)

    l = "L3_xattn_"
    data["m_big"] = np.stack([tiles_in(a[l + k].T) for k in ("Wk", "Wv", "Wr", "Wg", "Wo", "Wfk", "Wfr", "Wfv")], axis=1)
    data["m_maa1"] = tiles_in(a[l + "maa_w1"])
    data["m_maa2"] = a[l + "maa_w2"][:4].reshape(P, D)
    data["m_maa2g"] = a[l + "maa_w2"][4]
    data["m_td1"] = tiles_in(a[l + "td_w1"])
    data["m_td2"] = a[l + "td_w2"]
    stack = a[l + "maa_stack"][0]
    vec3 = [a[l + "ln1_w"], a[l + "ln1_b"], a[l + "ln2_w"], a[l + "ln2_b"], a[l + "maa_x"], *stack, a[l + "time_decay"], a[l + "u"].reshape(-1),
            a[l + "gn_w"], a[l + "gn_b"], a[l + "ffn_maa_k"], a[l + "ffn_maa_r"]]
    data["m_vec"] = np.concatenate([columns(v) for v in vec3], axis=1)
    data["m_s0"] = a["ctx_2048"][:, 2:18].reshape(B, FT, P, 16).transpose(0, 2, 1, 3)
    data["m_before"] = a["ctx_2048"][:, [1, 0]].reshape(B, 2, FT, P).transpose(3, 0, 1, 2)
    head, inner = np.arange(P) // 16, np.arange(P) % 16
    same = head[:, None] == head[None, :]
    data["m_heads"] = same.astype(f32)
    data["m_spread"] = np.stack([(same & (inner[:, None] == j)) for j in range(16)], axis=1).astype(f32)
    data["m_gather"] = np.stack([(same & (inner[None, :] == j)) for j in range(16)], axis=1).astype(f32)

    nc = bacc.Bacc("TRN2", target_bir_lowering=False, num_devices=1)
    data = {k: np.ascontiguousarray(v) for k, v in data.items()}
    t = {k: nc.dram_tensor(f"in_{k}", v.shape, mybir.dt.from_np(v.dtype), kind="ExternalInput").ap() for k, v in data.items()}
    out = nc.dram_tensor("out_0", (B, T, D), F32, kind="ExternalOutput").ap()
    shared = {k: t[k] for k in ("ident", "ones", "ctx_t")}
    two = dict(shared, mask=t["mask_u8"], **{k: t[k] for k in ("w_qkv", "w_out", "w_fc", "w_pr", "vec", "row")})
    gqa = dict(shared, mask=t["mask2"], w_qkv=t["w_qkv2"], w_out=t["w_out2"], vec=t["vec2"], row=t["row2"], gamma=t["gamma"], beta=t["beta"])
    mix = {k[2:]: v for k, v in t.items() if k.startswith("m_")}
    mix["ident"] = t["ident"]
    network(nc, t["x"], out, two, gqa, mix)
    r = run_bass_kernel_spmd(nc, [{f"in_{k}": v for k, v in data.items()}], core_ids=[0])
    return r.results[0]["out_0"]
```

```python
from contextlib import ExitStack

import concourse.bass as bass
from concourse import mybir

F32 = mybir.dt.float32
F32R = mybir.dt.float32r
U8 = mybir.dt.uint8
ALU = mybir.AluOpType
ACT = mybir.ActivationFunctionType

P = 128
B = 4
T = 512
D = 512
S = 1024
FT = D // P
QT = T // P
KT = S // P
HPG = 4
HR = P // HPG
STRIP = 7 * HR
F_TILES = 4 * D // P
FF = 4
UNITS = HPG * QT
BIG = 1.0e30


def attention_block(nc, name, layers, groups, scale, dram, x_res, feed_forward):
    G = groups
    with ExitStack() as ctx:
        def sb(what, shape, dt=F32):
            return ctx.enter_context(nc.sbuf_tensor(f"{name}_{what}", shape, dt))

        def sem(what):
            return ctx.enter_context(nc.semaphore(f"{name}_{what}"))

        four = [ctx.enter_context(nc.psum_tensor(f"{name}_score{i}", [P, 512], F32)) for i in range(4)]
        half = [ctx.enter_context(nc.psum_tensor(f"{name}_half{i}", [P, 512], F32)) for i in range(2)]
        head_out = ctx.enter_context(nc.psum_tensor(f"{name}_head_out", [P, 512], F32))
        turn = ctx.enter_context(nc.psum_tensor(f"{name}_turn", [P, 512], F32))
        four = [t[:, :] for t in four]

        ident = sb("ident", [P, P])
        ones = sb("ones", [1, P])
        ctx_t = sb("ctx_t", [P, FT, S])
        xn = sb("xn", [P, QT, D])
        h_t = sb("h_t", [P, FT, T])
        if feed_forward:
            w_qkv = sb("w_qkv", [P, 3, FT, P])
        else:
            w_qkv = sb("w_q", [P, 1, FT, P])
            w_kv = sb("w_kv", [P, 2, FT, P])
            pick_raw = sb("pick_raw", [P, 2, P])
            pick = sb("pick", [P, 2, P], F32R)
            ka_hi = sb("ka_hi", [P, S], F32R)
            ka_lo = sb("ka_lo", [P, S], F32R)
            v_all = xn[:, 2:4, :].rearrange("p a (b m) -> p (a b) m", m=P)
        if feed_forward:
            w_out = sb("w_out", [P, G, D])
        vec = sb("vec", [P, layers, dram["vec"].shape[2]])
        row = sb("row", [1, 2 if feed_forward else 1, D])
        stack_raw = xn[:, 0:2, :].rearrange("p a b -> p (a b)")[:, 0:HPG * STRIP].rearrange("p (j c) -> p j c", j=HPG)
        stack_w = sb("stack_w", [P, HPG, STRIP], F32R)
        q_s = sb("q_s", [P, T]) if not feed_forward else xn[:, 2, :]
        q_hi = sb("q_hi", [P, T], F32R)
        q_lo = sb("q_lo", [P, T], F32R)
        q_st = sb("q_st", [P, HPG, T], F32R)
        k_st = sb("k_st", [P, HPG if feed_forward else 1, S], F32R)
        if feed_forward:
            k_hi = sb("k_hi", [P, S], F32R)
            k_lo = sb("k_lo", [P, S], F32R)

        def stacker(j, low, keys):
            at = HR * ((1 if low else 3) if keys else (2 if low else 0))
            return stack_w[:, j, at:at + P]

        out_u = xn[:, 0, :]
        out_n = xn[:, 1, :].rearrange("p (q m) -> p q m", q=QT)
        v = sb("v", [P, KT, P if feed_forward else HR])
        probs = sb("probs", [P, 2, HPG, S])
        probs_t = sb("probs_t", [P, 2, HPG, KT, P])
        low = sb("low", [P, UNITS])
        total = sb("total", [P, UNITS])
        rec = sb("rec", [P, UNITS])
        o_t = sb("o_t", [P, G, T])
        stats = sb("stats", [P, QT, 6])
        mv = sb("mv", [P, QT, 2])
        rstd = sb("rstd", [P, QT, 1])
        power = sb("power", [P, QT, 1])
        if feed_forward:
            mask_u8 = sb("mask_u8", [P, S], U8)
            mask = sb("mask", [P, 1, S])
            w_fc = [probs[:, 0, i, 0:D].rearrange("p (f m) -> p f m", m=P) for i in range(FF)]
            w_pr = [probs[:, 0, i, D:2 * D] for i in range(FF)]
            hid = [xn[:, 2 + i, :] for i in range(2)]
            QB, KB, VB, LW, LB, LW2, LB2, FB = 0, G, 2 * G, 3 * G, 3 * G + 4, 3 * G + 8, 3 * G + 12, 3 * G + 16
        else:
            mask = sb("mask", [P, QT, S])
            w_out = probs[:, 0, :, :].rearrange("p j (a d) -> p (j a) d", d=D)
            gamma = sb("gamma", [P, D])
            beta = sb("beta", [P, D])
            QB, KB, VB = 0, G, G + 1
        LN = 2 if feed_forward else 1
        NORMS = LN

        s_pass_pe, s_pass_act, s_pass_dve, s_pass_sp, s_pass_pool = (sem("pass_" + e) for e in ("pe", "act", "dve", "sp", "pool"))
        CONST = 16 * (4 if feed_forward else 7)
        if feed_forward:
            STACKS = [(True, j, 0) for j in range(HPG)] + [(False, j, 0) for j in range(HPG)]
            LATE = [(True, j, 1) for j in range(HPG)]
        else:
            STACKS = [(True, 0, 0), (True, 0, 1)] + [(False, j, 0) for j in range(HPG)]
            LATE = []
        NS = len(STACKS)
        TILES = 3 if feed_forward else 1
        PIECES = TILES + NS + (len(LATE) + 2 if feed_forward else 0)
        TAKES_DVE = 4 if feed_forward else 2
        TAKES_ACT = 3 if feed_forward else 2
        PIECES_DVE = TAKES_DVE + NS // 2
        EARLY_ACT = TAKES_ACT + NS // 2
        PIECES_ACT = EARLY_ACT + (len(LATE) + 2 if feed_forward else 0)
        s_const = sem("const_loaded")
        s_ctx = sem("ctx_loaded")
        s_wqkv = sem("wqkv_loaded")
        s_wout = sem("wout_loaded")
        s_row = sem("row_loaded")
        s_mask = sem("mask_loaded")
        s_mready = sem("mask_ready")
        s_xn = sem("xn_ready")
        s_tp = sem("h_turned")
        s_ht = sem("h_ready")
        s_pj = sem("projected")
        s_pjd = sem("q_v0_copied")
        s_pja = sem("k_v1_copied")
        s_all, s_alla, s_alld = sem("kv_projected"), sem("k_v1_all_copied"), sem("v0_all_copied")
        s_pad = sem("v_padded")
        s_pick = sem("pick_ready")
        s_sw = sem("stacker_ready")
        s_qk = sem("scores_ready")
        s_low = sem("scores_masked")
        s_exp = sem("probs_ready")
        s_tr = sem("probs_turned")
        s_ptd = sem("probs_t_first_half")
        s_pta = sem("probs_t_second_half")
        s_av = sem("head_summed")
        s_ou = sem("out_copied")
        s_n1 = sem("out_token_major")
        s_rec = sem("rec_ready")
        s_on = sem("out_normalised")
        s_n2 = sem("out_feature_major")
        s_ot = sem("o_t_ready")
        s_c = sem("attended")
        s_dve = sem("dve_chain")
        s_xadd = sem("x_updated")
        s_power = sem("power_set")
        s_var = sem("variance_ready")
        s_rstd = sem("rstd_ready")
        if feed_forward:
            s_wf = [sem(f"ff_weights_loaded{i}") for i in range(FF)]
            s_h1 = sem("hidden_ready")
            s_gl = sem("gelu_done")
            s_p2 = [sem(f"hidden_used{i}") for i in range(FF)]

        block = ctx.enter_context(nc.Block())

        @block.sync
        def _(sp):
            sp.dma_start(ident[:, :], dram["ident"]).then_inc(s_const, 16)
            sp.dma_start(ones[:, :], dram["ones"]).then_inc(s_const, 16)
            sp.dma_start(vec[:, :, :], dram["vec"]).then_inc(s_const, 16)
            sp.dma_start(stack_raw, dram["stack"]).then_inc(s_const, 16)
            if not feed_forward:
                sp.dma_start(gamma[:, :], dram["gamma"].to_broadcast((P, D))).then_inc(s_const, 16)
                sp.dma_start(beta[:, :], dram["beta"].to_broadcast((P, D))).then_inc(s_const, 16)
                sp.dma_start(w_kv[:, :, :, :], dram["w_kv"]).then_inc(s_const, 16)
            with sp.Fori(0, layers) as lay:
                with sp.Fori(0, B) as b:
                    n = lay * B + b
                    if feed_forward:
                        sp.wait_ge(s_pj, 1 + n * (PIECES * G))
                    else:
                        sp.wait_ge(s_all, 1 + n * 4)
                    sp.sem_inc(s_pass_sp, 1)
                    sp.dma_start(ctx_t[:, :, :], dram["ctx_t"][bass.ds(b, 1)].rearrange("a p f s -> (a p) f s")).then_inc(s_ctx, 16)
                    sp.wait_ge(s_low, 1 + n * (2 * UNITS * G))
                    sp.sem_inc(s_pass_sp, 1)
                    if feed_forward:
                        sp.dma_start(mask_u8[:, :], dram["mask"][bass.ds(b, 1), :].to_broadcast((P, S))).then_inc(s_mask, 16)
                    else:
                        sp.dma_start(mask[:, :, :], dram["mask"][bass.ds(b, 1)].rearrange("a p q s -> (a p) q s")).then_inc(s_mask, 16)
                    with sp.Fori(0, G) as g:
                        sp.wait_ge(s_pj, 1 + (n * G + g) * PIECES)
                        sp.sem_inc(s_pass_sp, 1)
                        if not feed_forward:
                            sp.dma_start(pick_raw[:, :, :], dram["pick"][bass.ds(g, 1)].rearrange("a p k m -> (a p) k m")).then_inc(s_wqkv, 16)
                        sp.dma_start(w_qkv[:, :, :, :], dram["w_qkv"][bass.ds(lay * G + g, 1)].rearrange("a p k f m -> (a p) k f m")).then_inc(s_wqkv, 16)
                    sp.wait_ge(s_xadd, 1 + n * (QT * LN))
                    sp.sem_inc(s_pass_sp, 1)
                    if not feed_forward:
                        sp.wait_ge(s_tr, (n + 1) * (G * 2 * UNITS) - 2 * HPG)
                        sp.sem_inc(s_pass_sp, 1)
                    sp.dma_start(w_out[:, :, :], dram["w_out"][bass.ds(lay, 1)].rearrange("a p f m -> (a p) f m")).then_inc(s_wout, 16)
                    sp.dma_start(row[:, :, :], dram["row"][bass.ds(lay, 1)]).then_inc(s_row, 16)
                    if feed_forward:
                        sp.wait_ge(s_tr, (n + 1) * (G * 2 * UNITS) - 2 * HPG)
                        sp.sem_inc(s_pass_sp, 1)
                        with sp.Fori(0, F_TILES // FF) as ff:
                            for i in range(FF):
                                sp.wait_ge(s_p2[i], 1 + n * (F_TILES // FF) + ff)
                                sp.sem_inc(s_pass_sp, 1)
                                sp.dma_start(w_fc[i], dram["w_fc"][bass.ds(lay * F_TILES + ff * FF + i, 1)].rearrange("a p f m -> (a p) f m")).then_inc(s_wf[i], 16)
                                sp.dma_start(w_pr[i], dram["w_pr"][bass.ds(lay * F_TILES + ff * FF + i, 1)].rearrange("a p m -> (a p) m")).then_inc(s_wf[i], 16)

        @block.tensor
        def _(pe):
            for s in (s_pj, s_tp, s_all, s_av) + ((*s_p2,) if feed_forward else ()):
                pe.sem_inc(s, 1)
            pe.wait_ge(s_const, CONST)
            pe.wait_ge(s_sw, 1)

            def turn_stream(n, which):
                pe.wait_ge(s_xn, n * LN + which + 1)
                for ft in range(FT):
                    for qt in range(QT):
                        last = pe.transpose(four[ft][:, qt * P:(qt + 1) * P], xn[:, qt, ft * P:(ft + 1) * P], ident[:, :])
                    last.then_inc(s_tp, 1)

            with pe.Fori(0, layers) as lay:
                with pe.Fori(0, B) as b:
                    n = lay * B + b
                    pe.wait_ge(s_xadd, 1 + n * (QT * LN))
                    turn_stream(n, 0)
                    pe.wait_ge(s_ht, n * (FT * LN) + FT)
                    pe.wait_ge(s_ctx, n * 16 + 16)

                    def values(w, half_of_keys, dst):
                        for c in range(4):
                            kt = 4 * half_of_keys + c
                            for ft in range(FT):
                                last = pe.matmul(dst[:, c * P:(c + 1) * P], ctx_t[:, ft, kt * P:(kt + 1) * P], w[:, ft, :], start=(ft == 0), stop=(ft == FT - 1))
                        return last

                    if not feed_forward:
                        for s in range(2):
                            for ft in range(FT):
                                last = pe.matmul(four[s], w_kv[:, 0, ft, :], ctx_t[:, ft, 512 * s:512 * s + 512], start=(ft == 0), stop=(ft == FT - 1))
                            last.then_inc(s_all, 1)
                        for s in range(2):
                            values(w_kv[:, 1, :, :], s, four[2 + s]).then_inc(s_all, 1)
                        pe.wait_ge(s_alla, n * 3 + 3)
                        pe.wait_ge(s_alld, n * 3 + 3)

                    def project(m, piece):
                        if piece == ("k0" if feed_forward else "q"):
                            pe.wait_ge(s_wqkv, (m + 1) * (16 if feed_forward else 32))
                            pe.wait_ge(s_low, 1 + m * (2 * UNITS))
                        if piece in ("k0", "k1"):
                            i = int(piece[1])
                            for ft in range(FT):
                                last = pe.matmul(four[i], w_qkv[:, 1, ft, :], ctx_t[:, ft, 512 * i:512 * i + 512], start=(ft == 0), stop=(ft == FT - 1))
                        elif piece == "q":
                            for ft in range(FT):
                                last = pe.matmul(four[2], w_qkv[:, 0, ft, :], h_t[:, ft, :], start=(ft == 0), stop=(ft == FT - 1))
                        last.then_inc(s_pj, 1)

                    def stack(m, r):
                        keys, j, i = STACKS[r]
                        if r >= 4:
                            pe.wait_ge((s_pja, s_pjd)[r % 2], m * (PIECES_ACT, PIECES_DVE)[r % 2] + ((TAKES_ACT, TAKES_DVE)[r % 2] + (r - 4) // 2 + 1))
                        elif feed_forward:
                            pe.wait_ge(s_pjd, m * PIECES_DVE + max(r, 1))
                        elif r == 0:
                            pe.wait_ge(s_pick, m + 1)
                        elif r == 3:
                            pe.wait_ge(s_pjd, m * PIECES_DVE + 1)
                        if keys:
                            hi, lo = (k_hi, k_lo) if feed_forward else (ka_hi, ka_lo)
                            hi, lo = hi[:, 512 * i:512 * i + 512], lo[:, 512 * i:512 * i + 512]
                        else:
                            pe.wait_ge(s_pjd, m * PIECES_DVE + (4 if feed_forward else 2))
                            hi, lo = q_hi[:, :], q_lo[:, :]
                        if keys and not feed_forward:
                            w_hi, w_lo = pick[:, 0, :], pick[:, 1, :]
                        else:
                            w_hi, w_lo = stacker(j, False, keys), stacker(j, True, keys)
                        pe.matmul(four[(r + 3) % 4], w_hi, hi, start=True, stop=False)
                        pe.matmul(four[(r + 3) % 4], w_lo, lo, start=False, stop=True).then_inc(s_pj, 1)

                    def late_stack(m, r):
                        _, j, i = LATE[r]
                        if r >= 2:
                            pe.wait_ge(s_pja, m * PIECES_ACT + (EARLY_ACT + r - 1))
                        pe.matmul(half[r % 2][:, :], stacker(j, False, True), k_hi[:, 512 * i:512 * i + 512], start=True, stop=False)
                        pe.matmul(half[r % 2][:, :], stacker(j, True, True), k_lo[:, 512 * i:512 * i + 512], start=False, stop=True).then_inc(s_pj, 1)

                    def late_values(m, s):
                        pe.wait_ge(s_pja, m * PIECES_ACT + (EARLY_ACT + len(LATE) - 1 + s))
                        values(w_qkv[:, 2, :, :], s, half[s]).then_inc(s_pj, 1)

                    def attend(m, then):
                        pe.wait_ge(s_pjd, (m + 1) * PIECES_DVE)
                        pe.wait_ge(s_pja, m * PIECES_ACT + EARLY_ACT)

                        def scores(t, j):
                            qt, s = divmod(t, 2)
                            if t:
                                pe.wait_ge(s_low, 1 + m * (2 * UNITS) + (HPG * (t - 1) + j + 1))
                            pe.matmul(four[j], q_st[:, j, qt * P:(qt + 1) * P], k_st[:, j if feed_forward else 0, 512 * s:512 * s + 512],
                                      start=True, stop=True).then_inc(s_qk, 1)

                        def turn_probs(qt, j):
                            u = HPG * qt + j
                            pe.wait_ge(s_exp, 1 + m * UNITS + (u + 1))
                            for s in range(2):
                                pe.wait_ge((s_ptd, s_pta)[s], 1 + m * UNITS + u)
                                for c in range(4):
                                    last = pe.transpose(half[s][:, c * P:(c + 1) * P], probs[:, qt % 2, j, (4 * s + c) * P:(4 * s + c + 1) * P], ident[:, :])
                                last.then_inc(s_tr, 1)

                        def weigh(qt, part):
                            if part == 0:
                                pe.wait_ge(s_ptd, 1 + m * UNITS + HPG * (qt + 1))
                                pe.wait_ge(s_pta, 1 + m * UNITS + HPG * (qt + 1))
                                if qt == 0:
                                    pe.wait_ge(s_ou, 1 + m)
                            for kt in (2 * part, 2 * part + 1):
                                for j in range(HPG):
                                    last = pe.matmul(head_out[HR * j:HR * j + HR, qt * P:(qt + 1) * P],
                                                     v[:, kt, HR * j:HR * j + HR] if feed_forward else v[:, kt, :],
                                                     probs_t[:, qt % 2, j, kt, :], start=(kt == 0), stop=(kt == KT - 1))
                            if part == 3:
                                last.then_inc(s_av, 1)

                        def out_token_major():
                            pe.wait_ge(s_ou, 1 + m + 1)
                            for qt in range(QT):
                                last = pe.transpose(turn[:, qt * P:(qt + 1) * P], out_u[:, qt * P:(qt + 1) * P], ident[:, :])
                            last.then_inc(s_n1, 1)

                        def out_feature_major():
                            pe.wait_ge(s_on, m + 1)
                            for qt in range(QT):
                                last = pe.transpose(turn[:, qt * P:(qt + 1) * P], out_n[:, qt, :], ident[:, :])
                            last.then_inc(s_n2, 1)

                        for t in range(2 * QT):
                            qt, s = divmod(t, 2)
                            if feed_forward and t == 1:
                                pe.wait_ge(s_pja, m * PIECES_ACT + (EARLY_ACT + len(LATE)))
                            for k in range(2):
                                scores(t, 2 * k)
                                scores(t, 2 * k + 1)
                                if feed_forward and t == 0:
                                    late_stack(m, 2 * k)
                                    late_stack(m, 2 * k + 1)
                                if feed_forward and t == 1:
                                    late_values(m, k)
                                if qt >= 2:
                                    weigh(qt - 2, 2 * s + k)
                                if qt >= 1:
                                    if feed_forward and qt == 1 and s == 0 and k == 0:
                                        pe.wait_ge(s_pja, (m + 1) * PIECES_ACT)
                                    turn_probs(qt - 1, 2 * s + k)
                        pieces = () if not then else ("k0", "k1", "q") if feed_forward else ("q",)
                        turn_probs(QT - 1, 0)
                        for piece in pieces[0:1]:
                            project(m + 1, piece)
                        for j in range(1, HPG):
                            weigh(QT - 2, j - 1)
                            turn_probs(QT - 1, j)
                        weigh(QT - 2, 3)
                        for piece in pieces[1:]:
                            project(m + 1, piece)
                        for part in range(4):
                            weigh(QT - 1, part)
                        if then:
                            stack(m + 1, 0)
                            stack(m + 1, 1)
                        out_token_major()
                        for r in range(2, NS - 2) if then else ():
                            stack(m + 1, r)
                        out_feature_major()
                        for r in range(NS - 2, NS) if then else ():
                            stack(m + 1, r)

                    for piece in ("k0", "k1", "q") if feed_forward else ("q",):
                        project(n * G, piece)
                    for r in range(NS):
                        stack(n * G, r)
                    with pe.Fori(0, G - 1) as g:
                        attend(n * G + g, True)
                    attend(n * G + (G - 1), False)
                    pe.wait_ge(s_ot, 1 + n * G + G)
                    pe.wait_ge(s_wout, n * 16 + 16)
                    pe.wait_ge(s_row, n * 16 + 16)
                    pe.wait_ge(s_low, 1 + (n + 1) * (G * 2 * UNITS))
                    for qt in range(QT):
                        pe.matmul(four[qt], ones[:, :], row[:, 0, :], start=True, stop=False)
                        for g in range(G):
                            last = pe.matmul(four[qt], o_t[:, g, qt * P:(qt + 1) * P], w_out[:, g, :], start=False, stop=(g == G - 1))
                        last.then_inc(s_c, 1)
                    if feed_forward:
                        turn_stream(n, 1)
                        pe.wait_ge(s_ht, n * (FT * LN) + 2 * FT)
                        for qt in range(QT):
                            pe.matmul(four[qt], ones[:, :], row[:, 1, :], start=True, stop=False, skip_group_check=True)
                        pe.sem_inc(s_pass_pe, 1)
                        with pe.Fori(0, F_TILES // FF) as ff:
                            k = n * (F_TILES // FF) + ff

                            def hidden(i):
                                pe.wait_ge(s_wf[i], k * 32 + 32)
                                pe.wait_ge(s_gl, 1 + k * FF + max(i - 1, 0))
                                for ft in range(FT):
                                    last = pe.matmul(half[i % 2][:, :], w_fc[i][:, ft, :], h_t[:, ft, :], start=(ft == 0), stop=(ft == FT - 1))
                                last.then_inc(s_h1, 1)

                            def back(i):
                                pe.wait_ge(s_gl, 1 + k * FF + (i + 1))
                                for qt in range(QT):
                                    last = pe.matmul(four[qt], hid[i % 2][:, qt * P:(qt + 1) * P], w_pr[i], start=False, stop=False, skip_group_check=True)
                                last.then_inc(s_p2[i], 1)

                            hidden(0)
                            for i in range(1, FF):
                                hidden(i)
                                back(i - 1)
                            back(FF - 1)

        @block.gpsimd
        def _(pool):
            pool.memset(power[:, :, :], -0.5).then_inc(s_power, 1)
            pool.wait_ge(s_power, 1)
            if not feed_forward:
                with pool.Fori(0, B) as b:
                    with pool.Fori(0, G) as g:
                        m = b * G + g
                        pool.wait_ge(s_wqkv, (m + 1) * 32)
                        pool.wait_ge(s_pj, 1 + m * PIECES)
                        pool.sem_inc(s_pass_pool, 1)
                        pool.tensor_copy(pick[:, :, :], pick_raw[:, :, :]).then_inc(s_pick, 1)
                    pool.wait_ge(s_var, b + 1)
                    pool.tensor_tensor(rstd[:, :, :], rstd[:, :, :], power[:, :, :], ALU.pow).then_inc(s_rstd, 1)
                return
            with pool.Fori(0, layers * B * NORMS) as k:
                pool.wait_ge(s_var, k + 1)
                pool.tensor_tensor(rstd[:, :, :], rstd[:, :, :], power[:, :, :], ALU.pow).then_inc(s_rstd, 1)

        @block.scalar
        def _(act):
            for s in (s_ot, s_pta, s_ou, s_exp) + ((s_gl,) if feed_forward else ()):
                act.sem_inc(s, 1)
            act.wait_ge(s_const, CONST)

            act.copy(stack_w[:, :, :], stack_raw).then_inc(s_sw, 1)
            if not feed_forward:
                act.wait_ge(s_pad, 1)

            def feature_major(n, lay, which):
                for ft in range(FT):
                    act.wait_ge(s_tp, 1 + n * (FT * LN) + (which * FT + ft + 1))
                    if feed_forward:
                        lw, lb = ((LW, LB), (LW2, LB2))[which]
                        act.activation(h_t[:, ft, :], four[ft], ACT.Identity, bias=vec[:, bass.ds(lay, 1), lb + ft:lb + ft + 1].rearrange("p a b -> p (a b)"),
                                       scale=vec[:, bass.ds(lay, 1), lw + ft:lw + ft + 1].rearrange("p a b -> p (a b)")).then_inc(s_ht, 1)
                    else:
                        act.copy(h_t[:, ft, :], four[ft]).then_inc(s_ht, 1)

            def column(lay, c):
                return vec[:, bass.ds(lay, 1), bass.ds(c, 1)].rearrange("p a b -> p (a b)")

            with act.Fori(0, layers) as lay:
                with act.Fori(0, B) as b:
                    n = lay * B + b
                    feature_major(n, lay, 0)
                    if not feed_forward:
                        for s in range(2):
                            act.wait_ge(s_all, 1 + n * 4 + (s + 1))
                            act.activation(ka_hi[:, 512 * s:512 * s + 512], four[s], ACT.Identity, bias=vec[:, 0, KB:KB + 1]).then_inc(s_alla, 1)
                        act.wait_ge(s_all, 1 + n * 4 + 4)
                        act.copy(v_all[:, 4:8, :].rearrange("p a b -> p (a b)"), four[3]).then_inc(s_alla, 1)
                        act.wait_ge(s_alla, n * 3 + 3)
                        act.wait_ge(s_alld, n * 3 + 3)

                    def take_keys(m, g, i):
                        act.wait_ge(s_pj, 1 + m * PIECES + (i + 1))
                        act.sem_inc(s_pass_act, 1)
                        act.activation(k_hi[:, 512 * i:512 * i + 512], four[i], ACT.Identity, bias=column(lay, g + KB)).then_inc(s_pja, 1)

                    def take_query(m):
                        act.wait_ge(s_pjd, m * PIECES_DVE + (3 if feed_forward else 1))
                        act.copy(q_hi[:, :], q_s[:, :] if not feed_forward else q_s).then_inc(s_pja, 1)

                    def take_values(m, g):
                        if not feed_forward:
                            act.wait_ge(s_av, 1 + m * QT)
                            act.sem_inc(s_pass_act, 1)
                            act.copy(v[:, :, 0:16], v_all[:, :, bass.ds(g * 16, 16)]).then_inc(s_pja, 1)

                    def take_late(m):
                        for r, (_, j, i) in enumerate(LATE):
                            act.wait_ge(s_pj, 1 + m * PIECES + (TILES + NS + r + 1))
                            act.copy(k_st[:, j, 512 * i:512 * i + 512], half[r % 2][:, :]).then_inc(s_pja, 1)
                        for s in range(2):
                            act.wait_ge(s_pj, 1 + m * PIECES + (TILES + NS + len(LATE) + s + 1))
                            act.copy(v[:, 4 * s:4 * s + 4, :].rearrange("p a b -> p (a b)"), half[s][:, :]).then_inc(s_pja, 1)

                    def take_stack(m, r):
                        keys, j, i = STACKS[r]
                        act.wait_ge(s_pj, 1 + m * PIECES + (TILES + r + 1))
                        act.copy(k_st[:, j, 512 * i:512 * i + 512] if keys else q_st[:, j, :], four[(r + 3) % 4]).then_inc(s_pja, 1)

                    def attend(m, g, then):
                        def exponentials(qt, j):
                            u = HPG * qt + j
                            act.wait_ge(s_low, 1 + m * (2 * UNITS) + (2 * HPG * qt + HPG + j + 1))
                            act.activation(probs[:, qt % 2, j, :], probs[:, qt % 2, j, :], ACT.Exp, bias=low[:, u:u + 1], scale=-1.0,
                                           accum_out=total[:, u:u + 1]).then_inc(s_exp, 1)

                        def take_turned(qt, j):
                            act.wait_ge(s_tr, m * (2 * UNITS) + 2 * (HPG * qt + j) + 2)
                            if qt >= 2:
                                act.wait_ge(s_av, 1 + m * QT + (qt - 1))
                            act.copy(probs_t[:, qt % 2, j, 4:8, :].rearrange("p a b -> p (a b)"), half[1][:, :]).then_inc(s_pta, 1)

                        if feed_forward:
                            take_late(m)
                        for qt in range(QT + 1):
                            if qt >= 1:
                                exponentials(qt - 1, 2)
                                take_turned(qt - 1, 0)
                                if qt == QT and then and feed_forward:
                                    take_keys(m + 1, g + 1, 0)
                                exponentials(qt - 1, 3)
                                take_turned(qt - 1, 1)
                                take_turned(qt - 1, 2)
                            if qt < QT:
                                exponentials(qt, 0)
                            if qt >= 1:
                                take_turned(qt - 1, 3)
                            if qt < QT:
                                exponentials(qt, 1)
                        if then:
                            if feed_forward:
                                take_keys(m + 1, g + 1, 1)
                            take_query(m + 1)
                        act.wait_ge(s_av, 1 + m * QT + QT)
                        act.copy(out_u, head_out[:, :]).then_inc(s_ou, 1)
                        if then:
                            take_values(m + 1, g + 1)
                            for r in range(0, NS - 2, 2):
                                take_stack(m + 1, r)
                        act.wait_ge(s_n2, m + 1)
                        act.sem_inc(s_pass_act, 1)
                        act.activation(o_t[:, bass.ds(g, 1), :].rearrange("p a b -> p (a b)"), turn[:, :], ACT.Identity,
                                       bias=column(lay, g + VB)).then_inc(s_ot, 1)
                        if then:
                            take_stack(m + 1, NS - 2)

                    if feed_forward:
                        take_keys(n * G, 0, 0)
                        take_keys(n * G, 0, 1)
                    take_query(n * G)
                    take_values(n * G, 0)
                    for r in range(0, NS, 2):
                        take_stack(n * G, r)
                    with act.Fori(0, G - 1) as g:
                        attend(n * G + g, g, True)
                    attend(n * G + (G - 1), G - 1, False)
                    if feed_forward:
                        feature_major(n, lay, 1)
                        with act.Fori(0, F_TILES // FF) as ff:
                            k = n * (F_TILES // FF) + ff
                            for i in range(FF):
                                act.wait_ge(s_h1, k * FF + (i + 1))
                                act.wait_ge(s_p2[(i + 2) % FF], 1 + k + (i >= 2))
                                act.sem_inc(s_pass_act, 1)
                                act.activation(hid[i % 2], half[i % 2][:, :], ACT.Gelu_apprx_tanh, bias=column(lay, ff * FF + (FB + i))).then_inc(s_gl, 1)

        @block.vector
        def _(dve):
            for s in (s_low, s_xadd, s_ptd):
                dve.sem_inc(s, 1)
            dve.wait_ge(s_const, CONST)
            dve.wait_ge(s_sw, 1)

            CH = 2 * QT
            if not feed_forward:
                dve.memset(v[:, :, :], 0.0).then_inc(s_pad, 1)
            with dve.Fori(0, layers) as lay:
                with dve.Fori(0, B) as b:
                    n = lay * B + b
                    chain = n * (CH * LN + (0 if feed_forward else 3 * QT))
                    if feed_forward:
                        for qt in range(QT):
                            dve.sem_inc(s_pass_dve, 1)
                            dve.bn_stats(stats[:, qt, :], x_res[:, bass.ds(b, 1), qt, :].rearrange("p a d -> p (a d)")).then_inc(s_dve, 1)
                        for qt in range(QT):
                            dve.wait_ge(s_dve, chain + (qt + 1))
                            dve.sem_inc(s_pass_dve, 1)
                            dve.bn_aggr(mv[:, qt, :], stats[:, qt, :]).then_inc(s_dve, 1)
                        dve.wait_ge(s_dve, chain + 2 * QT)
                        dve.tensor_scalar(rstd[:, :, 0:1], mv[:, :, 1:2], 1e-5, None, ALU.add).then_inc(s_var, 1)
                        dve.wait_ge(s_rstd, n * NORMS + 1)
                        dve.wait_ge(s_tp, 1 + n * (FT * LN))
                        for qt in range(QT):
                            last = dve.tensor_scalar(xn[:, qt, :], x_res[:, bass.ds(b, 1), qt, :].rearrange("p a d -> p (a d)"), mv[:, qt, 0:1], rstd[:, qt, 0:1],
                                                     ALU.subtract, ALU.mult)
                        last.then_inc(s_xn, 1)
                        dve.wait_ge(s_mask, n * 16 + 16)
                        dve.tensor_scalar(mask[:, 0, :], mask_u8[:, :], -BIG, BIG, ALU.mult, ALU.add).then_inc(s_mready, 1)
                    else:
                        dve.wait_ge(s_tp, 1 + n * (FT * LN))
                        dve.tensor_copy(xn[:, :, :], x_res[:, bass.ds(b, 1), :, :].rearrange("p a q d -> p (a q) d")).then_inc(s_xn, 1)
                        dve.wait_ge(s_mask, n * 16 + 16)
                        dve.tensor_scalar(mask[:, :, :], mask[:, :, :], -1.0, None, ALU.mult).then_inc(s_mready, 1)
                    dve.wait_ge(s_mready, n + 1)
                    dve.sem_inc(s_pass_dve, 1)
                    if not feed_forward:
                        for s in range(2):
                            dve.wait_ge(s_alla, n * 3 + (s + 1))
                            dve.scalar_tensor_tensor(ka_lo[:, 512 * s:512 * s + 512], four[s], vec[:, 0, KB:KB + 1], ka_hi[:, 512 * s:512 * s + 512],
                                                     ALU.add, ALU.subtract).then_inc(s_alld, 1)
                        dve.wait_ge(s_all, 1 + n * 4 + 3)
                        dve.tensor_copy(v_all[:, 0:4, :].rearrange("p a b -> p (a b)"), four[2]).then_inc(s_alld, 1)

                    def take_keys(m, g, i):
                        dve.wait_ge(s_pja, m * PIECES_ACT + (i + 1))
                        dve.sem_inc(s_pass_dve, 1)
                        dve.scalar_tensor_tensor(k_lo[:, 512 * i:512 * i + 512], four[i], vec[:, bass.ds(lay, 1), bass.ds(g + KB, 1)].rearrange("p a b -> p (a b)"),
                                                 k_hi[:, 512 * i:512 * i + 512], ALU.add, ALU.subtract).then_inc(s_pjd, 1)

                    def take_query(m, g):
                        dve.wait_ge(s_pj, 1 + m * PIECES + (3 if feed_forward else 1))
                        dve.tensor_scalar(q_s[:, :] if not feed_forward else q_s, four[2], vec[:, bass.ds(lay, 1), bass.ds(g + QB, 1)].rearrange("p a b -> p (a b)"),
                                          -scale, ALU.add, ALU.mult).then_inc(s_pjd, 1)
                        dve.wait_ge(s_pja, m * PIECES_ACT + (3 if feed_forward else 1))
                        dve.tensor_tensor(q_lo[:, :], q_s[:, :] if not feed_forward else q_s, q_hi[:, :], ALU.subtract).then_inc(s_pjd, 1)

                    def take_stack(m, r):
                        keys, j, i = STACKS[r]
                        dve.wait_ge(s_pj, 1 + m * PIECES + (TILES + r + 1))
                        dve.tensor_copy(k_st[:, j, 512 * i:512 * i + 512] if keys else q_st[:, j, :], four[(r + 3) % 4]).then_inc(s_pjd, 1)

                    def attend(m, g, then):
                        def mask_scores(t, j):
                            qt, s = divmod(t, 2)
                            u = HPG * qt + j
                            dve.wait_ge(s_qk, m * (2 * UNITS) + (HPG * t + j + 1))
                            if s == 0 and qt >= 2:
                                dve.wait_ge(s_tr, m * (2 * UNITS) + 2 * (HPG * (qt - 2) + j) + 2)
                            if s == 1:
                                dve.wait_ge(s_low, 1 + m * (2 * UNITS) + (HPG * (t - 1) + j + 1))
                            dve.sem_inc(s_pass_dve, 1)
                            dve.tensor_tensor_reduce(out=probs[:, qt % 2, j, 512 * s:512 * s + 512], in0=four[j],
                                                     in1=mask[:, 0 if feed_forward else qt, 512 * s:512 * s + 512], scale=1.0,
                                                     scalar=3.0e38 if s == 0 else low[:, u:u + 1], op0=ALU.add, op1=ALU.min,
                                                     accum_out=low[:, u:u + 1]).then_inc(s_low, 1)

                        def take_turned(qt, j):
                            dve.wait_ge(s_tr, m * (2 * UNITS) + 2 * (HPG * qt + j) + 1)
                            if qt >= 2:
                                dve.wait_ge(s_av, 1 + m * QT + (qt - 1))
                            dve.tensor_copy(probs_t[:, qt % 2, j, 0:4, :].rearrange("p a b -> p (a b)"), half[0][:, :]).then_inc(s_ptd, 1)

                        for t in range(2 * QT):
                            qt, s = divmod(t, 2)
                            for k in range(2):
                                mask_scores(t, 2 * k)
                                mask_scores(t, 2 * k + 1)
                                if qt >= 1:
                                    take_turned(qt - 1, 2 * s + k)
                        take_turned(QT - 1, 0)
                        take_turned(QT - 1, 1)
                        if then and feed_forward:
                            take_keys(m + 1, g + 1, 0)
                        take_turned(QT - 1, 2)
                        take_turned(QT - 1, 3)
                        if then:
                            if feed_forward:
                                take_keys(m + 1, g + 1, 1)
                            take_query(m + 1, g + 1)
                            take_stack(m + 1, 1)
                        dve.wait_ge(s_exp, 1 + m * UNITS + UNITS)
                        dve.reciprocal(rec[:, :], total[:, :]).then_inc(s_rec, 1)
                        dve.wait_ge(s_rec, m + 1)
                        dve.wait_ge(s_n1, m + 1)
                        dve.tensor_tensor(out_n.rearrange("p q (j d) -> p q j d", j=HPG), turn[:, :].rearrange("p (q j d) -> p q j d", q=QT, j=HPG),
                                          rec[:, :].rearrange("p (q j a) -> p q j a", j=HPG, a=1).to_broadcast((P, QT, HPG, HR)), ALU.mult).then_inc(s_on, 1)
                        for r in range(3, NS, 2) if then else ():
                            take_stack(m + 1, r)

                    if feed_forward:
                        take_keys(n * G, 0, 0)
                        take_keys(n * G, 0, 1)
                    take_query(n * G, 0)
                    for r in range(1, NS, 2):
                        take_stack(n * G, r)
                    dve.sem_inc(s_pass_dve, 1)
                    with dve.Fori(0, G - 1) as g:
                        attend(n * G + g, g, True)
                    attend(n * G + (G - 1), G - 1, False)
                    for qt in range(QT):
                        xs = x_res[:, bass.ds(b, 1), qt, :].rearrange("p a d -> p (a d)")
                        dve.wait_ge(s_c, n * QT + (qt + 1))
                        dve.tensor_tensor(xs, xs, four[qt], ALU.add).then_inc(s_xadd, 1)
                    dve.wait_ge(s_xadd, 1 + n * (QT * LN) + QT)
                    chain2 = chain + (CH if feed_forward else 0)
                    for qt in range(QT):
                        dve.sem_inc(s_pass_dve, 1)
                        dve.bn_stats(stats[:, qt, :], x_res[:, bass.ds(b, 1), qt, :].rearrange("p a d -> p (a d)")).then_inc(s_dve, 1)
                    for qt in range(QT):
                        dve.wait_ge(s_dve, chain2 + (qt + 1))
                        dve.sem_inc(s_pass_dve, 1)
                        dve.bn_aggr(mv[:, qt, :], stats[:, qt, :]).then_inc(s_dve, 1)
                    dve.wait_ge(s_dve, chain2 + 2 * QT)
                    dve.tensor_scalar(rstd[:, :, 0:1], mv[:, :, 1:2], 1e-5 if feed_forward else 1e-6, None, ALU.add).then_inc(s_var, 1)
                    dve.wait_ge(s_rstd, n * NORMS + NORMS)
                    if feed_forward:
                        for qt in range(QT):
                            last = dve.tensor_scalar(xn[:, qt, :], x_res[:, bass.ds(b, 1), qt, :].rearrange("p a d -> p (a d)"), mv[:, qt, 0:1], rstd[:, qt, 0:1],
                                                     ALU.subtract, ALU.mult)
                        last.then_inc(s_xn, 1)
                        dve.wait_ge(s_p2[FF - 1], 1 + n * (F_TILES // FF) + F_TILES // FF)
                        for qt in range(QT):
                            xs = x_res[:, bass.ds(b, 1), qt, :].rearrange("p a d -> p (a d)")
                            dve.tensor_tensor(xs, xs, four[qt], ALU.add).then_inc(s_xadd, 1)
                        dve.wait_ge(s_xadd, 1 + n * (QT * LN) + QT * LN)
                    else:
                        for step in range(3):
                            for qt in range(QT):
                                xs = x_res[:, bass.ds(b, 1), qt, :].rearrange("p a d -> p (a d)")
                                if step:
                                    dve.wait_ge(s_dve, chain2 + (CH + (step - 1) * QT + qt + 1))
                                if step == 0:
                                    dve.tensor_scalar(xs, xs, mv[:, qt, 0:1], rstd[:, qt, 0:1], ALU.subtract, ALU.mult).then_inc(s_dve, 1)
                                elif step == 1:
                                    dve.tensor_tensor(xs, xs, gamma[:, :], ALU.mult).then_inc(s_dve, 1)
                                else:
                                    dve.tensor_tensor(xs, xs, beta[:, :], ALU.add).then_inc(s_dve, 1)
                        dve.wait_ge(s_dve, chain2 + (CH + 3 * QT))

VEC3 = ("ln1_w", "ln1_b", "ln2_w", "ln2_b", "maa_x", "maa_k", "maa_w", "maa_v", "maa_r", "maa_g", "decay", "u", "gn_w", "gn_b", "ffn_k", "ffn_r")


def time_mix_block(nc, dram, x_res):
    NAMES = ("k", "w", "v", "r", "g")
    SLOTS = 23
    N = 16
    NB = 4
    LAG = 3
    with ExitStack() as ctx:
        def sb(what, shape, dt=F32):
            return ctx.enter_context(nc.sbuf_tensor(f"mix_{what}", shape, dt))

        def sem(what):
            return ctx.enter_context(nc.semaphore(f"mix_{what}"))

        bank = [ctx.enter_context(nc.psum_tensor(f"mix_bank{i}", [P, 512], F32)) for i in range(8)]
        ident = sb("ident", [P, P])
        spread = sb("spread", [P, N, P])
        gather = sb("gather", [P, N, P])
        heads = sb("heads", [P, P])
        w_maa1 = sb("w_maa1", [P, FT, 5 * 32])
        w_maa2 = sb("w_maa2", [P, D])
        w_maa2g = sb("w_maa2g", [32, D])
        w_td1 = sb("w_td1", [P, FT, 64])
        w_td2 = sb("w_td2", [64, D])
        w_big = sb("w_big", [P, 8, FT, D])
        W = {name: w_big[:, i, :, :] for i, name in enumerate(("k", "v", "r", "g", "o", "fk", "fr", "fv"))}
        vec = sb("vec", [P, dram["vec"].shape[1]])
        column = {name: (lambda i: (lambda ft: vec[:, 4 * i + ft:4 * i + ft + 1]))(i) for i, name in enumerate(VEC3)}
        xn = sb("xn", [P, QT, D])
        xa = sb("xa", [P, FT, T + 1])
        sx = xn
        mixed = [sb(f"mixed{i}", [P, FT, T]) for i in range(2)]
        lora = sb("lora", [P, T])
        tmp = sb("tmp", [P, T])
        lora_g = sb("lora_g", [32, T])
        lora_w = tmp[0:64, :]
        act_t = {name: sb(f"{name}_t", [P, FT, T]) for name in NAMES}
        s0 = sb("s0", [P, FT, N])
        before = sb("before", [P, B, 2, FT])
        decay_in = [sb(f"decay_in{i}", [P, T + 1]) for i in range(2)]
        a_j = [mixed[1][:, i, :] for i in range(NB)]
        state = [decay_in[0][:, :], decay_in[1][:, :], xa[:, 0, :], xa[:, 1, :]]
        y_j = [xn[:, i, :] for i in range(NB)]
        spread_bank = [bank[i][:, :] for i in (6, 7, 0, 1)]
        bonus = lora
        stats = sb("stats", [P, QT, 6])
        mv = sb("mv", [P, QT, 2])
        rstd = sb("rstd", [P, QT, 1])
        power = sb("power", [P, QT, 1])
        og = mixed[0]
        kk = act_t["r"]
        gate = act_t["k"]

        LOADS = 12 * 16
        s_const = sem("const_loaded")
        s_first = sem("first_loaded")
        s_xn, s_tp, s_xa, s_sx, s_z = (sem(x) for x in ("xn_ready", "turned", "xa_ready", "sx_ready", "z_ready"))
        s_pp, s_pev = sem("projected"), sem("projection_copied")
        s_xx = sem("mix_ready")
        s_mix = sem("mixed_ready")
        s_vb, s_a = sem("v_spread"), sem("a_ready")
        s_s0, s_st, s_y, s_yu = sem("state_first"), sem("state_ready"), sem("y_ready"), sem("y_used")
        s_ruk, s_gp, s_gd, s_ga = sem("ruk_ready"), sem("heads_summed"), sem("norm_dve"), sem("norm_act")
        s_og, s_dec, s_pair, s_bonus, s_veps, s_half = (sem(x) for x in ("og_ready", "decay_exp", "mix_product", "bonus_ready", "norm_eps", "gate_product"))
        s_c, s_xadd = sem("mixed_out"), sem("x_updated")
        s_kk, s_kku, s_rr, s_gate, s_fv, s_end = (sem(x) for x in ("kk_psum", "kk_ready", "rr_psum", "gate_ready", "fv_psum", "x_final"))
        s_power, s_var, s_rstd, s_bn, s_mv = (sem(x) for x in ("power_set", "variance_ready", "rstd_ready", "bn_stats", "bn_aggr"))
        s_relu = sem("relu_ready")
        s_recip, s_pow, s_o = sem("norm_reciprocal"), sem("norm_rstd"), sem("o_summed")
        s_hm = sem("head_mean")
        pass_by = {e: sem("pass_" + e) for e in ("pe", "act", "dve", "pool", "sp")}
        block = ctx.enter_context(nc.Block())

        @block.sync
        def _(sp):
            for dst, name in ((ident[:, :], "ident"), (spread[:, :, :], "spread"), (gather[:, :, :], "gather"), (heads[:, :], "heads"),
                              (w_maa1[:, :, :], "maa1"), (w_maa2[:, :], "maa2"), (w_maa2g[:, :], "maa2g"), (w_td1[:, :, :], "td1"),
                              (w_td2[:, :], "td2"), (vec[:, :], "vec"), (before[:, :, :, :], "before")):
                sp.dma_start(dst, dram[name]).then_inc(s_const, 16)
            sp.dma_start(w_big[:, :, :, :], dram["big"]).then_inc(s_const, 16)
            with sp.Fori(0, B) as b:
                sp.wait_ge(s_end, 1 + b * QT)
                sp.sem_inc(pass_by["sp"], 1)
                sp.dma_start(s0[:, :, :], dram["s0"][bass.ds(b, 1)].rearrange("a p f j -> (a p) f j")).then_inc(s_first, 16)

        @block.tensor
        def _(pe):
            for s in (s_pp, s_xx, s_vb, s_yu, s_gp, s_c, s_kk, s_rr, s_fv, s_tp):
                pe.sem_inc(s, 1)
            pe.wait_ge(s_const, LOADS)

            def turn_stream(b, which):
                pe.wait_ge(s_xn, b * 2 + (which + 1))
                for ft in range(FT):
                    for qt in range(QT):
                        last = pe.transpose(bank[ft][:, qt * P:(qt + 1) * P], xn[:, qt, ft * P:(ft + 1) * P], ident[:, :])
                    last.then_inc(s_tp, 1)

            def slot(b, s):
                pe.wait_ge(s_pev, 1 + b * SLOTS + (s - 1 if s >= 2 else 0))
                return bank[4 + s % 2]

            with pe.Fori(0, B) as b:
                pe.wait_ge(s_end, 1 + b * QT)
                turn_stream(b, 0)
                pe.wait_ge(s_z, b * FT + FT)
                for s, (lo, hi) in enumerate(((0, 128), (128, 160))):
                    dst = slot(b, s)
                    for ft in range(FT):
                        last = pe.matmul(dst[0:hi - lo, :], w_maa1[:, ft, lo:hi], mixed[0][:, ft, :], start=(ft == 0), stop=(ft == FT - 1))
                    last.then_inc(s_pp, 1)

                def mix_in(f):
                    pe.wait_ge(s_pev, 1 + b * SLOTS + 2)
                    for ft in range(FT):
                        i = f * FT + ft
                        pe.wait_ge(s_pair, 1 + b * (5 * FT) + max(i - 1, 0))
                        if f < 4:
                            pe.matmul(bank[6 + i % 2][:, :], w_maa2[32 * f:32 * f + 32, ft * P:(ft + 1) * P], lora[32 * f:32 * f + 32, :], start=True, stop=True).then_inc(s_xx, 1)
                        else:
                            pe.matmul(bank[6 + i % 2][:, :], w_maa2g[:, ft * P:(ft + 1) * P], lora_g[:, :], start=True, stop=True).then_inc(s_xx, 1)

                def project(w, x, first, outs=FT, width=P, kt=FT):
                    for o in range(outs):
                        dst = slot(b, first + o)
                        for ft in range(kt):
                            last = pe.matmul(dst[0:width, :], w[:, ft, o * width:(o + 1) * width] if kt > 1 else w[:, o * width:(o + 1) * width],
                                             x[:, ft, :] if kt > 1 else x, start=(ft == 0), stop=(ft == kt - 1))
                        last.then_inc(s_pp, 1)

                mix_in(0)
                at = 2
                for f, name in enumerate(NAMES):
                    if f + 1 < 4:
                        mix_in(f + 1)
                    pe.wait_ge(s_mix, 1 + b * (5 * FT) + (f + 1) * FT)
                    x = mixed[1 - f % 2]
                    if name == "w":
                        project(w_td1, x, at, outs=1, width=64)
                        pe.wait_ge(s_pev, 1 + b * SLOTS + (at + 1))
                        project(w_td2, lora_w, at + 1, kt=1)
                        at += 5
                    else:
                        project(W[name], x, at)
                        at += 4
                    if f == 3:
                        mix_in(4)
                pe.wait_ge(s_pev, 1 + b * SLOTS + SLOTS)
                pe.wait_ge(s_pair, 1 + b * (5 * FT) + 5 * FT)
                pe.sem_inc(pass_by["pe"], 1)
                with pe.Fori(0, FT) as ft:
                    m = b * FT + ft

                    def per_ft(t):
                        return t[:, bass.ds(ft, 1), :].rearrange("p a t -> p (a t)")

                    pe.wait_ge(s_o, 1 + m)
                    for step in range(N + LAG):
                        if step < N:
                            pe.wait_ge(s_a, 1 + m * N + max(step + 1 - NB, 0))
                            pe.matmul(spread_bank[step % NB], spread[:, step, :], per_ft(act_t["v"]), start=True, stop=True).then_inc(s_vb, 1)
                        if step == 2:
                            pe.wait_ge(s_ruk, m + 1)
                            pe.matmul(bank[4][:, :], heads[:, :], tmp[:, :], start=True, stop=True).then_inc(s_gp, 1)
                        j = step - LAG
                        if j >= 0:
                            pe.wait_ge(s_y, 1 + m * N + (j + 1))
                            pe.matmul(bank[5][:, :], gather[:, j, :], y_j[j % NB], start=(j == 0), stop=(j == N - 1)).then_inc(s_yu, 1)
                pe.wait_ge(s_o, 1 + b * FT + FT)
                for ft in range(FT):
                    pe.matmul(bank[ft][:, :], heads[:, :], og[:, ft, :], start=True, stop=True).then_inc(s_hm, 1)
                for ft in range(FT):
                    pe.wait_ge(s_ga, b * (2 * FT) + (ft + 1))
                    pe.matmul(bank[4 + ft][:, :], heads[:, :], xn[:, ft, :], start=True, stop=True).then_inc(s_hm, 1)
                pe.wait_ge(s_og, 1 + b * FT + FT)
                for qt in range(QT):
                    for ft in range(FT):
                        last = pe.matmul(bank[qt][:, :], og[:, ft, qt * P:(qt + 1) * P], W["o"][:, ft, :], start=(ft == 0), stop=(ft == FT - 1))
                    last.then_inc(s_c, 1)
                turn_stream(b, 1)
                pe.wait_ge(s_sx, b * 4 + 3)
                for o in range(FT):
                    pe.wait_ge(s_kku, 1 + b * FT + max(o - 1, 0))
                    for ft in range(FT):
                        last = pe.matmul(bank[4 + o % 2][:, :], W["fk"][:, ft, o * P:(o + 1) * P], mixed[0][:, ft, :], start=(ft == 0), stop=(ft == FT - 1))
                    last.then_inc(s_kk, 1)
                pe.wait_ge(s_sx, b * 4 + 4)
                for qt in range(QT):
                    for ft in range(FT):
                        last = pe.matmul(bank[qt][:, :], mixed[1][:, ft, qt * P:(qt + 1) * P], W["fr"][:, ft, :], start=(ft == 0), stop=(ft == FT - 1))
                    last.then_inc(s_rr, 1)
                pe.wait_ge(s_kku, 1 + b * FT + FT)
                for qt in range(QT):
                    for ft in range(FT):
                        last = pe.matmul(bank[4 + qt][:, :], kk[:, ft, qt * P:(qt + 1) * P], W["fv"][:, ft, :], start=(ft == 0), stop=(ft == FT - 1))
                    last.then_inc(s_fv, 1)

        @block.scalar
        def _(act):
            for s in (s_pev, s_gate):
                act.sem_inc(s, 1)
            act.wait_ge(s_const, LOADS)
            with act.Fori(0, B) as b:
                def feature_major(which, w, bias):
                    for ft in range(FT):
                        act.wait_ge(s_tp, 1 + b * (2 * FT) + (which * FT + ft + 1))
                        act.activation(xa[:, ft, 1:T + 1], bank[ft][:, :], ACT.Identity, bias=column[bias](ft), scale=column[w](ft)).then_inc(s_xa, 1)
                    act.sem_inc(pass_by["act"], 1)
                    act.activation(xa[:, :, 0:1], before[:, bass.ds(b, 1), which, :].rearrange("p a (f c) -> p (a f) c", c=1), ACT.Copy).then_inc(s_xa, 1)

                feature_major(0, "ln1_w", "ln1_b")

                def evacuate(s, dst, src, func, **kw):
                    act.wait_ge(s_pp, 1 + b * SLOTS + (s + 1))
                    return act.activation(dst, src, func, **kw)

                evacuate(0, lora[:, :], bank[4][:, :], ACT.Tanh).then_inc(s_pev, 1)
                evacuate(1, lora_g[:, :], bank[5][0:32, :], ACT.Tanh).then_inc(s_pev, 1)
                at = 2
                for name in NAMES:
                    if name == "w":
                        evacuate(at, lora_w, bank[4 + at % 2][0:64, :], ACT.Tanh).then_inc(s_pev, 1)
                        at += 1
                    for ft in range(FT):
                        src, dst = bank[4 + at % 2][:, :], act_t[name][:, ft, :]
                        if name == "w":
                            evacuate(at, decay_in[ft % 2][:, 0:T], src, ACT.Exp, bias=column["decay"](ft)).then_inc(s_dec, 1)
                            act.wait_ge(s_dec, b * FT + (ft + 1))
                            act.activation(dst, decay_in[ft % 2][:, 0:T], ACT.Exp, scale=-1.0).then_inc(s_pev, 1)
                        elif name == "g":
                            evacuate(at, dst, src, ACT.Silu).then_inc(s_pev, 1)
                        else:
                            evacuate(at, dst, src, ACT.Copy).then_inc(s_pev, 1)
                        at += 1
                act.wait_ge(s_first, b * 16 + 16)
                act.sem_inc(pass_by["act"], 1)
                with act.Fori(0, FT) as ft:
                    m = b * FT + ft
                    for j in range(N):
                        act.wait_ge(s_y, 1 + m * N + max(j + 1 - NB, 0))
                        act.sem_inc(pass_by["act"], 1)
                        act.activation(state[j % NB][:, 0:1], s0[:, bass.ds(ft, 1), j:j + 1].rearrange("p a j -> p (a j)"), ACT.Copy).then_inc(s_s0, 1)
                for ft in range(FT):
                    act.wait_ge(s_gd, b * (2 * FT) + (ft + 1))
                    act.activation(xn[:, ft, :], og[:, ft, :], ACT.Square).then_inc(s_ga, 1)
                for ft in range(FT):
                    act.wait_ge(s_recip, b * FT + (ft + 1))
                    act.activation(xn[:, ft, :], xn[:, ft, :], ACT.Sqrt).then_inc(s_pow, 1)
                for ft in range(FT):
                    act.wait_ge(s_gd, b * (2 * FT) + (FT + ft + 1))
                    act.activation(xn[:, ft, :], og[:, ft, :], ACT.Identity, bias=column["gn_b"](ft), scale=column["gn_w"](ft)).then_inc(s_ga, 1)
                act.wait_ge(s_mix, 1 + b * (5 * FT) + 5 * FT)
                feature_major(1, "ln2_w", "ln2_b")
                for o in range(FT):
                    act.wait_ge(s_kk, 1 + b * FT + (o + 1))
                    act.activation(kk[:, o, :], bank[4 + o % 2][:, :], ACT.Relu).then_inc(s_relu, 1)
                for qt in range(QT):
                    act.wait_ge(s_rr, 1 + b * QT + (qt + 1))
                    act.activation(gate[:, qt, :], bank[qt][:, :], ACT.Sigmoid).then_inc(s_gate, 1)

        @block.gpsimd
        def _(pool):
            for s in (s_mix, s_y):
                pool.sem_inc(s, 1)
            pool.memset(power[:, :, :], -0.5).then_inc(s_power, 1)
            pool.wait_ge(s_power, 1)
            with pool.Fori(0, B) as b:
                pool.wait_ge(s_var, b * 2 + 1)
                pool.tensor_tensor(rstd[:, :, :], rstd[:, :, :], power[:, :, :], ALU.pow).then_inc(s_rstd, 1)
                for f in range(5):
                    for ft in range(FT):
                        dst = mixed[1 - f % 2][:, ft, :]
                        pool.wait_ge(s_pair, 1 + b * (5 * FT) + (f * FT + ft + 1))
                        pool.tensor_tensor(dst, dst, xa[:, ft, 1:T + 1], ALU.add).then_inc(s_mix, 1)
                pool.wait_ge(s_pev, 1 + b * SLOTS + SLOTS)
                pool.sem_inc(pass_by["pool"], 1)
                with pool.Fori(0, FT) as ft:
                    m = b * FT + ft
                    for j in range(N):
                        pool.wait_ge(s_yu, 1 + m * N + max(j + 1 - NB, 0))
                        pool.wait_ge(s_s0, m * N + (j + 1))
                        pool.wait_ge(s_st, m * N + (j + 1))
                        pool.sem_inc(pass_by["pool"], 1)
                        pool.tensor_tensor(y_j[j % NB], act_t["r"][:, bass.ds(ft, 1), :].rearrange("p a t -> p (a t)"), state[j % NB][:, 0:T], ALU.mult).then_inc(s_y, 1)
                pool.wait_ge(s_var, b * 2 + 2)
                pool.tensor_tensor(rstd[:, :, :], rstd[:, :, :], power[:, :, :], ALU.pow).then_inc(s_rstd, 1)

        @block.vector
        def _(dve):
            for s in (s_pair, s_a, s_og, s_kku, s_end, s_o):
                dve.sem_inc(s, 1)
            dve.wait_ge(s_const, LOADS)
            with dve.Fori(0, B) as b:
                def stream(qt):
                    return x_res[:, bass.ds(b, 1), qt, :].rearrange("p a d -> p (a d)")

                def layer_norm(which):
                    k = b * 2 + which
                    for qt in range(QT):
                        dve.sem_inc(pass_by["dve"], 1)
                        dve.bn_stats(stats[:, qt, :], stream(qt)).then_inc(s_bn, 1)
                    for qt in range(QT):
                        dve.wait_ge(s_bn, k * QT + (qt + 1))
                        dve.sem_inc(pass_by["dve"], 1)
                        dve.bn_aggr(mv[:, qt, :], stats[:, qt, :]).then_inc(s_mv, 1)
                    dve.wait_ge(s_mv, k * QT + QT)
                    dve.tensor_scalar(rstd[:, :, 0:1], mv[:, :, 1:2], 1e-5, None, ALU.add).then_inc(s_var, 1)
                    dve.wait_ge(s_rstd, k + 1)
                    dve.wait_ge(s_tp, 1 + k * FT)
                    for qt in range(QT):
                        last = dve.tensor_scalar(xn[:, qt, :], stream(qt), mv[:, qt, 0:1], rstd[:, qt, 0:1], ALU.subtract, ALU.mult)
                    last.then_inc(s_xn, 1)

                def difference(which):
                    dve.wait_ge(s_xa, b * (2 * FT + 2) + (which + 1) * (FT + 1))
                    dve.tensor_tensor(sx[:, :, :], xa[:, :, 0:T], xa[:, :, 1:T + 1], ALU.subtract).then_inc(s_sx, 1)
                    dve.wait_ge(s_sx, b * 4 + (2 * which + 1 if which == 0 else 2))

                layer_norm(0)
                difference(0)
                for ft in range(FT):
                    dve.scalar_tensor_tensor(mixed[0][:, ft, :], sx[:, ft, :], column["maa_x"](ft), xa[:, ft, 1:T + 1], ALU.mult, ALU.add).then_inc(s_z, 1)
                for f, used in enumerate((0, 2, 6, 7, 15)):
                    dve.wait_ge(s_pp, 1 + b * SLOTS + used)
                    for ft in range(FT):
                        i = f * FT + ft
                        dve.wait_ge(s_xx, 1 + b * (5 * FT) + (i + 1))
                        dve.scalar_tensor_tensor(mixed[1 - f % 2][:, ft, :], bank[6 + i % 2][:, :], column["maa_" + NAMES[f]](ft), sx[:, ft, :], ALU.add, ALU.mult).then_inc(s_pair, 1)
                dve.wait_ge(s_pev, 1 + b * SLOTS + SLOTS)
                dve.wait_ge(s_first, b * 16 + 16)
                dve.sem_inc(pass_by["dve"], 1)
                with dve.Fori(0, FT) as ft:
                    m = b * FT + ft

                    def per_ft(name):
                        return act_t[name][:, bass.ds(ft, 1), :].rearrange("p a t -> p (a t)")

                    dve.scalar_tensor_tensor(tmp[:, :], per_ft("r"), vec[:, bass.ds(ft + 4 * VEC3.index("u"), 1)], per_ft("k"), ALU.mult, ALU.mult).then_inc(s_ruk, 1)
                    for j in range(N + 1):
                        if j < N:
                            dve.wait_ge(s_vb, 1 + m * N + (j + 1))
                            dve.tensor_tensor(a_j[j % NB], spread_bank[j % NB], per_ft("k"), ALU.mult).then_inc(s_a, 1)
                        if j >= 1:
                            i = j - 1
                            dve.wait_ge(s_a, 1 + m * N + (i + 1))
                            dve.wait_ge(s_y, 1 + m * N + max(i + 1 - NB, 0))
                            dve.tensor_tensor_scan(state[i % NB][:, 1:T + 1], per_ft("w"), a_j[i % NB],
                                                   s0[:, bass.ds(ft, 1), i:i + 1].rearrange("p a j -> p (a j)"), ALU.mult, ALU.add).then_inc(s_st, 1)
                        if j == 4:
                            dve.wait_ge(s_gp, 1 + m + 1)
                            dve.tensor_tensor(bonus[:, :], bank[4][:, :], per_ft("v"), ALU.mult).then_inc(s_bonus, 1)
                    dve.wait_ge(s_yu, 1 + m * N + N)
                    dve.wait_ge(s_bonus, m + 1)
                    dve.tensor_tensor(og[:, bass.ds(ft, 1), :].rearrange("p a t -> p (a t)"), bank[5][:, :], bonus[:, :], ALU.add).then_inc(s_o, 1)
                for ft in range(FT):
                    dve.wait_ge(s_hm, b * (2 * FT) + (ft + 1))
                    dve.scalar_tensor_tensor(og[:, ft, :], bank[ft][:, :], -1.0 / N, og[:, ft, :], ALU.mult, ALU.add).then_inc(s_gd, 1)
                for ft in range(FT):
                    dve.wait_ge(s_hm, b * (2 * FT) + (FT + ft + 1))
                    dve.tensor_scalar(xn[:, ft, :], bank[4 + ft][:, :], 1.0 / N, 1e-5, ALU.mult, ALU.add).then_inc(s_veps, 1)
                    dve.wait_ge(s_veps, b * FT + (ft + 1))
                    dve.reciprocal(xn[:, ft, :], xn[:, ft, :]).then_inc(s_recip, 1)
                for ft in range(FT):
                    dve.wait_ge(s_pow, b * FT + (ft + 1))
                    dve.tensor_tensor(og[:, ft, :], og[:, ft, :], xn[:, ft, :], ALU.mult).then_inc(s_gd, 1)
                for ft in range(FT):
                    dve.wait_ge(s_ga, b * (2 * FT) + (FT + ft + 1))
                    dve.tensor_tensor(og[:, ft, :], xn[:, ft, :], act_t["g"][:, ft, :], ALU.mult).then_inc(s_og, 1)
                for qt in range(QT):
                    dve.wait_ge(s_c, 1 + b * QT + (qt + 1))
                    dve.tensor_tensor(stream(qt), stream(qt), bank[qt][:, :], ALU.add).then_inc(s_xadd, 1)
                dve.wait_ge(s_xadd, b * QT + QT)
                layer_norm(1)
                difference(1)
                for which, name in enumerate(("ffn_k", "ffn_r")):
                    for ft in range(FT):
                        last = dve.scalar_tensor_tensor(mixed[which][:, ft, :], sx[:, ft, :], column[name](ft), xa[:, ft, 1:T + 1], ALU.mult, ALU.add)
                    last.then_inc(s_sx, 1)
                for o in range(FT):
                    dve.wait_ge(s_relu, b * FT + (o + 1))
                    dve.tensor_tensor(kk[:, o, :], kk[:, o, :], kk[:, o, :], ALU.mult).then_inc(s_kku, 1)
                for qt in range(QT):
                    dve.wait_ge(s_fv, 1 + b * QT + (qt + 1))
                    dve.wait_ge(s_gate, 1 + b * QT + (qt + 1))
                    dve.tensor_tensor(xn[:, qt, :], bank[4 + qt][:, :], gate[:, qt, :], ALU.mult).then_inc(s_half, 1)
                for qt in range(QT):
                    dve.wait_ge(s_half, b * QT + (qt + 1))
                    dve.tensor_tensor(stream(qt), stream(qt), xn[:, qt, :], ALU.add).then_inc(s_end, 1)
                dve.wait_ge(s_end, 1 + b * QT + QT)


def load_stream(nc, x, x_res):
    with nc.semaphore("x_loaded") as s_x, nc.Block() as block:
        @block.sync
        def _(sp):
            sp.dma_start(x_res[:, :, :, :], x.rearrange("b (q p) d -> p b q d", p=P)).then_inc(s_x, 16)
            sp.wait_ge(s_x, 16)


def store_stream(nc, out, x_res):
    with nc.semaphore("x_stored") as s_x, nc.Block() as block:
        @block.sync
        def _(sp):
            sp.dma_start(out.rearrange("b (q p) d -> p b q d", p=P), x_res[:, :, :, :]).then_inc(s_x, 16)
            sp.wait_ge(s_x, 16)


def network(nc, x, out, two, gqa, mix):
    with nc.sbuf_tensor("x_res", [P, B, QT, D], F32) as x_res:
        load_stream(nc, x, x_res)
        attention_block(nc, "mha", 2, 4, 32 ** -0.5, two, x_res, True)
        attention_block(nc, "gqa", 1, 8, 16 ** -0.5, gqa, x_res, False)
        time_mix_block(nc, mix, x_res)
        store_stream(nc, out, x_res)


def kernel(**inputs):
    import numpy as np
    import concourse.bacc as bacc
    from concourse.bass_utils import run_bass_kernel_spmd

    a = {k: np.ascontiguousarray(v) for k, v in inputs.items()}
    f32 = np.float32

    def tiles_in(w):
        return w.reshape(-1, P, w.shape[1]).transpose(1, 0, 2)

    def columns(w):
        return w.reshape(-1, P).T

    def spread_heads(w, repeat):
        heads = w.reshape(*w.shape[:-1], -1, 1, 16)
        out = np.zeros((*w.shape[:-1], heads.shape[-3], repeat, 32), f32)
        out[..., :16] = heads
        return out.reshape(*w.shape[:-1], -1)

    def qkv(wq, wk, wv):
        return np.stack([tiles_in(w).reshape(P, FT, -1, P).transpose(2, 0, 1, 3) for w in (wq, wk, wv)], axis=2)

    stacker = np.zeros((P, HPG, 7, HR), f32)
    for j in range(HPG):
        for block in (0, 3, 4):
            stacker[HR * j:HR * j + HR, j, block] = np.eye(HR)
    stacker = stacker.reshape(P, HPG, STRIP)
    data = {"ident": np.eye(P, dtype=f32), "stack": stacker, "ones": np.ones((1, P), f32)}
    data["ctx_t"] = a["ctx_2048"].transpose(0, 2, 1).reshape(B, FT, P, S).transpose(0, 2, 1, 3)
    data["mask_u8"] = a["mask_BxS2_bf1"].view(np.uint8)
    data["x"] = a["x"]

    L = ["L0_xattn_", "L1_xattn_"]
    data["w_qkv"] = np.concatenate([qkv(a[l + "q_w"], a[l + "k_w"], a[l + "v_w"]) for l in L])
    data["w_out"] = np.stack([tiles_in(a[l + "cproj_w"]) for l in L])
    data["w_fc"] = np.concatenate([tiles_in(a[l + "fc_w"]).reshape(P, FT, F_TILES, P).transpose(2, 0, 1, 3) for l in L])
    data["w_pr"] = np.concatenate([a[l + "proj_w"].reshape(F_TILES, P, D) for l in L])
    data["vec"] = np.stack([np.concatenate([columns(a[l + k]) for k in ("q_b", "k_b", "v_b", "ln1_w", "ln1_b", "ln2_w", "ln2_b", "fc_b")], axis=1)
                            for l in L], axis=1)
    data["row"] = np.stack([np.stack([a[l + "cproj_b"], a[l + "proj_b"]]) for l in L])

    l = "L2_xattn_"
    data["w_q2"] = tiles_in(spread_heads(a[l + "Wq"], 1)).reshape(P, FT, 8, P).transpose(2, 0, 1, 3)[:, :, None]
    data["w_kv2"] = np.stack([tiles_in(a[l + "Wk"]), tiles_in(a[l + "Wv"])], axis=1)
    to = np.arange(P)
    take = np.stack([(np.arange(P)[:, None] == 16 * g + to % 32) & (to % 32 < 16) for g in range(8)])
    data["pick2"] = np.stack([take & (to < 64), take & (to >= 64)], axis=2).astype(f32)
    data["w_out2"] = tiles_in(spread_heads(a[l + "Wo"].T, 1).T)[None]
    data["vec2"] = np.concatenate([columns(spread_heads(a[l + "bq"], 1)), columns(a[l + "bk"]), columns(spread_heads(a[l + "bv"], 4))], axis=1)[:, None]
    data["row2"] = a[l + "bo"][None, None]
    data["gamma"] = a[l + "gamma"][None]
    data["beta"] = a[l + "beta"][None]
    data["mask2"] = a["mask_Bx1xSxS2_ff0"].reshape(B, QT, P, S).transpose(0, 2, 1, 3)

    l = "L3_xattn_"
    data["m_big"] = np.stack([tiles_in(a[l + k].T) for k in ("Wk", "Wv", "Wr", "Wg", "Wo", "Wfk", "Wfr", "Wfv")], axis=1)
    data["m_maa1"] = tiles_in(a[l + "maa_w1"])
    data["m_maa2"] = a[l + "maa_w2"][:4].reshape(P, D)
    data["m_maa2g"] = a[l + "maa_w2"][4]
    data["m_td1"] = tiles_in(a[l + "td_w1"])
    data["m_td2"] = a[l + "td_w2"]
    stack = a[l + "maa_stack"][0]
    vec3 = [a[l + "ln1_w"], a[l + "ln1_b"], a[l + "ln2_w"], a[l + "ln2_b"], a[l + "maa_x"], *stack, a[l + "time_decay"], a[l + "u"].reshape(-1),
            a[l + "gn_w"], a[l + "gn_b"], a[l + "ffn_maa_k"], a[l + "ffn_maa_r"]]
    data["m_vec"] = np.concatenate([columns(v) for v in vec3], axis=1)
    data["m_s0"] = a["ctx_2048"][:, 2:18].reshape(B, FT, P, 16).transpose(0, 2, 1, 3)
    data["m_before"] = a["ctx_2048"][:, [1, 0]].reshape(B, 2, FT, P).transpose(3, 0, 1, 2)
    head, inner = np.arange(P) // 16, np.arange(P) % 16
    same = head[:, None] == head[None, :]
    data["m_heads"] = same.astype(f32)
    data["m_spread"] = np.stack([(same & (inner[:, None] == j)) for j in range(16)], axis=1).astype(f32)
    data["m_gather"] = np.stack([(same & (inner[None, :] == j)) for j in range(16)], axis=1).astype(f32)

    nc = bacc.Bacc("TRN2", target_bir_lowering=False, num_devices=1)
    data = {k: np.ascontiguousarray(v) for k, v in data.items()}
    t = {k: nc.dram_tensor(f"in_{k}", v.shape, mybir.dt.from_np(v.dtype), kind="ExternalInput").ap() for k, v in data.items()}
    out = nc.dram_tensor("out_0", (B, T, D), F32, kind="ExternalOutput").ap()
    shared = {k: t[k] for k in ("ident", "ones", "ctx_t", "stack")}
    two = dict(shared, mask=t["mask_u8"], **{k: t[k] for k in ("w_qkv", "w_out", "w_fc", "w_pr", "vec", "row")})
    gqa = dict(shared, mask=t["mask2"], w_qkv=t["w_q2"], w_kv=t["w_kv2"], pick=t["pick2"], w_out=t["w_out2"], vec=t["vec2"], row=t["row2"], gamma=t["gamma"], beta=t["beta"])
    mix = {k[2:]: v for k, v in t.items() if k.startswith("m_")}
    mix["ident"] = t["ident"]
    network(nc, t["x"], out, two, gqa, mix)
    r = run_bass_kernel_spmd(nc, [{f"in_{k}": v for k, v in data.items()}], core_ids=[0])
    return r.results[0]["out_0"]
```

```python
from contextlib import ExitStack

import concourse.bass as bass
from concourse import mybir

F32 = mybir.dt.float32
F32R = mybir.dt.float32r
U8 = mybir.dt.uint8
ALU = mybir.AluOpType
ACT = mybir.ActivationFunctionType

P = 128
B = 4
T = 512
D = 512
S = 1024
FT = D // P
QT = T // P
KT = S // P
HPG = 4
HR = P // HPG
STRIP = 7 * HR
F_TILES = 4 * D // P
FF = 4
UNITS = HPG * QT
BIG = 1.0e30


def attention_block(nc, name, layers, groups, scale, dram, x_res, feed_forward):
    G = groups
    with ExitStack() as ctx:
        def sb(what, shape, dt=F32):
            return ctx.enter_context(nc.sbuf_tensor(f"{name}_{what}", shape, dt))

        def sem(what):
            return ctx.enter_context(nc.semaphore(f"{name}_{what}"))

        four = [ctx.enter_context(nc.psum_tensor(f"{name}_score{i}", [P, 512], F32)) for i in range(4)]
        half = [ctx.enter_context(nc.psum_tensor(f"{name}_half{i}", [P, 512], F32)) for i in range(2)]
        head_out = ctx.enter_context(nc.psum_tensor(f"{name}_head_out", [P, 512], F32))
        turn = ctx.enter_context(nc.psum_tensor(f"{name}_turn", [P, 512], F32))
        four = [t[:, :] for t in four]

        ident = sb("ident", [P, P])
        ctx_t = sb("ctx_t", [P, FT, S])
        xn = sb("xn", [P, QT, D])
        h_t = sb("h_t", [P, FT, T])
        if feed_forward:
            w_qkv = sb("w_qkv", [P, 3, FT, P])
        else:
            w_qkv = sb("w_q", [P, 1, FT, P])
            w_kv = sb("w_kv", [P, 2, FT, P])
            pick_raw = sb("pick_raw", [P, 2, P])
            pick = sb("pick", [P, 2, P], F32R)
            ka_hi = sb("ka_hi", [P, S], F32R)
            ka_lo = sb("ka_lo", [P, S], F32R)
            v_all = xn[:, 2:4, :].rearrange("p a (b m) -> p (a b) m", m=P)
        if feed_forward:
            w_out = sb("w_out", [P, G, D])
        vec = sb("vec", [P, layers, dram["vec"].shape[2]])
        bias_row = sb("bias_row", [P, 2 if feed_forward else 1, D])
        stack_raw = xn[:, 0:2, :].rearrange("p a b -> p (a b)")[:, 0:HPG * STRIP].rearrange("p (j c) -> p j c", j=HPG)
        stack_w = sb("stack_w", [P, HPG, STRIP], F32R)
        q_s = xn[:, 2, :] if feed_forward else sb("q_s", [P, T])[:, :]
        q_hi = sb("q_hi", [P, T], F32R)
        q_lo = sb("q_lo", [P, T], F32R)
        q_st = sb("q_st", [P, HPG, T], F32R)
        k_st = sb("k_st", [P, HPG if feed_forward else 1, S], F32R)
        if feed_forward:
            k_hi = sb("k_hi", [P, S], F32R)
            k_lo = sb("k_lo", [P, S], F32R)

        def stacker(j, low, keys):
            at = HR * ((1 if low else 3) if keys else (2 if low else 0))
            return stack_w[:, j, at:at + P]

        out_u = xn[:, 0, :]
        out_n = xn[:, 1, :].rearrange("p (q m) -> p q m", q=QT)
        v = sb("v", [P, KT, P if feed_forward else HR])
        probs = sb("probs", [P, 2, HPG, S])
        probs_t = sb("probs_t", [P, 2, HPG, KT, P])
        low = sb("low", [P, UNITS])
        total = sb("total", [P, UNITS])
        rec = sb("rec", [P, UNITS])
        o_t = sb("o_t", [P, G, T])
        stats = sb("stats", [P, QT, 6])
        mv = sb("mv", [P, QT, 2])
        rstd = sb("rstd", [P, QT, 1])
        power = sb("power", [P, QT, 1])
        if feed_forward:
            mask_u8 = sb("mask_u8", [P, S], U8)
            mask = sb("mask", [P, 1, S])
            w_fc = [probs[:, 0, i, 0:D] for i in range(FF)]
            w_pr = [probs[:, 0, i, D:2 * D] for i in range(FF)]
            hid = [xn[:, 2 + i, :] for i in range(2)]
            h_hi = [q_st[:, ft, :] for ft in range(FT)]
            h_lo = [(k_hi, k_lo)[ft // 2][:, ft % 2 * T:ft % 2 * T + T] for ft in range(FT)]
            fc_hi, fc_lo = ([k_st[:, c + i, 0:D] for i in range(2)] for c in (0, 2))
            pr_hi, pr_lo = ([k_st[:, c + i, D:2 * D] for i in range(2)] for c in (0, 2))
            hid_hi, hid_lo = q_hi, q_lo
            QB, KB, VB, LW, LB, LW2, LB2, FB = 0, G, 2 * G, 3 * G, 3 * G + 4, 3 * G + 8, 3 * G + 12, 3 * G + 16
        else:
            mask = sb("mask", [P, QT, S])
            w_out = probs[:, 0, :, :].rearrange("p j (a d) -> p (j a) d", d=D)
            gamma = sb("gamma", [P, D])
            beta = sb("beta", [P, D])
            QB, KB, VB = 0, G, G + 1
        LN = 2 if feed_forward else 1
        NORMS = LN

        s_pass_act, s_pass_dve, s_pass_sp, s_pass_pool = (sem("pass_" + e) for e in ("act", "dve", "sp", "pool"))
        CONST = 16 * (3 if feed_forward else 6)
        if feed_forward:
            STACKS = [(True, j, 0) for j in range(HPG)] + [(False, j, 0) for j in range(HPG)]
            LATE = [(True, j, 1) for j in range(HPG)]
        else:
            STACKS = [(True, 0, 0), (True, 0, 1)] + [(False, j, 0) for j in range(HPG)]
            LATE = []
        NS = len(STACKS)
        TILES = 3 if feed_forward else 1
        PIECES = TILES + NS + (len(LATE) + 2 if feed_forward else 0)
        TAKES_DVE = 4 if feed_forward else 2
        TAKES_ACT = 3 if feed_forward else 2
        PIECES_DVE = TAKES_DVE + NS // 2
        EARLY_ACT = TAKES_ACT + NS // 2
        PIECES_ACT = EARLY_ACT + (len(LATE) + 2 if feed_forward else 0)
        s_const = sem("const_loaded")
        s_ctx = sem("ctx_loaded")
        s_wqkv = sem("wqkv_loaded")
        s_wout = sem("wout_loaded")
        s_row = sem("bias_row_loaded")
        s_bias = sem("bias_row_added")
        s_mask = sem("mask_loaded")
        s_mready = sem("mask_ready")
        s_xn = sem("xn_ready")
        s_tp = sem("h_turned")
        s_ht = sem("h_ready")
        s_pj = sem("projected")
        s_pjd = sem("prepared_dve")
        s_pja = sem("prepared_act")
        if not feed_forward:
            s_all, s_alla, s_alld = sem("kv_projected"), sem("kv_all_copied_act"), sem("kv_all_copied_dve")
            s_pad = sem("v_padded")
            s_pick = sem("pick_ready")
        s_sw = sem("stacker_ready")
        s_qk = sem("scores_ready")
        s_low = sem("scores_masked")
        s_exp = sem("probs_ready")
        s_tr = sem("probs_turned")
        s_ptd = sem("probs_t_first_half")
        s_pta = sem("probs_t_second_half")
        s_av = sem("head_summed")
        s_ou = sem("out_copied")
        s_n1 = sem("out_token_major")
        s_rec = sem("rec_ready")
        s_on = sem("out_normalised")
        s_n2 = sem("out_feature_major")
        s_ot = sem("o_t_ready")
        s_c = sem("attended")
        s_dve = sem("dve_chain")
        s_xadd = sem("x_updated")
        s_power = sem("power_set")
        s_var = sem("variance_ready")
        s_rstd = sem("rstd_ready")
        if feed_forward:
            s_wf = [sem(f"ff_weights_loaded{i}") for i in range(FF)]
            s_h1 = sem("hidden_ready")
            s_gl = sem("gelu_done")
            s_hhi, s_hlo = sem("h_high"), sem("h_low")
            s_fchi, s_fclo, s_prhi, s_prlo = sem("w_fc_high"), sem("w_fc_low"), sem("w_pr_high"), sem("w_pr_low")
            s_hidhi, s_hidlo = sem("hidden_high"), sem("hidden_low")
            FFT = F_TILES // FF
            s_p2 = [sem(f"hidden_used{i}") for i in range(FF)]

        block = ctx.enter_context(nc.Block())

        @block.sync
        def _(sp):
            sp.dma_start(ident[:, :], dram["ident"]).then_inc(s_const, 16)
            sp.dma_start(vec[:, :, :], dram["vec"]).then_inc(s_const, 16)
            sp.dma_start(stack_raw, dram["stack"]).then_inc(s_const, 16)
            if not feed_forward:
                sp.dma_start(gamma[:, :], dram["gamma"].to_broadcast((P, D))).then_inc(s_const, 16)
                sp.dma_start(beta[:, :], dram["beta"].to_broadcast((P, D))).then_inc(s_const, 16)
                sp.dma_start(w_kv[:, :, :, :], dram["w_kv"]).then_inc(s_const, 16)
            with sp.Fori(0, layers) as lay:
                with sp.Fori(0, B) as b:
                    n = lay * B + b
                    if feed_forward:
                        sp.wait_ge(s_pj, 1 + n * (PIECES * G))
                    else:
                        sp.wait_ge(s_all, 1 + n * 4)
                    sp.sem_inc(s_pass_sp, 1)
                    sp.dma_start(ctx_t[:, :, :], dram["ctx_t"][bass.ds(b, 1)].rearrange("a p f s -> (a p) f s")).then_inc(s_ctx, 16)
                    sp.wait_ge(s_bias, 1 + n * LN)
                    sp.sem_inc(s_pass_sp, 1)
                    sp.dma_start(bias_row[:, :, :], dram["row"][bass.ds(lay, 1)].to_broadcast((P, LN, D))).then_inc(s_row, 16)
                    sp.wait_ge(s_low, 1 + n * (2 * UNITS * G))
                    sp.sem_inc(s_pass_sp, 1)
                    if feed_forward:
                        sp.dma_start(mask_u8[:, :], dram["mask"][bass.ds(b, 1), :].to_broadcast((P, S))).then_inc(s_mask, 16)
                    else:
                        sp.dma_start(mask[:, :, :], dram["mask"][bass.ds(b, 1)].rearrange("a p q s -> (a p) q s")).then_inc(s_mask, 16)
                    with sp.Fori(0, G) as g:
                        sp.wait_ge(s_pj, 1 + (n * G + g) * PIECES)
                        sp.sem_inc(s_pass_sp, 1)
                        if not feed_forward:
                            sp.dma_start(pick_raw[:, :, :], dram["pick"][bass.ds(g, 1)].rearrange("a p k m -> (a p) k m")).then_inc(s_wqkv, 16)
                        sp.dma_start(w_qkv[:, :, :, :], dram["w_qkv"][bass.ds(lay * G + g, 1)].rearrange("a p k f m -> (a p) k f m")).then_inc(s_wqkv, 16)
                    sp.wait_ge(s_xadd, 1 + n * (QT * LN))
                    sp.sem_inc(s_pass_sp, 1)
                    if not feed_forward:
                        sp.wait_ge(s_tr, (n + 1) * (G * 2 * UNITS) - 2 * HPG)
                        sp.sem_inc(s_pass_sp, 1)
                    sp.dma_start(w_out[:, :, :], dram["w_out"][bass.ds(lay, 1)].rearrange("a p f m -> (a p) f m")).then_inc(s_wout, 16)
                    if feed_forward:
                        sp.wait_ge(s_tr, (n + 1) * (G * 2 * UNITS) - 2 * HPG)
                        sp.sem_inc(s_pass_sp, 1)
                        with sp.Fori(0, FFT) as ff:
                            for i in range(FF):
                                sp.wait_ge(s_p2[i], 1 + n * FFT + ff)
                                sp.sem_inc(s_pass_sp, 1)
                                sp.dma_start(w_fc[i], dram["w_fc"][bass.ds(lay * F_TILES + ff * FF + i, 1)].rearrange("a p f m -> (a p) (f m)")).then_inc(s_wf[i], 16)
                                sp.dma_start(w_pr[i], dram["w_pr"][bass.ds(lay * F_TILES + ff * FF + i, 1)].rearrange("a p m -> (a p) m")).then_inc(s_wf[i], 16)

        @block.tensor
        def _(pe):
            for s in (s_pj, s_tp, s_av) + ((*s_p2,) if feed_forward else (s_all,)):
                pe.sem_inc(s, 1)
            if feed_forward:
                pe.sem_inc(s_h1, 2)
            pe.wait_ge(s_const, CONST)
            pe.wait_ge(s_sw, 1)

            def turn_stream(n, which):
                pe.wait_ge(s_xn, n * LN + which + 1)
                for ft in range(FT):
                    for qt in range(QT):
                        last = pe.transpose(four[ft][:, qt * P:(qt + 1) * P], xn[:, qt, ft * P:(ft + 1) * P], ident[:, :])
                    last.then_inc(s_tp, 1)

            with pe.Fori(0, layers) as lay:
                with pe.Fori(0, B) as b:
                    n = lay * B + b
                    pe.wait_ge(s_xadd, 1 + n * (QT * LN))
                    turn_stream(n, 0)
                    pe.wait_ge(s_ht, n * (FT * LN) + FT)
                    pe.wait_ge(s_ctx, n * 16 + 16)

                    def values(w, half_of_keys, dst):
                        for c in range(4):
                            kt = 4 * half_of_keys + c
                            for ft in range(FT):
                                last = pe.matmul(dst[:, c * P:(c + 1) * P], ctx_t[:, ft, kt * P:(kt + 1) * P], w[:, ft, :], start=(ft == 0), stop=(ft == FT - 1))
                        return last

                    if not feed_forward:
                        for s in range(2):
                            for ft in range(FT):
                                last = pe.matmul(four[s], w_kv[:, 0, ft, :], ctx_t[:, ft, 512 * s:512 * s + 512], start=(ft == 0), stop=(ft == FT - 1))
                            last.then_inc(s_all, 1)
                        for s in range(2):
                            values(w_kv[:, 1, :, :], s, four[2 + s]).then_inc(s_all, 1)
                        pe.wait_ge(s_alla, n * 3 + 3)
                        pe.wait_ge(s_alld, n * 3 + 3)

                    def project(m, piece):
                        if piece == ("k0" if feed_forward else "q"):
                            pe.wait_ge(s_wqkv, (m + 1) * (16 if feed_forward else 32))
                            pe.wait_ge(s_low, 1 + m * (2 * UNITS))
                        if piece in ("k0", "k1"):
                            i = int(piece[1])
                            for ft in range(FT):
                                last = pe.matmul(four[i], w_qkv[:, 1, ft, :], ctx_t[:, ft, 512 * i:512 * i + 512], start=(ft == 0), stop=(ft == FT - 1))
                        elif piece == "q":
                            for ft in range(FT):
                                last = pe.matmul(four[2], w_qkv[:, 0, ft, :], h_t[:, ft, :], start=(ft == 0), stop=(ft == FT - 1))
                        last.then_inc(s_pj, 1)

                    def stack(m, r):
                        keys, j, i = STACKS[r]
                        if r >= 4:
                            pe.wait_ge((s_pja, s_pjd)[r % 2], m * (PIECES_ACT, PIECES_DVE)[r % 2] + ((TAKES_ACT, TAKES_DVE)[r % 2] + (r - 4) // 2 + 1))
                        elif feed_forward:
                            pe.wait_ge(s_pjd, m * PIECES_DVE + max(r, 1))
                        elif r == 0:
                            pe.wait_ge(s_pick, m + 1)
                        elif r == 3:
                            pe.wait_ge(s_pjd, m * PIECES_DVE + 1)
                        if keys:
                            hi, lo = (k_hi, k_lo) if feed_forward else (ka_hi, ka_lo)
                            hi, lo = hi[:, 512 * i:512 * i + 512], lo[:, 512 * i:512 * i + 512]
                        else:
                            pe.wait_ge(s_pjd, m * PIECES_DVE + (4 if feed_forward else 2))
                            hi, lo = q_hi[:, :], q_lo[:, :]
                        if keys and not feed_forward:
                            w_hi, w_lo = pick[:, 0, :], pick[:, 1, :]
                        else:
                            w_hi, w_lo = stacker(j, False, keys), stacker(j, True, keys)
                        pe.matmul(four[(r + 3) % 4], w_hi, hi, start=True, stop=False)
                        pe.matmul(four[(r + 3) % 4], w_lo, lo, start=False, stop=True).then_inc(s_pj, 1)

                    def late_stack(m, r):
                        _, j, i = LATE[r]
                        if r >= 2:
                            pe.wait_ge(s_pja, m * PIECES_ACT + (EARLY_ACT + r - 1))
                        pe.matmul(half[r % 2][:, :], stacker(j, False, True), k_hi[:, 512 * i:512 * i + 512], start=True, stop=False)
                        pe.matmul(half[r % 2][:, :], stacker(j, True, True), k_lo[:, 512 * i:512 * i + 512], start=False, stop=True).then_inc(s_pj, 1)

                    def late_values(m, s):
                        pe.wait_ge(s_pja, m * PIECES_ACT + (EARLY_ACT + len(LATE) - 1 + s))
                        values(w_qkv[:, 2, :, :], s, half[s]).then_inc(s_pj, 1)

                    def attend(m, then):
                        pe.wait_ge(s_pjd, (m + 1) * PIECES_DVE)
                        pe.wait_ge(s_pja, m * PIECES_ACT + EARLY_ACT)

                        def scores(t, j):
                            qt, s = divmod(t, 2)
                            if t:
                                pe.wait_ge(s_low, 1 + m * (2 * UNITS) + (HPG * (t - 1) + j + 1))
                            pe.matmul(four[j], q_st[:, j, qt * P:(qt + 1) * P], k_st[:, j if feed_forward else 0, 512 * s:512 * s + 512],
                                      start=True, stop=True).then_inc(s_qk, 1)

                        def turn_probs(qt, j):
                            u = HPG * qt + j
                            pe.wait_ge(s_exp, 1 + m * UNITS + (u + 1))
                            for s in range(2):
                                pe.wait_ge((s_ptd, s_pta)[s], 1 + m * UNITS + u)
                                for c in range(4):
                                    last = pe.transpose(half[s][:, c * P:(c + 1) * P], probs[:, qt % 2, j, (4 * s + c) * P:(4 * s + c + 1) * P], ident[:, :])
                                last.then_inc(s_tr, 1)

                        def weigh(qt, part):
                            if part == 0:
                                pe.wait_ge(s_ptd, 1 + m * UNITS + HPG * (qt + 1))
                                pe.wait_ge(s_pta, 1 + m * UNITS + HPG * (qt + 1))
                                if qt == 0:
                                    pe.wait_ge(s_ou, 1 + m)
                            for kt in (2 * part, 2 * part + 1):
                                for j in range(HPG):
                                    last = pe.matmul(head_out[HR * j:HR * j + HR, qt * P:(qt + 1) * P],
                                                     v[:, kt, HR * j:HR * j + HR] if feed_forward else v[:, kt, :],
                                                     probs_t[:, qt % 2, j, kt, :], start=(kt == 0), stop=(kt == KT - 1))
                            if part == 3:
                                last.then_inc(s_av, 1)

                        def out_token_major():
                            pe.wait_ge(s_ou, 1 + m + 1)
                            for qt in range(QT):
                                last = pe.transpose(turn[:, qt * P:(qt + 1) * P], out_u[:, qt * P:(qt + 1) * P], ident[:, :])
                            last.then_inc(s_n1, 1)

                        def out_feature_major():
                            pe.wait_ge(s_on, m + 1)
                            for qt in range(QT):
                                last = pe.transpose(turn[:, qt * P:(qt + 1) * P], out_n[:, qt, :], ident[:, :])
                            last.then_inc(s_n2, 1)

                        for t in range(2 * QT):
                            qt, s = divmod(t, 2)
                            if feed_forward and t == 1:
                                pe.wait_ge(s_pja, m * PIECES_ACT + (EARLY_ACT + len(LATE)))
                            for k in range(2):
                                scores(t, 2 * k)
                                scores(t, 2 * k + 1)
                                if feed_forward and t == 0:
                                    late_stack(m, 2 * k)
                                    late_stack(m, 2 * k + 1)
                                if feed_forward and t == 1:
                                    late_values(m, k)
                                if qt >= 2:
                                    weigh(qt - 2, 2 * s + k)
                                if qt >= 1:
                                    if feed_forward and qt == 1 and s == 0 and k == 0:
                                        pe.wait_ge(s_pja, (m + 1) * PIECES_ACT)
                                    turn_probs(qt - 1, 2 * s + k)
                        pieces = () if not then else ("k0", "k1", "q") if feed_forward else ("q",)
                        turn_probs(QT - 1, 0)
                        for piece in pieces[0:1]:
                            project(m + 1, piece)
                        for j in range(1, HPG):
                            weigh(QT - 2, j - 1)
                            turn_probs(QT - 1, j)
                        weigh(QT - 2, 3)
                        for piece in pieces[1:]:
                            project(m + 1, piece)
                        for part in range(4):
                            weigh(QT - 1, part)
                        if then:
                            stack(m + 1, 0)
                            stack(m + 1, 1)
                        out_token_major()
                        for r in range(2, NS - 2) if then else ():
                            stack(m + 1, r)
                        out_feature_major()
                        for r in range(NS - 2, NS) if then else ():
                            stack(m + 1, r)

                    for piece in ("k0", "k1", "q") if feed_forward else ("q",):
                        project(n * G, piece)
                    for r in range(NS):
                        stack(n * G, r)
                    with pe.Fori(0, G - 1) as g:
                        attend(n * G + g, True)
                    attend(n * G + (G - 1), False)
                    pe.wait_ge(s_ot, 1 + n * G + G)
                    pe.wait_ge(s_wout, n * 16 + 16)
                    pe.wait_ge(s_low, 1 + (n + 1) * (G * 2 * UNITS))
                    for qt in range(QT):
                        for g in range(G):
                            last = pe.matmul(four[qt], o_t[:, g, qt * P:(qt + 1) * P], w_out[:, g, :], start=(g == 0), stop=(g == G - 1))
                        last.then_inc(s_c, 1)
                    if feed_forward:
                        turn_stream(n, 1)
                        pe.wait_ge(s_hlo, (n + 1) * FT)
                        def hidden(k, i, first=False):
                            pe.wait_ge(s_fclo, k * FF + i + 1)
                            pe.wait_ge(s_gl, k * FF + i + (1 if first else 0))
                            for ft in range(FT):
                                w_hi, w_lo = fc_hi[i % 2][:, ft * P:(ft + 1) * P], fc_lo[i % 2][:, ft * P:(ft + 1) * P]
                                pe.matmul(half[i % 2][:, :], w_hi, h_hi[ft], start=(ft == 0), stop=False)
                                pe.matmul(half[i % 2][:, :], w_hi, h_lo[ft], start=False, stop=False)
                                last = pe.matmul(half[i % 2][:, :], w_lo, h_hi[ft], start=False, stop=(ft == FT - 1))
                            last.then_inc(s_h1, 1)

                        def back(k, i, first=False):
                            pe.wait_ge(s_prlo, k * FF + i + 1)
                            pe.wait_ge(s_hidlo, 2 + k * FF + i + 1)
                            for qt in range(QT):
                                x_hi, x_lo = hid_hi[:, qt * P:(qt + 1) * P], hid_lo[:, qt * P:(qt + 1) * P]
                                pe.matmul(four[qt], x_hi, pr_hi[i % 2], start=first, stop=False, skip_group_check=True)
                                pe.matmul(four[qt], x_hi, pr_lo[i % 2], start=False, stop=False, skip_group_check=True)
                                last = pe.matmul(four[qt], x_lo, pr_hi[i % 2], start=False, stop=False, skip_group_check=True)
                            last.then_inc(s_p2[i], 1)

                        def forward(k, then):
                            for i in range(2, FF):
                                hidden(k, i)
                                back(k, i - 1)
                            if then:
                                hidden(k + 1, 0)
                            back(k, FF - 1)
                            if then:
                                hidden(k + 1, 1)
                                back(k + 1, 0)

                        hidden(n * FFT, 0, first=True)
                        hidden(n * FFT, 1)
                        back(n * FFT, 0, first=True)
                        with pe.Fori(0, FFT - 1) as ff:
                            forward(n * FFT + ff, True)
                        forward(n * FFT + (FFT - 1), False)

        @block.gpsimd
        def _(pool):
            pool.sem_inc(s_bias, 1)
            pool.memset(power[:, :, :], -0.5).then_inc(s_power, 1)
            pool.wait_ge(s_power, 1)

            def add_bias(n, b, which):
                pool.wait_ge(s_row, n * 16 + 16)
                pool.wait_ge(s_xn, n * LN + which + 1)
                pool.sem_inc(s_pass_pool, 1)
                for qt in range(QT):
                    xs = x_res[:, bass.ds(b, 1), qt, :].rearrange("p a d -> p (a d)")
                    last = pool.tensor_tensor(xs, xs, bias_row[:, which, :], ALU.add)
                last.then_inc(s_bias, 1)

            if not feed_forward:
                with pool.Fori(0, B) as b:
                    add_bias(b, b, 0)
                    with pool.Fori(0, G) as g:
                        m = b * G + g
                        pool.wait_ge(s_wqkv, (m + 1) * 32)
                        pool.wait_ge(s_pj, 1 + m * PIECES)
                        pool.sem_inc(s_pass_pool, 1)
                        pool.tensor_copy(pick[:, :, :], pick_raw[:, :, :]).then_inc(s_pick, 1)
                    pool.wait_ge(s_var, b + 1)
                    pool.tensor_tensor(rstd[:, :, :], rstd[:, :, :], power[:, :, :], ALU.pow).then_inc(s_rstd, 1)
                return
            with pool.Fori(0, layers) as lay, pool.Fori(0, B) as b:
                n = lay * B + b
                for which in range(NORMS):
                    pool.wait_ge(s_var, n * NORMS + which + 1)
                    pool.tensor_tensor(rstd[:, :, :], rstd[:, :, :], power[:, :, :], ALU.pow).then_inc(s_rstd, 1)
                    if which == 0:
                        add_bias(n, b, 0)
                pool.wait_ge(s_qk, (n + 1) * (G * 2 * UNITS))
                pool.sem_inc(s_pass_pool, 1)
                with pool.Fori(0, FFT) as ff:
                    k = n * FFT + ff
                    for i in range(FF):
                        pool.wait_ge(s_wf[i], k * 32 + 32)
                        pool.wait_ge(s_h1, 1 + k * FF + i)
                        pool.sem_inc(s_pass_pool, 1)
                        pool.tensor_copy(fc_hi[i % 2], w_fc[i]).then_inc(s_fchi, 1)
                        pool.wait_ge(s_p2[(i + 2) % FF], 1 + k + (i >= 2))
                        pool.sem_inc(s_pass_pool, 1)
                        pool.tensor_copy(pr_hi[i % 2], w_pr[i]).then_inc(s_prhi, 1)
                add_bias(n, b, 1)

        @block.scalar
        def _(act):
            for s in (s_ot, s_pta, s_ou, s_exp) + ((s_gl,) if feed_forward else ()):
                act.sem_inc(s, 1)
            act.wait_ge(s_const, CONST)

            act.copy(stack_w[:, :, :], stack_raw).then_inc(s_sw, 1)
            if not feed_forward:
                act.wait_ge(s_pad, 1)

            def feature_major(n, lay, which):
                for ft in range(FT):
                    act.wait_ge(s_tp, 1 + n * (FT * LN) + (which * FT + ft + 1))
                    if feed_forward:
                        lw, lb = ((LW, LB), (LW2, LB2))[which]
                        act.activation(h_t[:, ft, :], four[ft], ACT.Identity, bias=vec[:, bass.ds(lay, 1), lb + ft:lb + ft + 1].rearrange("p a b -> p (a b)"),
                                       scale=vec[:, bass.ds(lay, 1), lw + ft:lw + ft + 1].rearrange("p a b -> p (a b)")).then_inc(s_ht, 1)
                    else:
                        act.copy(h_t[:, ft, :], four[ft]).then_inc(s_ht, 1)

            def column(lay, c):
                return vec[:, bass.ds(lay, 1), bass.ds(c, 1)].rearrange("p a b -> p (a b)")

            with act.Fori(0, layers) as lay:
                with act.Fori(0, B) as b:
                    n = lay * B + b
                    feature_major(n, lay, 0)
                    if not feed_forward:
                        for s in range(2):
                            act.wait_ge(s_all, 1 + n * 4 + (s + 1))
                            act.activation(ka_hi[:, 512 * s:512 * s + 512], four[s], ACT.Identity, bias=vec[:, 0, KB:KB + 1]).then_inc(s_alla, 1)
                        act.wait_ge(s_all, 1 + n * 4 + 4)
                        act.copy(v_all[:, 4:8, :].rearrange("p a b -> p (a b)"), four[3]).then_inc(s_alla, 1)
                        act.wait_ge(s_alla, n * 3 + 3)
                        act.wait_ge(s_alld, n * 3 + 3)

                    def take_keys(m, g, i):
                        act.wait_ge(s_pj, 1 + m * PIECES + (i + 1))
                        act.sem_inc(s_pass_act, 1)
                        act.activation(k_hi[:, 512 * i:512 * i + 512], four[i], ACT.Identity, bias=column(lay, g + KB)).then_inc(s_pja, 1)

                    def take_query(m):
                        act.wait_ge(s_pjd, m * PIECES_DVE + (3 if feed_forward else 1))
                        act.copy(q_hi[:, :], q_s).then_inc(s_pja, 1)

                    def take_values(m, g):
                        if not feed_forward:
                            act.wait_ge(s_av, 1 + m * QT)
                            act.sem_inc(s_pass_act, 1)
                            act.copy(v[:, :, 0:16], v_all[:, :, bass.ds(g * 16, 16)]).then_inc(s_pja, 1)

                    def take_late(m):
                        for r, (_, j, i) in enumerate(LATE):
                            act.wait_ge(s_pj, 1 + m * PIECES + (TILES + NS + r + 1))
                            act.copy(k_st[:, j, 512 * i:512 * i + 512], half[r % 2][:, :]).then_inc(s_pja, 1)
                        for s in range(2):
                            act.wait_ge(s_pj, 1 + m * PIECES + (TILES + NS + len(LATE) + s + 1))
                            act.copy(v[:, 4 * s:4 * s + 4, :].rearrange("p a b -> p (a b)"), half[s][:, :]).then_inc(s_pja, 1)

                    def take_stack(m, r):
                        keys, j, i = STACKS[r]
                        act.wait_ge(s_pj, 1 + m * PIECES + (TILES + r + 1))
                        act.copy(k_st[:, j, 512 * i:512 * i + 512] if keys else q_st[:, j, :], four[(r + 3) % 4]).then_inc(s_pja, 1)

                    def attend(m, g, then):
                        def exponentials(qt, j):
                            u = HPG * qt + j
                            act.wait_ge(s_low, 1 + m * (2 * UNITS) + (2 * HPG * qt + HPG + j + 1))
                            act.activation(probs[:, qt % 2, j, :], probs[:, qt % 2, j, :], ACT.Exp, bias=low[:, u:u + 1], scale=-1.0,
                                           accum_out=total[:, u:u + 1]).then_inc(s_exp, 1)

                        def take_turned(qt, j):
                            act.wait_ge(s_tr, m * (2 * UNITS) + 2 * (HPG * qt + j) + 2)
                            if qt >= 2:
                                act.wait_ge(s_av, 1 + m * QT + (qt - 1))
                            act.copy(probs_t[:, qt % 2, j, 4:8, :].rearrange("p a b -> p (a b)"), half[1][:, :]).then_inc(s_pta, 1)

                        if feed_forward:
                            take_late(m)
                        for qt in range(QT + 1):
                            if qt >= 1:
                                exponentials(qt - 1, 2)
                                take_turned(qt - 1, 0)
                                if qt == QT and then and feed_forward:
                                    take_keys(m + 1, g + 1, 0)
                                exponentials(qt - 1, 3)
                                take_turned(qt - 1, 1)
                                take_turned(qt - 1, 2)
                            if qt < QT:
                                exponentials(qt, 0)
                            if qt >= 1:
                                take_turned(qt - 1, 3)
                            if qt < QT:
                                exponentials(qt, 1)
                        if then:
                            if feed_forward:
                                take_keys(m + 1, g + 1, 1)
                            take_query(m + 1)
                        act.wait_ge(s_av, 1 + m * QT + QT)
                        act.copy(out_u, head_out[:, :]).then_inc(s_ou, 1)
                        if then:
                            take_values(m + 1, g + 1)
                            for r in range(0, NS - 2, 2):
                                take_stack(m + 1, r)
                        act.wait_ge(s_n2, m + 1)
                        act.sem_inc(s_pass_act, 1)
                        act.activation(o_t[:, bass.ds(g, 1), :].rearrange("p a b -> p (a b)"), turn[:, :], ACT.Identity,
                                       bias=column(lay, g + VB)).then_inc(s_ot, 1)
                        if then:
                            take_stack(m + 1, NS - 2)

                    if feed_forward:
                        take_keys(n * G, 0, 0)
                        take_keys(n * G, 0, 1)
                    take_query(n * G)
                    take_values(n * G, 0)
                    for r in range(0, NS, 2):
                        take_stack(n * G, r)
                    with act.Fori(0, G - 1) as g:
                        attend(n * G + g, g, True)
                    attend(n * G + (G - 1), G - 1, False)
                    if feed_forward:
                        feature_major(n, lay, 1)
                        for ft in range(FT):
                            act.wait_ge(s_ht, n * (FT * LN) + (FT + ft + 1))
                            act.sem_inc(s_pass_act, 1)
                            act.copy(h_hi[ft], h_t[:, ft, :]).then_inc(s_hhi, 1)
                        with act.Fori(0, FFT) as ff:
                            k = n * FFT + ff
                            for i in range(FF):
                                act.wait_ge(s_h1, 2 + k * FF + (i + 1))
                                act.wait_ge(s_hidlo, 1 + k * FF + i)
                                act.sem_inc(s_pass_act, 1)
                                act.activation(hid[i % 2], half[i % 2][:, :], ACT.Gelu_apprx_tanh, bias=column(lay, ff * FF + (FB + i))).then_inc(s_gl, 1)
                                act.wait_ge(s_gl, 1 + k * FF + (i + 1))
                                act.wait_ge(s_p2[(i + 3) % FF], 1 + k + (i >= 1))
                                act.sem_inc(s_pass_act, 1)
                                act.copy(hid_hi[:, :], hid[i % 2]).then_inc(s_hidhi, 1)

        @block.vector
        def _(dve):
            for s in (s_low, s_xadd, s_ptd):
                dve.sem_inc(s, 1)
            if feed_forward:
                dve.sem_inc(s_hidlo, 2)
            dve.wait_ge(s_const, CONST)
            dve.wait_ge(s_sw, 1)

            CH = 2 * QT
            if not feed_forward:
                dve.memset(v[:, :, :], 0.0).then_inc(s_pad, 1)
            with dve.Fori(0, layers) as lay:
                with dve.Fori(0, B) as b:
                    n = lay * B + b
                    chain = n * (CH * LN + (0 if feed_forward else 3 * QT))
                    if feed_forward:
                        for qt in range(QT):
                            dve.sem_inc(s_pass_dve, 1)
                            dve.bn_stats(stats[:, qt, :], x_res[:, bass.ds(b, 1), qt, :].rearrange("p a d -> p (a d)")).then_inc(s_dve, 1)
                        for qt in range(QT):
                            dve.wait_ge(s_dve, chain + (qt + 1))
                            dve.sem_inc(s_pass_dve, 1)
                            dve.bn_aggr(mv[:, qt, :], stats[:, qt, :]).then_inc(s_dve, 1)
                        dve.wait_ge(s_dve, chain + 2 * QT)
                        dve.tensor_scalar(rstd[:, :, 0:1], mv[:, :, 1:2], 1e-5, None, ALU.add).then_inc(s_var, 1)
                        dve.wait_ge(s_rstd, n * NORMS + 1)
                        dve.wait_ge(s_tp, 1 + n * (FT * LN))
                        for qt in range(QT):
                            last = dve.tensor_scalar(xn[:, qt, :], x_res[:, bass.ds(b, 1), qt, :].rearrange("p a d -> p (a d)"), mv[:, qt, 0:1], rstd[:, qt, 0:1],
                                                     ALU.subtract, ALU.mult)
                        last.then_inc(s_xn, 1)
                        dve.wait_ge(s_mask, n * 16 + 16)
                        dve.tensor_scalar(mask[:, 0, :], mask_u8[:, :], -BIG, BIG, ALU.mult, ALU.add).then_inc(s_mready, 1)
                    else:
                        dve.wait_ge(s_tp, 1 + n * (FT * LN))
                        dve.tensor_copy(xn[:, :, :], x_res[:, bass.ds(b, 1), :, :].rearrange("p a q d -> p (a q) d")).then_inc(s_xn, 1)
                        dve.wait_ge(s_mask, n * 16 + 16)
                        dve.tensor_scalar(mask[:, :, :], mask[:, :, :], -1.0, None, ALU.mult).then_inc(s_mready, 1)
                    dve.wait_ge(s_mready, n + 1)
                    dve.sem_inc(s_pass_dve, 1)
                    if not feed_forward:
                        for s in range(2):
                            dve.wait_ge(s_alla, n * 3 + (s + 1))
                            dve.scalar_tensor_tensor(ka_lo[:, 512 * s:512 * s + 512], four[s], vec[:, 0, KB:KB + 1], ka_hi[:, 512 * s:512 * s + 512],
                                                     ALU.add, ALU.subtract).then_inc(s_alld, 1)
                        dve.wait_ge(s_all, 1 + n * 4 + 3)
                        dve.tensor_copy(v_all[:, 0:4, :].rearrange("p a b -> p (a b)"), four[2]).then_inc(s_alld, 1)

                    def take_keys(m, g, i):
                        dve.wait_ge(s_pja, m * PIECES_ACT + (i + 1))
                        dve.sem_inc(s_pass_dve, 1)
                        dve.scalar_tensor_tensor(k_lo[:, 512 * i:512 * i + 512], four[i], vec[:, bass.ds(lay, 1), bass.ds(g + KB, 1)].rearrange("p a b -> p (a b)"),
                                                 k_hi[:, 512 * i:512 * i + 512], ALU.add, ALU.subtract).then_inc(s_pjd, 1)

                    def take_query(m, g):
                        dve.wait_ge(s_pj, 1 + m * PIECES + (3 if feed_forward else 1))
                        dve.tensor_scalar(q_s, four[2], vec[:, bass.ds(lay, 1), bass.ds(g + QB, 1)].rearrange("p a b -> p (a b)"),
                                          -scale, ALU.add, ALU.mult).then_inc(s_pjd, 1)
                        dve.wait_ge(s_pja, m * PIECES_ACT + (3 if feed_forward else 1))
                        dve.tensor_tensor(q_lo[:, :], q_s, q_hi[:, :], ALU.subtract).then_inc(s_pjd, 1)

                    def take_stack(m, r):
                        keys, j, i = STACKS[r]
                        dve.wait_ge(s_pj, 1 + m * PIECES + (TILES + r + 1))
                        dve.tensor_copy(k_st[:, j, 512 * i:512 * i + 512] if keys else q_st[:, j, :], four[(r + 3) % 4]).then_inc(s_pjd, 1)

                    def attend(m, g, then):
                        def mask_scores(t, j):
                            qt, s = divmod(t, 2)
                            u = HPG * qt + j
                            dve.wait_ge(s_qk, m * (2 * UNITS) + (HPG * t + j + 1))
                            if s == 0 and qt >= 2:
                                dve.wait_ge(s_tr, m * (2 * UNITS) + 2 * (HPG * (qt - 2) + j) + 2)
                            if s == 1:
                                dve.wait_ge(s_low, 1 + m * (2 * UNITS) + (HPG * (t - 1) + j + 1))
                            dve.sem_inc(s_pass_dve, 1)
                            dve.tensor_tensor_reduce(out=probs[:, qt % 2, j, 512 * s:512 * s + 512], in0=four[j],
                                                     in1=mask[:, 0 if feed_forward else qt, 512 * s:512 * s + 512], scale=1.0,
                                                     scalar=3.0e38 if s == 0 else low[:, u:u + 1], op0=ALU.add, op1=ALU.min,
                                                     accum_out=low[:, u:u + 1]).then_inc(s_low, 1)

                        def take_turned(qt, j):
                            dve.wait_ge(s_tr, m * (2 * UNITS) + 2 * (HPG * qt + j) + 1)
                            if qt >= 2:
                                dve.wait_ge(s_av, 1 + m * QT + (qt - 1))
                            dve.tensor_copy(probs_t[:, qt % 2, j, 0:4, :].rearrange("p a b -> p (a b)"), half[0][:, :]).then_inc(s_ptd, 1)

                        for t in range(2 * QT):
                            qt, s = divmod(t, 2)
                            for k in range(2):
                                mask_scores(t, 2 * k)
                                mask_scores(t, 2 * k + 1)
                                if qt >= 1:
                                    take_turned(qt - 1, 2 * s + k)
                        take_turned(QT - 1, 0)
                        take_turned(QT - 1, 1)
                        if then and feed_forward:
                            take_keys(m + 1, g + 1, 0)
                        take_turned(QT - 1, 2)
                        take_turned(QT - 1, 3)
                        if then:
                            if feed_forward:
                                take_keys(m + 1, g + 1, 1)
                            take_query(m + 1, g + 1)
                            take_stack(m + 1, 1)
                        dve.wait_ge(s_exp, 1 + m * UNITS + UNITS)
                        dve.reciprocal(rec[:, :], total[:, :]).then_inc(s_rec, 1)
                        dve.wait_ge(s_rec, m + 1)
                        dve.wait_ge(s_n1, m + 1)
                        dve.tensor_tensor(out_n.rearrange("p q (j d) -> p q j d", j=HPG), turn[:, :].rearrange("p (q j d) -> p q j d", q=QT, j=HPG),
                                          rec[:, :].rearrange("p (q j a) -> p q j a", j=HPG, a=1).to_broadcast((P, QT, HPG, HR)), ALU.mult).then_inc(s_on, 1)
                        for r in range(3, NS, 2) if then else ():
                            take_stack(m + 1, r)

                    if feed_forward:
                        take_keys(n * G, 0, 0)
                        take_keys(n * G, 0, 1)
                    take_query(n * G, 0)
                    for r in range(1, NS, 2):
                        take_stack(n * G, r)
                    dve.sem_inc(s_pass_dve, 1)
                    with dve.Fori(0, G - 1) as g:
                        attend(n * G + g, g, True)
                    attend(n * G + (G - 1), G - 1, False)
                    chain2 = chain + (CH if feed_forward else 0)
                    dve.wait_ge(s_bias, 1 + n * LN + 1)
                    for qt in range(QT):
                        xs = x_res[:, bass.ds(b, 1), qt, :].rearrange("p a d -> p (a d)")
                        dve.wait_ge(s_c, n * QT + (qt + 1))
                        dve.tensor_tensor(xs, xs, four[qt], ALU.add).then_inc(s_xadd, 1)
                        dve.wait_ge(s_xadd, 1 + n * (QT * LN) + (qt + 1))
                        dve.sem_inc(s_pass_dve, 1)
                        dve.bn_stats(stats[:, qt, :], xs).then_inc(s_dve, 1)
                    for qt in range(QT):
                        dve.wait_ge(s_dve, chain2 + (qt + 1))
                        dve.sem_inc(s_pass_dve, 1)
                        dve.bn_aggr(mv[:, qt, :], stats[:, qt, :]).then_inc(s_dve, 1)
                    dve.wait_ge(s_dve, chain2 + 2 * QT)
                    dve.tensor_scalar(rstd[:, :, 0:1], mv[:, :, 1:2], 1e-5 if feed_forward else 1e-6, None, ALU.add).then_inc(s_var, 1)
                    dve.wait_ge(s_rstd, n * NORMS + NORMS)
                    if feed_forward:
                        for qt in range(QT):
                            last = dve.tensor_scalar(xn[:, qt, :], x_res[:, bass.ds(b, 1), qt, :].rearrange("p a d -> p (a d)"), mv[:, qt, 0:1], rstd[:, qt, 0:1],
                                                     ALU.subtract, ALU.mult)
                        last.then_inc(s_xn, 1)
                        for ft in range(FT):
                            dve.wait_ge(s_hhi, n * FT + (ft + 1))
                            dve.sem_inc(s_pass_dve, 1)
                            dve.tensor_tensor(h_lo[ft], h_t[:, ft, :], h_hi[ft], ALU.subtract).then_inc(s_hlo, 1)

                        def low_fc(k, i):
                            dve.wait_ge(s_fchi, k * FF + i + 1)
                            dve.sem_inc(s_pass_dve, 1)
                            dve.tensor_tensor(fc_lo[i % 2], w_fc[i], fc_hi[i % 2], ALU.subtract).then_inc(s_fclo, 1)

                        def low_pr(k, i):
                            dve.wait_ge(s_prhi, k * FF + i + 1)
                            dve.sem_inc(s_pass_dve, 1)
                            dve.tensor_tensor(pr_lo[i % 2], w_pr[i], pr_hi[i % 2], ALU.subtract).then_inc(s_prlo, 1)

                        def low_hidden(k, i):
                            dve.wait_ge(s_hidhi, k * FF + i + 1)
                            dve.sem_inc(s_pass_dve, 1)
                            dve.tensor_tensor(hid_lo[:, :], hid[i % 2], hid_hi[:, :], ALU.subtract).then_inc(s_hidlo, 1)

                        def low_parts(k, then):
                            for i in range(1, FF):
                                low_fc(k, i)
                                low_hidden(k, i - 1)
                                low_pr(k, i)
                            if then:
                                low_fc(k + 1, 0)
                            low_hidden(k, FF - 1)
                            if then:
                                low_pr(k + 1, 0)

                        low_fc(n * FFT, 0)
                        low_pr(n * FFT, 0)
                        with dve.Fori(0, FFT - 1) as ff:
                            low_parts(n * FFT + ff, True)
                        low_parts(n * FFT + (FFT - 1), False)
                        dve.wait_ge(s_p2[FF - 1], 1 + n * FFT + FFT)
                        dve.wait_ge(s_bias, 1 + n * LN + 2)
                        for qt in range(QT):
                            xs = x_res[:, bass.ds(b, 1), qt, :].rearrange("p a d -> p (a d)")
                            dve.tensor_tensor(xs, xs, four[qt], ALU.add).then_inc(s_xadd, 1)
                        dve.wait_ge(s_xadd, 1 + n * (QT * LN) + QT * LN)
                    else:
                        for step in range(3):
                            for qt in range(QT):
                                xs = x_res[:, bass.ds(b, 1), qt, :].rearrange("p a d -> p (a d)")
                                if step:
                                    dve.wait_ge(s_dve, chain2 + (CH + (step - 1) * QT + qt + 1))
                                if step == 0:
                                    dve.tensor_scalar(xs, xs, mv[:, qt, 0:1], rstd[:, qt, 0:1], ALU.subtract, ALU.mult).then_inc(s_dve, 1)
                                elif step == 1:
                                    dve.tensor_tensor(xs, xs, gamma[:, :], ALU.mult).then_inc(s_dve, 1)
                                else:
                                    dve.tensor_tensor(xs, xs, beta[:, :], ALU.add).then_inc(s_dve, 1)
                        dve.wait_ge(s_dve, chain2 + (CH + 3 * QT))

VEC3 = ("ln1_w", "ln1_b", "ln2_w", "ln2_b", "maa_x", "maa_k", "maa_w", "maa_v", "maa_r", "maa_g", "decay", "u", "gn_w", "gn_b", "ffn_k", "ffn_r")


def time_mix_block(nc, dram, x_res):
    NAMES = ("k", "w", "v", "r", "g")
    SLOTS = 23
    N = 16
    NB = 4
    LAG = 3
    with ExitStack() as ctx:
        def sb(what, shape, dt=F32):
            return ctx.enter_context(nc.sbuf_tensor(f"mix_{what}", shape, dt))

        def sem(what):
            return ctx.enter_context(nc.semaphore(f"mix_{what}"))

        bank = [ctx.enter_context(nc.psum_tensor(f"mix_bank{i}", [P, 512], F32)) for i in range(8)]
        ident = sb("ident", [P, P])
        spread = sb("spread", [P, N, P], F32R)
        gather = sb("gather", [P, N, P])
        heads = sb("heads", [P, P])
        w_maa1 = sb("w_maa1", [P, FT, 5 * 32])
        w_maa2 = sb("w_maa2", [P, 4, D])
        w_maa2g = sb("w_maa2g", [32, D])
        w_td1 = sb("w_td1", [P, FT, 64])
        w_td2 = sb("w_td2", [64, D])
        w_big = sb("w_big", [P, 8, FT, D])
        W = {name: w_big[:, i, :, :] for i, name in enumerate(("k", "v", "r", "g", "o", "fk", "fr", "fv"))}
        vec = sb("vec", [P, dram["vec"].shape[1]])
        column = {name: (lambda i: (lambda ft: vec[:, 4 * i + ft:4 * i + ft + 1]))(i) for i, name in enumerate(VEC3)}
        xn = sb("xn", [P, QT, D])
        xa = sb("xa", [P, FT, T + 1])
        mixed = [sb(f"mixed{i}", [P, FT, T]) for i in range(2)]
        spread_raw = mixed[1].rearrange("p a (b m) -> p (a b) m", m=P)
        v_hi = sb("v_hi", [P, T], F32R)
        v_lo = sb("v_lo", [P, T], F32R)
        sx = xn
        lora = sb("lora", [P, T])
        act_t = {name: sb(f"{name}_t", [P, FT, T]) for name in NAMES}
        lora_w = act_t["g"][0:64, 0, :]
        lora_g = act_t["g"][0:32, 1, :]
        s0 = sb("s0", [P, FT, N])
        before = sb("before", [P, B, 2, FT])
        a_j = [mixed[1][:, i, :] for i in range(NB)]
        state = [xa[:, i, :] for i in range(NB)]
        y_j = [xn[:, i, :] for i in range(NB)]
        spread_bank = [bank[i][:, :] for i in (6, 7, 0, 1)]
        bonus = lora
        stats = sb("stats", [P, QT, 6])
        mv = sb("mv", [P, QT, 2])
        rstd = sb("rstd", [P, QT, 1])
        power = sb("power", [P, QT, 1])
        og = mixed[0]
        kk = act_t["r"]
        gate = act_t["k"]

        LOADS = 9 * 16
        s_const = sem("const_loaded")
        s_big = [sem(x) for x in ("w_key_loaded", "w_mix_loaded", "w_rest_loaded")]
        s_spread, s_vhi, s_vlo = sem("spread_ready"), sem("v_high_ready"), sem("v_low_ready")
        s_first = sem("first_loaded")
        s_xn, s_tp, s_xa, s_sx, s_z = (sem(x) for x in ("xn_ready", "turned", "xa_ready", "sx_ready", "z_ready"))
        s_pp, s_pev = sem("projected"), sem("projection_copied")
        s_xx = sem("mix_ready")
        s_mix = sem("mixed_ready")
        s_vb, s_a = sem("v_spread"), sem("a_ready")
        s_s0, s_st, s_y, s_yu = sem("state_first"), sem("state_ready"), sem("y_ready"), sem("y_used")
        s_ruk, s_gp, s_gd, s_ga = sem("ruk_ready"), sem("heads_summed"), sem("norm_dve"), sem("norm_act")
        s_og, s_dec, s_pair, s_bonus, s_veps, s_half = (sem(x) for x in ("og_ready", "decay_exp", "mix_product", "bonus_ready", "norm_eps", "gate_product"))
        s_c, s_xadd = sem("mixed_out"), sem("x_updated")
        s_kk, s_kku, s_rr, s_gate, s_fv, s_end = (sem(x) for x in ("kk_psum", "kk_ready", "rr_psum", "gate_ready", "fv_psum", "x_final"))
        s_power, s_var, s_rstd, s_bn, s_mv = (sem(x) for x in ("power_set", "variance_ready", "rstd_ready", "bn_stats", "bn_aggr"))
        s_relu = sem("relu_ready")
        s_recip, s_pow, s_o = sem("norm_reciprocal"), sem("norm_rstd"), sem("o_summed")
        s_hm = sem("head_mean")
        pass_by = {e: sem("pass_" + e) for e in ("pe", "act", "dve", "pool", "sp")}
        block = ctx.enter_context(nc.Block())

        @block.sync
        def _(sp):
            def load(signal, *pairs):
                for dst, src in pairs:
                    sp.dma_start(dst, src).then_inc(signal, 16)

            load(s_const, *((dst, dram[name]) for dst, name in (
                (spread_raw, "spread"), (ident[:, :], "ident"), (vec[:, :], "vec"), (before[:, :, :, :], "before"),
                (w_maa1[:, :, :], "maa1"), (w_maa2[:, :, :], "maa2"), (w_maa2g[:, :], "maa2g"), (w_td1[:, :, :], "td1"), (w_td2[:, :], "td2"))))
            load(s_big[0], (w_big[:, 0, :, :], dram["big"][:, 0]))
            load(s_big[1], (w_big[:, 1:4, :, :], dram["big"][:, 1:4]), (gather[:, :, :], dram["gather"]), (heads[:, :], dram["heads"]))
            load(s_big[2], (w_big[:, 4:8, :, :], dram["big"][:, 4:8]))
            with sp.Fori(0, B) as b:
                sp.wait_ge(s_end, 1 + b * QT)
                sp.sem_inc(pass_by["sp"], 1)
                sp.dma_start(s0[:, :, :], dram["s0"][bass.ds(b, 1)].rearrange("a p f j -> (a p) f j")).then_inc(s_first, 16)

        @block.tensor
        def _(pe):
            for s in (s_pp, s_xx, s_vb, s_yu, s_gp, s_c, s_kk, s_rr, s_fv, s_tp):
                pe.sem_inc(s, 1)
            pe.wait_ge(s_const, LOADS)
            pe.wait_ge(s_spread, 1)

            def turn_stream(b, which):
                pe.wait_ge(s_xn, b * 2 + (which + 1))
                for ft in range(FT):
                    for qt in range(QT):
                        last = pe.transpose(bank[ft][:, qt * P:(qt + 1) * P], xn[:, qt, ft * P:(ft + 1) * P], ident[:, :])
                    last.then_inc(s_tp, 1)

            def slot(b, s):
                pe.wait_ge(s_pev, 1 + b * SLOTS + (s - 1 if s >= 2 else 0))
                return bank[4 + s % 2]

            with pe.Fori(0, B) as b:
                pe.wait_ge(s_end, 1 + b * QT)
                turn_stream(b, 0)
                pe.wait_ge(s_z, b * FT + FT)
                for s, (lo, hi) in enumerate(((0, 128), (128, 160))):
                    dst = slot(b, s)
                    for ft in range(FT):
                        last = pe.matmul(dst[0:hi - lo, :], w_maa1[:, ft, lo:hi], mixed[0][:, ft, :], start=(ft == 0), stop=(ft == FT - 1))
                    last.then_inc(s_pp, 1)

                def mix_in(f):
                    pe.wait_ge(s_pev, 1 + b * SLOTS + 2)
                    for ft in range(FT):
                        i = f * FT + ft
                        pe.wait_ge(s_pair, 1 + b * (5 * FT) + max(i - 1, 0))
                        if f < 4:
                            pe.matmul(bank[6 + i % 2][:, :], w_maa2[:, f, ft * P:(ft + 1) * P], lora[:, :], start=True, stop=True).then_inc(s_xx, 1)
                        else:
                            pe.matmul(bank[6 + i % 2][:, :], w_maa2g[:, ft * P:(ft + 1) * P], lora_g, start=True, stop=True).then_inc(s_xx, 1)

                def project(w, x, first, outs=FT, width=P, kt=FT):
                    for o in range(outs):
                        dst = slot(b, first + o)
                        for ft in range(kt):
                            last = pe.matmul(dst[0:width, :], w[:, ft, o * width:(o + 1) * width] if kt > 1 else w[:, o * width:(o + 1) * width],
                                             x[:, ft, :] if kt > 1 else x, start=(ft == 0), stop=(ft == kt - 1))
                        last.then_inc(s_pp, 1)

                mix_in(0)
                at = 2
                for f, name in enumerate(NAMES):
                    if f + 1 < 4:
                        mix_in(f + 1)
                    if f == 0:
                        pe.wait_ge(s_big[0], 16)
                    if f == 2:
                        pe.wait_ge(s_big[1], 3 * 16)
                    pe.wait_ge(s_mix, 1 + b * (5 * FT) + (f + 1) * FT)
                    x = mixed[1 - f % 2]
                    if name == "w":
                        project(w_td1, x, at, outs=1, width=64)
                        pe.wait_ge(s_pev, 1 + b * SLOTS + (at + 1))
                        project(w_td2, lora_w, at + 1, kt=1)
                        at += 5
                    else:
                        project(W[name], x, at)
                        at += 4
                    if f == 3:
                        mix_in(4)
                pe.wait_ge(s_pev, 1 + b * SLOTS + SLOTS)
                pe.wait_ge(s_pair, 1 + b * (5 * FT) + 5 * FT)
                pe.sem_inc(pass_by["pe"], 1)
                with pe.Fori(0, FT) as ft:
                    m = b * FT + ft

                    def per_ft(t):
                        return t[:, bass.ds(ft, 1), :].rearrange("p a t -> p (a t)")

                    pe.wait_ge(s_o, 1 + m)
                    pe.wait_ge(s_vhi, m + 1)
                    pe.wait_ge(s_vlo, m + 1)
                    for step in range(N + LAG):
                        if step < N:
                            pe.wait_ge(s_a, 1 + m * N + max(step + 1 - NB, 0))
                            pe.matmul(spread_bank[step % NB], spread[:, step, :], v_hi[:, :], start=True, stop=False)
                            pe.matmul(spread_bank[step % NB], spread[:, step, :], v_lo[:, :], start=False, stop=True).then_inc(s_vb, 1)
                        if step == 2:
                            pe.wait_ge(s_ruk, m + 1)
                            pe.matmul(bank[4][:, :], heads[:, :], per_ft(og), start=True, stop=True).then_inc(s_gp, 1)
                        j = step - LAG
                        if j >= 0:
                            pe.wait_ge(s_y, 1 + m * N + (j + 1))
                            pe.matmul(bank[5][:, :], gather[:, j, :], y_j[j % NB], start=(j == 0), stop=(j == N - 1)).then_inc(s_yu, 1)
                pe.wait_ge(s_big[2], 16)
                pe.wait_ge(s_o, 1 + b * FT + FT)
                for ft in range(FT):
                    pe.matmul(bank[ft][:, :], heads[:, :], og[:, ft, :], start=True, stop=True).then_inc(s_hm, 1)
                for ft in range(FT):
                    pe.wait_ge(s_ga, b * (2 * FT) + (ft + 1))
                    pe.matmul(bank[4 + ft][:, :], heads[:, :], xn[:, ft, :], start=True, stop=True).then_inc(s_hm, 1)
                for ft in range(FT):
                    pe.wait_ge(s_og, 1 + b * FT + (ft + 1))
                    for qt in range(QT):
                        last = pe.matmul(bank[qt][:, :], og[:, ft, qt * P:(qt + 1) * P], W["o"][:, ft, :], start=(ft == 0), stop=(ft == FT - 1))
                        if ft == FT - 1:
                            last.then_inc(s_c, 1)
                turn_stream(b, 1)
                pe.wait_ge(s_sx, b * 4 + 3)
                for o in range(FT):
                    pe.wait_ge(s_kku, 1 + b * FT + max(o - 1, 0))
                    for ft in range(FT):
                        last = pe.matmul(bank[4 + o % 2][:, :], W["fk"][:, ft, o * P:(o + 1) * P], mixed[0][:, ft, :], start=(ft == 0), stop=(ft == FT - 1))
                    last.then_inc(s_kk, 1)
                pe.wait_ge(s_sx, b * 4 + 4)
                for qt in range(QT):
                    for ft in range(FT):
                        last = pe.matmul(bank[qt][:, :], mixed[1][:, ft, qt * P:(qt + 1) * P], W["fr"][:, ft, :], start=(ft == 0), stop=(ft == FT - 1))
                    last.then_inc(s_rr, 1)
                pe.wait_ge(s_kku, 1 + b * FT + FT)
                for qt in range(QT):
                    for ft in range(FT):
                        last = pe.matmul(bank[4 + qt][:, :], kk[:, ft, qt * P:(qt + 1) * P], W["fv"][:, ft, :], start=(ft == 0), stop=(ft == FT - 1))
                    last.then_inc(s_fv, 1)

        @block.scalar
        def _(act):
            for s in (s_pev, s_gate):
                act.sem_inc(s, 1)
            act.wait_ge(s_const, LOADS)
            act.copy(spread[:, :, :].rearrange("p j m -> p (j m)"), spread_raw.rearrange("p j m -> p (j m)")).then_inc(s_spread, 1)
            with act.Fori(0, B) as b:
                def feature_major(which, w, bias):
                    for ft in range(FT):
                        act.wait_ge(s_tp, 1 + b * (2 * FT) + (which * FT + ft + 1))
                        act.activation(xa[:, ft, 1:T + 1], bank[ft][:, :], ACT.Identity, bias=column[bias](ft), scale=column[w](ft)).then_inc(s_xa, 1)
                    act.sem_inc(pass_by["act"], 1)
                    act.activation(xa[:, :, 0:1], before[:, bass.ds(b, 1), which, :].rearrange("p a (f c) -> p (a f) c", c=1), ACT.Copy).then_inc(s_xa, 1)

                feature_major(0, "ln1_w", "ln1_b")

                def evacuate(s, dst, src, func, **kw):
                    act.wait_ge(s_pp, 1 + b * SLOTS + (s + 1))
                    return act.activation(dst, src, func, **kw)

                evacuate(0, lora[:, :], bank[4][:, :], ACT.Tanh).then_inc(s_pev, 1)
                evacuate(1, lora_g, bank[5][0:32, :], ACT.Tanh).then_inc(s_pev, 1)
                at = 2
                for name in NAMES:
                    if name == "w":
                        evacuate(at, lora_w, bank[4 + at % 2][0:64, :], ACT.Tanh).then_inc(s_pev, 1)
                        at += 1
                    for ft in range(FT):
                        src, dst = bank[4 + at % 2][:, :], act_t[name][:, ft, :]
                        if name == "w":
                            evacuate(at, dst, src, ACT.Exp, bias=column["decay"](ft)).then_inc(s_dec, 1)
                            act.wait_ge(s_dec, b * FT + (ft + 1))
                            act.activation(dst, dst, ACT.Exp, scale=-1.0).then_inc(s_pev, 1)
                        elif name == "g":
                            evacuate(at, dst, src, ACT.Silu).then_inc(s_pev, 1)
                        else:
                            evacuate(at, dst, src, ACT.Copy).then_inc(s_pev, 1)
                        at += 1
                act.wait_ge(s_first, b * 16 + 16)
                act.sem_inc(pass_by["act"], 1)
                with act.Fori(0, FT) as ft:
                    m = b * FT + ft
                    act.wait_ge(s_vb, 1 + m * N)
                    act.sem_inc(pass_by["act"], 1)
                    act.copy(v_hi[:, :], act_t["v"][:, bass.ds(ft, 1), :].rearrange("p a t -> p (a t)")).then_inc(s_vhi, 1)
                    for j in range(N):
                        act.wait_ge(s_y, 1 + m * N + max(j + 1 - NB, 0))
                        act.sem_inc(pass_by["act"], 1)
                        act.activation(state[j % NB][:, 0:1], s0[:, bass.ds(ft, 1), j:j + 1].rearrange("p a j -> p (a j)"), ACT.Copy).then_inc(s_s0, 1)
                for ft in range(FT):
                    act.wait_ge(s_gd, b * (2 * FT) + (ft + 1))
                    act.activation(xn[:, ft, :], og[:, ft, :], ACT.Square).then_inc(s_ga, 1)
                for step in range(FT + 1):
                    if step < FT:
                        act.wait_ge(s_recip, b * FT + (step + 1))
                        act.activation(xn[:, step, :], xn[:, step, :], ACT.Sqrt).then_inc(s_pow, 1)
                    if step == 0:
                        continue
                    ft = step - 1
                    act.wait_ge(s_gd, b * (2 * FT) + (FT + ft + 1))
                    act.activation(xn[:, ft, :], og[:, ft, :], ACT.Identity, bias=column["gn_b"](ft), scale=column["gn_w"](ft)).then_inc(s_ga, 1)
                act.wait_ge(s_mix, 1 + b * (5 * FT) + 5 * FT)
                feature_major(1, "ln2_w", "ln2_b")
                for o in range(FT):
                    act.wait_ge(s_kk, 1 + b * FT + (o + 1))
                    act.activation(kk[:, o, :], bank[4 + o % 2][:, :], ACT.Relu).then_inc(s_relu, 1)
                for qt in range(QT):
                    act.wait_ge(s_rr, 1 + b * QT + (qt + 1))
                    act.activation(gate[:, qt, :], bank[qt][:, :], ACT.Sigmoid).then_inc(s_gate, 1)

        @block.gpsimd
        def _(pool):
            for s in (s_mix, s_y):
                pool.sem_inc(s, 1)
            pool.memset(power[:, :, :], -0.5).then_inc(s_power, 1)
            pool.wait_ge(s_power, 1)
            with pool.Fori(0, B) as b:
                pool.wait_ge(s_var, b * 2 + 1)
                pool.tensor_tensor(rstd[:, :, :], rstd[:, :, :], power[:, :, :], ALU.pow).then_inc(s_rstd, 1)
                for f in range(5):
                    for ft in range(FT):
                        dst = mixed[1 - f % 2][:, ft, :]
                        pool.wait_ge(s_pair, 1 + b * (5 * FT) + (f * FT + ft + 1))
                        pool.tensor_tensor(dst, dst, xa[:, ft, 1:T + 1], ALU.add).then_inc(s_mix, 1)
                pool.wait_ge(s_pev, 1 + b * SLOTS + SLOTS)
                pool.sem_inc(pass_by["pool"], 1)
                with pool.Fori(0, FT) as ft:
                    m = b * FT + ft
                    pool.wait_ge(s_vhi, m + 1)
                    pool.sem_inc(pass_by["pool"], 1)
                    pool.tensor_tensor(v_lo[:, :], act_t["v"][:, bass.ds(ft, 1), :].rearrange("p a t -> p (a t)"), v_hi[:, :], ALU.subtract).then_inc(s_vlo, 1)
                    for j in range(N):
                        pool.wait_ge(s_yu, 1 + m * N + max(j + 1 - NB, 0))
                        pool.wait_ge(s_s0, m * N + (j + 1))
                        pool.wait_ge(s_st, m * N + (j + 1))
                        pool.sem_inc(pass_by["pool"], 1)
                        pool.tensor_tensor(y_j[j % NB], act_t["r"][:, bass.ds(ft, 1), :].rearrange("p a t -> p (a t)"), state[j % NB][:, 0:T], ALU.mult).then_inc(s_y, 1)
                pool.wait_ge(s_var, b * 2 + 2)
                pool.tensor_tensor(rstd[:, :, :], rstd[:, :, :], power[:, :, :], ALU.pow).then_inc(s_rstd, 1)

        @block.vector
        def _(dve):
            for s in (s_pair, s_a, s_og, s_kku, s_end, s_o):
                dve.sem_inc(s, 1)
            with dve.Fori(0, B) as b:
                def stream(qt):
                    return x_res[:, bass.ds(b, 1), qt, :].rearrange("p a d -> p (a d)")

                def layer_norm(which):
                    k = b * 2 + which
                    for qt in range(QT) if which == 0 else ():
                        dve.sem_inc(pass_by["dve"], 1)
                        dve.bn_stats(stats[:, qt, :], stream(qt)).then_inc(s_bn, 1)
                    for qt in range(QT):
                        dve.wait_ge(s_bn, k * QT + (qt + 1))
                        dve.sem_inc(pass_by["dve"], 1)
                        dve.bn_aggr(mv[:, qt, :], stats[:, qt, :]).then_inc(s_mv, 1)
                    dve.wait_ge(s_mv, k * QT + QT)
                    dve.tensor_scalar(rstd[:, :, 0:1], mv[:, :, 1:2], 1e-5, None, ALU.add).then_inc(s_var, 1)
                    dve.wait_ge(s_rstd, k + 1)
                    dve.wait_ge(s_tp, 1 + k * FT)
                    for qt in range(QT):
                        last = dve.tensor_scalar(xn[:, qt, :], stream(qt), mv[:, qt, 0:1], rstd[:, qt, 0:1], ALU.subtract, ALU.mult)
                    last.then_inc(s_xn, 1)

                def difference(which):
                    dve.wait_ge(s_xa, b * (2 * FT + 2) + (which + 1) * (FT + 1))
                    dve.tensor_tensor(sx[:, :, :], xa[:, :, 0:T], xa[:, :, 1:T + 1], ALU.subtract).then_inc(s_sx, 1)
                    dve.wait_ge(s_sx, b * 4 + (2 * which + 1 if which == 0 else 2))

                layer_norm(0)
                dve.wait_ge(s_const, LOADS)
                dve.wait_ge(s_spread, 1)
                difference(0)
                for ft in range(FT):
                    dve.scalar_tensor_tensor(mixed[0][:, ft, :], sx[:, ft, :], column["maa_x"](ft), xa[:, ft, 1:T + 1], ALU.mult, ALU.add).then_inc(s_z, 1)
                for f, used in enumerate((0, 2, 6, 7, 15)):
                    dve.wait_ge(s_pp, 1 + b * SLOTS + used)
                    for ft in range(FT):
                        i = f * FT + ft
                        dve.wait_ge(s_xx, 1 + b * (5 * FT) + (i + 1))
                        dve.scalar_tensor_tensor(mixed[1 - f % 2][:, ft, :], bank[6 + i % 2][:, :], column["maa_" + NAMES[f]](ft), sx[:, ft, :], ALU.add, ALU.mult).then_inc(s_pair, 1)
                dve.wait_ge(s_pev, 1 + b * SLOTS + SLOTS)
                dve.wait_ge(s_first, b * 16 + 16)
                dve.sem_inc(pass_by["dve"], 1)
                with dve.Fori(0, FT) as ft:
                    m = b * FT + ft

                    def per_ft(name):
                        return act_t[name][:, bass.ds(ft, 1), :].rearrange("p a t -> p (a t)")

                    dve.scalar_tensor_tensor(og[:, bass.ds(ft, 1), :].rearrange("p a t -> p (a t)"), per_ft("r"), vec[:, bass.ds(ft + 4 * VEC3.index("u"), 1)], per_ft("k"), ALU.mult, ALU.mult).then_inc(s_ruk, 1)
                    for j in range(N + 1):
                        if j < N:
                            dve.wait_ge(s_vb, 1 + m * N + (j + 1))
                            dve.tensor_tensor(a_j[j % NB], spread_bank[j % NB], per_ft("k"), ALU.mult).then_inc(s_a, 1)
                        if j >= 1:
                            i = j - 1
                            dve.wait_ge(s_a, 1 + m * N + (i + 1))
                            dve.wait_ge(s_y, 1 + m * N + max(i + 1 - NB, 0))
                            dve.tensor_tensor_scan(state[i % NB][:, 1:T + 1], per_ft("w"), a_j[i % NB],
                                                   s0[:, bass.ds(ft, 1), i:i + 1].rearrange("p a j -> p (a j)"), ALU.mult, ALU.add).then_inc(s_st, 1)
                        if j == 4:
                            dve.wait_ge(s_gp, 1 + m + 1)
                            dve.tensor_tensor(bonus[:, :], bank[4][:, :], per_ft("v"), ALU.mult).then_inc(s_bonus, 1)
                    dve.wait_ge(s_yu, 1 + m * N + N)
                    dve.wait_ge(s_bonus, m + 1)
                    dve.tensor_tensor(og[:, bass.ds(ft, 1), :].rearrange("p a t -> p (a t)"), bank[5][:, :], bonus[:, :], ALU.add).then_inc(s_o, 1)
                for ft in range(FT):
                    dve.wait_ge(s_hm, b * (2 * FT) + (ft + 1))
                    dve.scalar_tensor_tensor(og[:, ft, :], bank[ft][:, :], -1.0 / N, og[:, ft, :], ALU.mult, ALU.add).then_inc(s_gd, 1)
                for step in range(FT + 2):
                    if step < FT:
                        dve.wait_ge(s_hm, b * (2 * FT) + (FT + step + 1))
                        dve.tensor_scalar(xn[:, step, :], bank[4 + step][:, :], 1.0 / N, 1e-5, ALU.mult, ALU.add).then_inc(s_veps, 1)
                        dve.wait_ge(s_veps, b * FT + (step + 1))
                        dve.reciprocal(xn[:, step, :], xn[:, step, :]).then_inc(s_recip, 1)
                    if 1 <= step <= FT:
                        ft = step - 1
                        dve.wait_ge(s_pow, b * FT + (ft + 1))
                        dve.tensor_tensor(og[:, ft, :], og[:, ft, :], xn[:, ft, :], ALU.mult).then_inc(s_gd, 1)
                    if step >= 2:
                        ft = step - 2
                        dve.wait_ge(s_ga, b * (2 * FT) + (FT + ft + 1))
                        dve.tensor_tensor(og[:, ft, :], xn[:, ft, :], act_t["g"][:, ft, :], ALU.mult).then_inc(s_og, 1)
                for qt in range(QT):
                    dve.wait_ge(s_c, 1 + b * QT + (qt + 1))
                    dve.tensor_tensor(stream(qt), stream(qt), bank[qt][:, :], ALU.add).then_inc(s_xadd, 1)
                    dve.wait_ge(s_xadd, b * QT + (qt + 1))
                    dve.sem_inc(pass_by["dve"], 1)
                    dve.bn_stats(stats[:, qt, :], stream(qt)).then_inc(s_bn, 1)
                layer_norm(1)
                difference(1)
                for which, name in enumerate(("ffn_k", "ffn_r")):
                    for ft in range(FT):
                        last = dve.scalar_tensor_tensor(mixed[which][:, ft, :], sx[:, ft, :], column[name](ft), xa[:, ft, 1:T + 1], ALU.mult, ALU.add)
                    last.then_inc(s_sx, 1)
                for o in range(FT):
                    dve.wait_ge(s_relu, b * FT + (o + 1))
                    dve.tensor_tensor(kk[:, o, :], kk[:, o, :], kk[:, o, :], ALU.mult).then_inc(s_kku, 1)
                for qt in range(QT):
                    dve.wait_ge(s_fv, 1 + b * QT + (qt + 1))
                    dve.wait_ge(s_gate, 1 + b * QT + (qt + 1))
                    dve.tensor_tensor(xn[:, qt, :], bank[4 + qt][:, :], gate[:, qt, :], ALU.mult).then_inc(s_half, 1)
                for qt in range(QT):
                    dve.wait_ge(s_half, b * QT + (qt + 1))
                    dve.tensor_tensor(stream(qt), stream(qt), xn[:, qt, :], ALU.add).then_inc(s_end, 1)
                dve.wait_ge(s_end, 1 + b * QT + QT)


def load_stream(nc, x, x_res):
    with nc.semaphore("x_loaded") as s_x, nc.Block() as block:
        @block.sync
        def _(sp):
            sp.dma_start(x_res[:, :, :, :], x.rearrange("b (q p) d -> p b q d", p=P)).then_inc(s_x, 16)
            sp.wait_ge(s_x, 16)


def store_stream(nc, out, x_res):
    with nc.semaphore("x_stored") as s_x, nc.Block() as block:
        @block.sync
        def _(sp):
            sp.dma_start(out.rearrange("b (q p) d -> p b q d", p=P), x_res[:, :, :, :]).then_inc(s_x, 16)
            sp.wait_ge(s_x, 16)


def network(nc, x, out, two, gqa, mix):
    with nc.sbuf_tensor("x_res", [P, B, QT, D], F32) as x_res:
        load_stream(nc, x, x_res)
        attention_block(nc, "mha", 2, 4, 32 ** -0.5, two, x_res, True)
        attention_block(nc, "gqa", 1, 8, 16 ** -0.5, gqa, x_res, False)
        time_mix_block(nc, mix, x_res)
        store_stream(nc, out, x_res)


def kernel(**inputs):
    import numpy as np
    import concourse.bacc as bacc
    from concourse.bass_utils import run_bass_kernel_spmd

    a = {k: np.ascontiguousarray(v) for k, v in inputs.items()}
    f32 = np.float32

    def tiles_in(w):
        return w.reshape(-1, P, w.shape[1]).transpose(1, 0, 2)

    def columns(w):
        return w.reshape(-1, P).T

    def spread_heads(w, repeat):
        heads = w.reshape(*w.shape[:-1], -1, 1, 16)
        out = np.zeros((*w.shape[:-1], heads.shape[-3], repeat, 32), f32)
        out[..., :16] = heads
        return out.reshape(*w.shape[:-1], -1)

    def qkv(wq, wk, wv):
        return np.stack([tiles_in(w).reshape(P, FT, -1, P).transpose(2, 0, 1, 3) for w in (wq, wk, wv)], axis=2)

    stacker = np.zeros((P, HPG, 7, HR), f32)
    for j in range(HPG):
        for block in (0, 3, 4):
            stacker[HR * j:HR * j + HR, j, block] = np.eye(HR)
    stacker = stacker.reshape(P, HPG, STRIP)
    data = {"ident": np.eye(P, dtype=f32), "stack": stacker}
    data["ctx_t"] = a["ctx_2048"].transpose(0, 2, 1).reshape(B, FT, P, S).transpose(0, 2, 1, 3)
    data["mask_u8"] = a["mask_BxS2_bf1"].view(np.uint8)
    data["x"] = a["x"]

    L = ["L0_xattn_", "L1_xattn_"]
    data["w_qkv"] = np.concatenate([qkv(a[l + "q_w"], a[l + "k_w"], a[l + "v_w"]) for l in L])
    data["w_out"] = np.stack([tiles_in(a[l + "cproj_w"]) for l in L])
    data["w_fc"] = np.concatenate([tiles_in(a[l + "fc_w"]).reshape(P, FT, F_TILES, P).transpose(2, 0, 1, 3) for l in L])
    data["w_pr"] = np.concatenate([a[l + "proj_w"].reshape(F_TILES, P, D) for l in L])
    data["vec"] = np.stack([np.concatenate([columns(a[l + k]) for k in ("q_b", "k_b", "v_b", "ln1_w", "ln1_b", "ln2_w", "ln2_b", "fc_b")], axis=1)
                            for l in L], axis=1)
    data["row"] = np.stack([np.stack([a[l + "cproj_b"], a[l + "proj_b"]]) for l in L])

    l = "L2_xattn_"
    data["w_q2"] = tiles_in(spread_heads(a[l + "Wq"], 1)).reshape(P, FT, 8, P).transpose(2, 0, 1, 3)[:, :, None]
    data["w_kv2"] = np.stack([tiles_in(a[l + "Wk"]), tiles_in(a[l + "Wv"])], axis=1)
    to = np.arange(P)
    take = np.stack([(np.arange(P)[:, None] == 16 * g + to % 32) & (to % 32 < 16) for g in range(8)])
    data["pick2"] = np.stack([take & (to < 64), take & (to >= 64)], axis=2).astype(f32)
    data["w_out2"] = tiles_in(spread_heads(a[l + "Wo"].T, 1).T)[None]
    data["vec2"] = np.concatenate([columns(spread_heads(a[l + "bq"], 1)), columns(a[l + "bk"]), columns(spread_heads(a[l + "bv"], 4))], axis=1)[:, None]
    data["row2"] = a[l + "bo"][None, None]
    data["gamma"] = a[l + "gamma"][None]
    data["beta"] = a[l + "beta"][None]
    data["mask2"] = a["mask_Bx1xSxS2_ff0"].reshape(B, QT, P, S).transpose(0, 2, 1, 3)

    l = "L3_xattn_"
    data["m_big"] = np.stack([tiles_in(a[l + k].T) for k in ("Wk", "Wv", "Wr", "Wg", "Wo", "Wfk", "Wfr", "Wfv")], axis=1)
    data["m_maa1"] = tiles_in(a[l + "maa_w1"])
    rows = np.zeros((4, 32, 4, D), f32)
    for f in range(4):
        rows[f, :, f] = a[l + "maa_w2"][f]
    data["m_maa2"] = rows.reshape(P, 4, D)
    data["m_maa2g"] = a[l + "maa_w2"][4]
    data["m_td1"] = tiles_in(a[l + "td_w1"])
    data["m_td2"] = a[l + "td_w2"]
    stack = a[l + "maa_stack"][0]
    vec3 = [a[l + "ln1_w"], a[l + "ln1_b"], a[l + "ln2_w"], a[l + "ln2_b"], a[l + "maa_x"], *stack, a[l + "time_decay"], a[l + "u"].reshape(-1),
            a[l + "gn_w"], a[l + "gn_b"], a[l + "ffn_maa_k"], a[l + "ffn_maa_r"]]
    data["m_vec"] = np.concatenate([columns(v) for v in vec3], axis=1)
    data["m_s0"] = a["ctx_2048"][:, 2:18].reshape(B, FT, P, 16).transpose(0, 2, 1, 3)
    data["m_before"] = a["ctx_2048"][:, [1, 0]].reshape(B, 2, FT, P).transpose(3, 0, 1, 2)
    head, inner = np.arange(P) // 16, np.arange(P) % 16
    same = head[:, None] == head[None, :]
    data["m_heads"] = same.astype(f32)
    data["m_spread"] = np.stack([(same & (inner[:, None] == j)) for j in range(16)], axis=1).astype(f32)
    data["m_gather"] = np.stack([(same & (inner[None, :] == j)) for j in range(16)], axis=1).astype(f32)

    nc = bacc.Bacc("TRN2", target_bir_lowering=False, num_devices=1)
    data = {k: np.ascontiguousarray(v) for k, v in data.items()}
    t = {k: nc.dram_tensor(f"in_{k}", v.shape, mybir.dt.from_np(v.dtype), kind="ExternalInput").ap() for k, v in data.items()}
    out = nc.dram_tensor("out_0", (B, T, D), F32, kind="ExternalOutput").ap()
    shared = {k: t[k] for k in ("ident", "ctx_t", "stack")}
    two = dict(shared, mask=t["mask_u8"], **{k: t[k] for k in ("w_qkv", "w_out", "w_fc", "w_pr", "vec", "row")})
    gqa = dict(shared, mask=t["mask2"], w_qkv=t["w_q2"], w_kv=t["w_kv2"], pick=t["pick2"], w_out=t["w_out2"], vec=t["vec2"], row=t["row2"], gamma=t["gamma"], beta=t["beta"])
    mix = {k[2:]: v for k, v in t.items() if k.startswith("m_")}
    mix["ident"] = t["ident"]
    network(nc, t["x"], out, two, gqa, mix)
    r = run_bass_kernel_spmd(nc, [{f"in_{k}": v for k, v in data.items()}], core_ids=[0])
    return r.results[0]["out_0"]
```
